# Optimizing a Trainium2 kernel written in Bass

```python
import numpy as np
import jax
import jax.numpy as jnp

def _softmax(x, axis=-1):
    return jax.nn.softmax(x, axis=axis)

def _gelu(x):
    return jax.nn.gelu(x, approximate=True)

def _silu(x):
    return jax.nn.silu(x)

def _sigmoid(x):
    return jax.nn.sigmoid(x)

def _layernorm(x, axis=-1, eps=1e-05):
    m = jnp.mean(x, axis=axis, keepdims=True)
    v = jnp.var(x, axis=axis, keepdims=True)
    return (x - m) / jnp.sqrt(v + eps)

def _scatter_add(tgt, idx, src, axis=0):
    return tgt.at[idx].add(src)

def _segment_sum(src, seg, n):
    return jax.ops.segment_sum(src, seg, n)
kernel_name = 'mk_sandwich_d2_jaxref_r4_7f4602'

def setup_inputs(seed: int=0):
    np.random.seed(seed)
    _w = jnp.asarray

    def _L0_attn_setup():
        import jax, jax.numpy as jnp
        import numpy as np
        GROUP = 64
        MAX_REL = 32

        def _silu(x):
            return x * jax.nn.sigmoid(x)

        def _ln(x, w, b, eps=1e-05):
            m = x.mean(-1, keepdims=True)
            v = ((x - m) ** 2).mean(-1, keepdims=True)
            return (x - m) / jnp.sqrt(v + eps) * w + b

        def _rope(x):
            n, d = (x.shape[-2], x.shape[-1])
            half = d // 2
            pos = jnp.arange(n, dtype=x.dtype)
            inv_freq = 10000.0 ** (-jnp.arange(half, dtype=x.dtype) / half)
            sinusoid = pos[:, None] * inv_freq[None, :]
            sin, cos = (jnp.sin(sinusoid), jnp.cos(sinusoid))
            x1, x2 = (x[..., :half], x[..., half:])
            return jnp.concatenate([x1 * cos - x2 * sin, x2 * cos + x1 * sin], axis=-1)
        key = jax.random.key(seed)
        ks = jax.random.split(key, 8)
        B, N, D, QK, H = (4, 1024, 256, 64, 512)
        s = 0.02
        return {'x': jax.random.normal(ks[0], (B, N, D), dtype=jnp.float32), 'ln1_w': jnp.ones((D,), jnp.float32), 'ln1_b': jnp.zeros((D,), jnp.float32), 'Wqk': jax.random.normal(ks[1], (QK, D), jnp.float32) * s, 'bqk': jnp.zeros((QK,), jnp.float32), 'Wv': jax.random.normal(ks[2], (H, D), jnp.float32) * s, 'bv': jnp.zeros((H,), jnp.float32), 'Wg': jax.random.normal(ks[3], (H, D), jnp.float32) * s, 'bg': jnp.zeros((H,), jnp.float32), 'Wo': jax.random.normal(ks[4], (D, H), jnp.float32) * s, 'bo': jnp.zeros((D,), jnp.float32), 'ln2_w': jnp.ones((D,), jnp.float32), 'ln2_b': jnp.zeros((D,), jnp.float32), 'gamma': jax.random.normal(ks[5], (4, QK), jnp.float32) * 0.02, 'beta': jnp.zeros((4, QK), jnp.float32), 'pos_emb': jax.random.normal(ks[6], (2 * MAX_REL + 1,), jnp.float32)}
    _L0_attn_in = _L0_attn_setup()

    def _L0_ffn_setup():
        import jax, jax.numpy as jnp
        import numpy as np
        DIM = 256

        def _reference_tuple_inner(x, W_r, W_k, W_v, mu_r, mu_k):
            B, T, C = x.shape
            x_prev = jnp.concatenate([jnp.zeros((B, 1, C), x.dtype), x[:, :-1, :]], axis=1)
            xr = mu_r * x + (1.0 - mu_r) * x_prev
            xk = mu_k * x + (1.0 - mu_k) * x_prev
            r = jax.nn.sigmoid(jnp.einsum('btc,dc->btd', xr, W_r))
            k = jnp.einsum('btc,dc->btd', xk, W_k)
            k_act = jnp.square(jax.nn.relu(k))
            out = r * jnp.einsum('btc,dc->btd', k_act, W_v)
            new_state = x[:, -1, :]
            return (out, new_state)
        key = jax.random.key(seed)
        ks = jax.random.split(key, 6)
        B, T, C = (8, 512, DIM)
        x = jax.random.normal(ks[0], (B, T, C), dtype=jnp.float32)
        s = 1.0 / np.sqrt(C)
        W_r = jax.random.uniform(ks[1], (C, C), jnp.float32, -s, s)
        W_k = jax.random.uniform(ks[2], (C, C), jnp.float32, -s, s)
        W_v = jax.random.uniform(ks[3], (C, C), jnp.float32, -s, s)
        mu_r = jax.random.uniform(ks[4], (C,), jnp.float32)
        mu_k = jax.random.uniform(ks[5], (C,), jnp.float32)
        return {'x': x, 'W_r': W_r, 'W_k': W_k, 'W_v': W_v, 'mu_r': mu_r, 'mu_k': mu_k}
    _L0_ffn_in = _L0_ffn_setup()

    def _L1_attn_setup():
        import jax, jax.numpy as jnp
        import numpy as np
        DIM = 256
        HEADS = 16
        HEAD_DIM = DIM // HEADS

        def _feature_map(z, W, b):
            p = jnp.einsum('bhtd,ed->bhte', z, W) + b
            return jnp.concatenate([jax.nn.softmax(p, axis=-1), jax.nn.softmax(-p, axis=-1)], axis=-1)
        key = jax.random.key(seed)
        ks = jax.random.split(key, 7)
        s = 0.02
        x = jax.random.normal(ks[0], (1, 256, DIM), dtype=jnp.float32)
        w_qkv = jax.random.normal(ks[1], (3 * DIM, DIM), dtype=jnp.float32) * s
        wq_map = jnp.eye(HEAD_DIM, dtype=jnp.float32) + jax.random.normal(ks[2], (HEAD_DIM, HEAD_DIM), dtype=jnp.float32) * s
        bq_map = jax.random.normal(ks[3], (HEAD_DIM,), dtype=jnp.float32) * s
        wk_map = jnp.eye(HEAD_DIM, dtype=jnp.float32) + jax.random.normal(ks[4], (HEAD_DIM, HEAD_DIM), dtype=jnp.float32) * s
        bk_map = jax.random.normal(ks[5], (HEAD_DIM,), dtype=jnp.float32) * s
        w_out = jax.random.normal(ks[6], (DIM, DIM), dtype=jnp.float32) * s
        return {'x': x, 'w_qkv': w_qkv, 'wq_map': wq_map, 'bq_map': bq_map, 'wk_map': wk_map, 'bk_map': bk_map, 'w_out': w_out}
    _L1_attn_in = _L1_attn_setup()

    def _L1_ffn_setup():
        import jax, jax.numpy as jnp
        import numpy as np
        NUM_EXPERTS = 8
        CAPACITY = 1024
        key = jax.random.key(seed)
        ks = jax.random.split(key, 5)
        dim, hidden = (256, 512)
        x = jax.random.normal(ks[0], (4, 1024, dim), dtype=jnp.float32)
        wg = jax.random.normal(ks[1], (dim, NUM_EXPERTS), dtype=jnp.float32) * 0.02
        w1 = jax.random.normal(ks[2], (NUM_EXPERTS, dim, hidden), dtype=jnp.float32) * 0.02
        w3 = jax.random.normal(ks[3], (NUM_EXPERTS, dim, hidden), dtype=jnp.float32) * 0.02
        w2 = jax.random.normal(ks[4], (NUM_EXPERTS, hidden, dim), dtype=jnp.float32) * 0.02
        return {'x': x, 'wg': wg, 'w1': w1, 'w3': w3, 'w2': w2}
    _L1_ffn_in = _L1_ffn_setup()
    _d = {'L0_attn_x': _L0_attn_in['x'], 'L0_attn_ln1_w': _L0_attn_in['ln1_w'], 'L0_attn_ln1_b': _L0_attn_in['ln1_b'], 'L0_attn_Wqk': _L0_attn_in['Wqk'], 'L0_attn_bqk': _L0_attn_in['bqk'], 'L0_attn_Wv': _L0_attn_in['Wv'], 'L0_attn_bv': _L0_attn_in['bv'], 'L0_attn_Wg': _L0_attn_in['Wg'], 'L0_attn_bg': _L0_attn_in['bg'], 'L0_attn_Wo': _L0_attn_in['Wo'], 'L0_attn_bo': _L0_attn_in['bo'], 'L0_attn_ln2_w': _L0_attn_in['ln2_w'], 'L0_attn_ln2_b': _L0_attn_in['ln2_b'], 'L0_attn_gamma': _L0_attn_in['gamma'], 'L0_attn_beta': _L0_attn_in['beta'], 'L0_attn_pos_emb': _L0_attn_in['pos_emb'], 'L0_ffn_W_r': _L0_ffn_in['W_r'], 'L0_ffn_W_k': _L0_ffn_in['W_k'], 'L0_ffn_W_v': _L0_ffn_in['W_v'], 'L0_ffn_mu_r': _L0_ffn_in['mu_r'], 'L0_ffn_mu_k': _L0_ffn_in['mu_k'], 'L1_attn_w_qkv': _L1_attn_in['w_qkv'], 'L1_attn_wq_map': _L1_attn_in['wq_map'], 'L1_attn_bq_map': _L1_attn_in['bq_map'], 'L1_attn_wk_map': _L1_attn_in['wk_map'], 'L1_attn_bk_map': _L1_attn_in['bk_map'], 'L1_attn_w_out': _L1_attn_in['w_out'], 'L1_ffn_wg': _L1_ffn_in['wg'], 'L1_ffn_w1': _L1_ffn_in['w1'], 'L1_ffn_w3': _L1_ffn_in['w3'], 'L1_ffn_w2': _L1_ffn_in['w2']}
    _x0 = _d['L0_attn_x']
    _d['L0_attn_x'] = jax.random.normal(jax.random.fold_in(jax.random.key(seed), 1), (8, 512, 256), dtype=_x0.dtype)
    del _x0
    return _d

def reference(L0_attn_x, L0_attn_ln1_w, L0_attn_ln1_b, L0_attn_Wqk, L0_attn_bqk, L0_attn_Wv, L0_attn_bv, L0_attn_Wg, L0_attn_bg, L0_attn_Wo, L0_attn_bo, L0_attn_ln2_w, L0_attn_ln2_b, L0_attn_gamma, L0_attn_beta, L0_attn_pos_emb, L0_ffn_W_r, L0_ffn_W_k, L0_ffn_W_v, L0_ffn_mu_r, L0_ffn_mu_k, L1_attn_w_qkv, L1_attn_wq_map, L1_attn_bq_map, L1_attn_wk_map, L1_attn_bk_map, L1_attn_w_out, L1_ffn_wg, L1_ffn_w1, L1_ffn_w3, L1_ffn_w2):

    def _L0_attn_ref(x, ln1_w, ln1_b, Wqk, bqk, Wv, bv, Wg, bg, Wo, bo, ln2_w, ln2_b, gamma, beta, pos_emb):
        import jax, jax.numpy as jnp
        import numpy as np
        GROUP = 64
        MAX_REL = 32

        def _silu(x):
            return x * jax.nn.sigmoid(x)

        def _ln(x, w, b, eps=1e-05):
            m = x.mean(-1, keepdims=True)
            v = ((x - m) ** 2).mean(-1, keepdims=True)
            return (x - m) / jnp.sqrt(v + eps) * w + b

        def _rope(x):
            n, d = (x.shape[-2], x.shape[-1])
            half = d // 2
            pos = jnp.arange(n, dtype=x.dtype)
            inv_freq = 10000.0 ** (-jnp.arange(half, dtype=x.dtype) / half)
            sinusoid = pos[:, None] * inv_freq[None, :]
            sin, cos = (jnp.sin(sinusoid), jnp.cos(sinusoid))
            x1, x2 = (x[..., :half], x[..., half:])
            return jnp.concatenate([x1 * cos - x2 * sin, x2 * cos + x1 * sin], axis=-1)
        b, n, d = x.shape
        G = GROUP
        x = _ln(x, ln1_w, ln1_b)
        qk = _silu(x @ Wqk.T + bqk)
        v = _silu(x @ Wv.T + bv)
        heads = qk[..., None, :] * gamma + beta
        quad_q, lin_q, quad_k, lin_k = (heads[..., i, :] for i in range(4))
        quad_q, lin_q, quad_k, lin_k = map(_rope, (quad_q, lin_q, quad_k, lin_k))
        g = n // G
        rs = lambda t: t.reshape(b, g, G, t.shape[-1])
        qq, lq, qkk, lk, vg = map(rs, (quad_q, lin_q, quad_k, lin_k, v))
        idx = jnp.arange(G)
        dist = jnp.clip(jnp.abs(idx[:, None] - idx[None, :]), 0, MAX_REL)
        bias = pos_emb[dist]
        quad_att = jnp.einsum('bgid,bgjd->bgij', qq, qkk) / G + bias
        attn = jax.nn.relu(quad_att) ** 2
        quad_out = jnp.einsum('bgij,bgje->bgie', attn, vg)
        lin_kv = jnp.einsum('bgnd,bgne->bde', lk, vg) / n
        lin_out = jnp.einsum('bgnd,bde->bgne', lq, lin_kv)
        qo = quad_out.reshape(b, n, -1)
        lo = lin_out.reshape(b, n, -1)
        gate = _silu(x @ Wg.T + bg)
        out = gate * (qo + lo)
        out = out @ Wo.T + bo
        return _ln(out, ln2_w, ln2_b)

    def _L0_ffn_ref(x, W_r, W_k, W_v, mu_r, mu_k):
        import jax, jax.numpy as jnp
        import numpy as np
        DIM = 256

        def _reference_tuple_inner(x, W_r, W_k, W_v, mu_r, mu_k):
            B, T, C = x.shape
            x_prev = jnp.concatenate([jnp.zeros((B, 1, C), x.dtype), x[:, :-1, :]], axis=1)
            xr = mu_r * x + (1.0 - mu_r) * x_prev
            xk = mu_k * x + (1.0 - mu_k) * x_prev
            r = jax.nn.sigmoid(jnp.einsum('btc,dc->btd', xr, W_r))
            k = jnp.einsum('btc,dc->btd', xk, W_k)
            k_act = jnp.square(jax.nn.relu(k))
            out = r * jnp.einsum('btc,dc->btd', k_act, W_v)
            new_state = x[:, -1, :]
            return (out, new_state)
        return _reference_tuple_inner(x, W_r, W_k, W_v, mu_r, mu_k)[0]

    def _L1_attn_ref(x, w_qkv, wq_map, bq_map, wk_map, bk_map, w_out):
        import jax, jax.numpy as jnp
        import numpy as np
        DIM = 256
        HEADS = 16
        HEAD_DIM = DIM // HEADS

        def _feature_map(z, W, b):
            p = jnp.einsum('bhtd,ed->bhte', z, W) + b
            return jnp.concatenate([jax.nn.softmax(p, axis=-1), jax.nn.softmax(-p, axis=-1)], axis=-1)
        b, t, dim = x.shape
        h, hd = (HEADS, HEAD_DIM)
        qkv = (x @ w_qkv.T).reshape(b, t, 3, h, hd)
        q, k, v = [jnp.transpose(qkv[:, :, i], (0, 2, 1, 3)) for i in range(3)]
        q = _feature_map(q, wq_map, bq_map)
        k = _feature_map(k, wk_map, bk_map)
        k_prefix = jnp.cumsum(k, axis=2)
        kv_prefix = jnp.cumsum(jnp.einsum('bhtf,bhtd->bhtfd', k, v), axis=2)
        numer = jnp.einsum('bhtf,bhtfd->bhtd', q, kv_prefix)
        denom = jnp.maximum(jnp.einsum('bhtf,bhtf->bht', q, k_prefix)[..., None], 1e-06)
        y = jnp.transpose(numer / denom, (0, 2, 1, 3)).reshape(b, t, dim)
        return y @ w_out.T

    def _L1_ffn_ref(x, wg, w1, w3, w2):
        import jax, jax.numpy as jnp
        import numpy as np
        NUM_EXPERTS = 8
        CAPACITY = 1024
        bz, slen, dim = x.shape
        xt = x.reshape(bz * slen, dim)
        scores = jax.nn.softmax(xt @ wg, axis=-1)
        top_scores, sel = jax.lax.top_k(scores.T, CAPACITY)
        token_idx = sel.reshape(-1)
        routed = xt[token_idx] * top_scores.reshape(-1, 1)
        routed = routed.reshape(NUM_EXPERTS, CAPACITY, dim)
        h = jax.nn.silu(jnp.einsum('ecd,edh->ech', routed, w1)) * jnp.einsum('ecd,edh->ech', routed, w3)
        routed_out = jnp.einsum('ech,ehd->ecd', h, w2).reshape(-1, dim)
        out = jnp.zeros_like(xt).at[token_idx].add(routed_out)
        return out.reshape(bz, slen, dim)
    x = L0_attn_x
    x = x + _layernorm(_L0_attn_ref(_layernorm(x, axis=-1), L0_attn_ln1_w, L0_attn_ln1_b, L0_attn_Wqk, L0_attn_bqk, L0_attn_Wv, L0_attn_bv, L0_attn_Wg, L0_attn_bg, L0_attn_Wo, L0_attn_bo, L0_attn_ln2_w, L0_attn_ln2_b, L0_attn_gamma, L0_attn_beta, L0_attn_pos_emb), axis=-1)
    x = x + _layernorm(_L0_ffn_ref(_layernorm(x, axis=-1), L0_ffn_W_r, L0_ffn_W_k, L0_ffn_W_v, L0_ffn_mu_r, L0_ffn_mu_k), axis=-1)
    x = x + _layernorm(_L1_attn_ref(_layernorm(x, axis=-1), L1_attn_w_qkv, L1_attn_wq_map, L1_attn_bq_map, L1_attn_wk_map, L1_attn_bk_map, L1_attn_w_out), axis=-1)
    x = x + _layernorm(_L1_ffn_ref(_layernorm(x, axis=-1), L1_ffn_wg, L1_ffn_w1, L1_ffn_w3, L1_ffn_w2), axis=-1)
    return x

_drawn_inputs = setup_inputs


def setup_inputs(seed=0):
    import zlib

    import numpy as np

    out = dict(_drawn_inputs(seed))
    spreads = {'L0_attn_ln1_w': (1.0, 0.2),
     'L0_attn_ln1_b': (0.0, 0.1),
     'L0_attn_bqk': (0.0, 2.0),
     'L0_attn_bv': (0.0, 0.1),
     'L0_attn_bg': (0.0, 0.1),
     'L0_attn_bo': (0.0, 0.1),
     'L0_attn_ln2_w': (1.0, 0.2),
     'L0_attn_ln2_b': (0.0, 0.1),
     'L0_attn_beta': (0.0, 0.8)}
    factors = {'L0_attn_Wqk': 8.0,
     'L0_attn_gamma': 8.0,
     'L1_attn_wq_map': 8.0,
     'L1_attn_bq_map': 26.502,
     'L1_attn_wk_map': 8.0,
     'L1_attn_bk_map': 41.389}
    for name, (base, spread) in spreads.items():
        noise = np.random.default_rng([zlib.crc32(name.encode()), seed]).standard_normal(out[name].shape)
        drawn = base * np.exp(spread * noise) if base else spread * noise
        out[name] = jnp.asarray(drawn.astype(out[name].dtype))
    for name, factor in factors.items():
        out[name] = (out[name] * factor).astype(out[name].dtype)
    return out
```

```python
import numpy as np
from contextlib import ExitStack

import concourse.bass as bass
from concourse import mybir

F32 = mybir.dt.float32
BF16 = mybir.dt.bfloat16
I32 = mybir.dt.int32
ALU = mybir.AluOpType
ACT = mybir.ActivationFunctionType
AX = mybir.AxisListType

B, T, D = 8, 512, 256
P = 128
TT = T // P
KC = D // P
NTOK = B * T
EPS = 1e-5
QK, H = 64, 512
EC = H // P
GROUP, MAX_REL = 64, 32
HEADS, HD = 16, 16
HPC = 4
FC = HEADS // HPC
VW = HD + 1
NE, CAP, HID = 8, 1024, 512


class Steps:

    def __init__(self, eng, sem):
        self.eng, self.sem, self.count, self.reg = eng, sem, 0, None

    def did(self, ins):
        ins.then_inc(self.sem, 1)
        self.count += 1

    def settle(self):
        if self.reg is None:
            self.eng.wait_ge(self.sem, self.count)
        else:
            self.eng.wait_ge(self.sem, self.reg * self.per + (self.count - self.lo * self.per))

    def loop(self, lo, hi, body, per):
        first = self.count
        with self.eng.Fori(lo, hi) as i:
            self.reg, self.per, self.lo = i, per, lo
            body(i)
        assert self.count - first == per, (self.count - first, per)
        self.reg, self.count = None, first + per * (hi - lo)


def tile_of(x, b, t):
    return x[:, bass.ds(b * (TT * D) + t * D, D)]


def batch_of(x, b):
    return x[:, bass.ds(b * (TT * D), TT * D)]


class Norm:

    def __init__(self, sb):
        self.st = sb("ln_stats", [P, TT, 6])
        self.sum = sb("ln_sum", [P, TT])
        self.dif = sb("ln_dif", [P, TT])
        self.cv = sb("ln_cv", [P, TT])
        self.sq = sb("ln_sq", [P, TT])
        self.v = sb("ln_v", [P, TT])
        self.mean = sb("ln_mean", [P, TT])
        self.var = sb("ln_var", [P, TT])
        self.rstd = sb("ln_rstd", [P, TT])
        self.mhalf = sb("ln_mhalf", [P, TT])

    def stats(self, nc, steps, tiles, var_ready, twice=False):
        for t in range(len(tiles)):
            steps.did(nc.vector.bn_stats(self.st[:, t, :], tiles[t]))
        steps.settle()
        steps.did(nc.vector.tensor_tensor(self.dif[:, :], self.st[:, :, 1], self.st[:, :, 4], ALU.subtract))
        steps.did(nc.vector.tensor_tensor(self.sum[:, :], self.st[:, :, 1], self.st[:, :, 4], ALU.add))
        steps.did(nc.vector.tensor_tensor(self.cv[:, :], self.st[:, :, 2], self.st[:, :, 5], ALU.add))
        steps.settle()
        steps.did(nc.vector.tensor_tensor(self.sq[:, :], self.dif[:, :], self.dif[:, :], ALU.mult))
        steps.did(nc.vector.tensor_scalar(self.mean[:, :], self.sum[:, :], 0.5, None, ALU.mult))
        steps.settle()
        steps.did(nc.vector.scalar_tensor_tensor(out=self.v[:, :], in0=self.sq[:, :], scalar=D / 4.0,
                                                 in1=self.cv[:, :], op0=ALU.mult, op1=ALU.add))
        steps.settle()
        a, e = (1 + EPS, EPS * EPS) if twice else (1.0, EPS)
        nc.vector.tensor_scalar(self.var[:, :], self.v[:, :], a / D, e, ALU.mult, ALU.add).then_inc(var_ready, 1)

    STATS_STEPS = TT + 6

    def root(self, pool, rstd_ready):
        pool.tensor_tensor(self.rstd[:, :], self.var[:, :], self.mhalf[:, :], ALU.pow).then_inc(rstd_ready, 1)

    def apply(self, nc, out, in_, t):
        return nc.vector.tensor_scalar(out, in_, self.mean[:, t:t + 1], self.rstd[:, t:t + 1],
                                       ALU.subtract, ALU.mult)


def gau_layer(nc, s, w):
    x, nm, bank, ident = s.x, s.norm, s.bank, s.ident
    with ExitStack() as ctx:
        sb = lambda n, shape, d=F32: ctx.enter_context(nc.sbuf_tensor("gau_" + n, shape, d))
        sem = lambda n: ctx.enter_context(nc.semaphore("gau_" + n))
        wqk = sb("wqk", [P, KC, 2 * QK])
        wv = sb("wv", [P, KC, H])
        wg = sb("wg", [P, KC, H])
        wo = sb("wo", [P, EC, D])
        cos, sin = sb("cos", [P, T]), sb("sin", [P, T])
        turn = sb("turn", [P, P])
        ln1 = sb("ln1", [P, 2, KC])
        bqk = sb("bqk", [P, 1])
        gamma, beta = sb("gamma", [P, 2]), sb("beta", [P, 2])
        bg = sb("bg", [P, EC])
        bv_row = sb("bv_row", [P, H])
        bo_row = sb("bo_row", [P, D])
        ln2 = sb("ln2", [P, 2, D])
        pos_row = sb("pos_row", [1, 2 * MAX_REL + 1])
        rel_row = sb("rel_row", [1, 2 * GROUP])
        rel_flip = sb("rel_flip", [P, GROUP])
        rel = sb("rel", [P, 1, GROUP])
        z = sb("z", [P, TT * D])
        xnT = sb("xnT", [P, KC, T])
        sT = sb("sT", [P, T])
        lin = sb("lin", [P, 2, T])
        lcos = sb("lcos", [P, 2, T])
        lsin = sb("lsin", [P, 2, T])
        rope = sb("rope", [P, 2, T])
        v = sb("v", [P, TT, H])
        k_tok = sb("k_tok", [P, TT, P])
        sim = sb("sim", [P, TT, GROUP])
        att = sb("att", [P, TT, P])
        kv = sb("kv", [P, H])
        gT = sb("gT", [P, EC, T])
        oT = sb("oT", [P, EC, T])
        y = sb("y", [P, TT, D])
        zn = sb("zn", [P, TT, D])
        wz = sb("wz", [P, TT, D])
        rel_dram = nc.dram_tensor("rel_dram", (2 * GROUP,), F32, kind="Internal").ap()

        w_early, w_late, w_rows = sem("w_early"), sem("w_late"), sem("w_rows")
        pos_in, rel_out, rel_in = sem("pos_in"), sem("rel_out"), sem("rel_in")
        x_first, x_rest = sem("x_first"), sem("x_rest")
        fill = sem("fill")
        dve_step, pool_step = sem("dve_step"), sem("pool_step")
        var_ready, rstd_ready = sem("var_ready"), sem("rstd_ready")
        z_ready, zT_done, xn_ready = sem("z_ready"), sem("zT_done"), sem("xn_ready")
        qk_done, s_ready, lin_ready = sem("qk_done"), sem("s_ready"), sem("lin_ready")
        v_done, v_biased, v_ready = sem("v_done"), sem("v_biased"), sem("v_ready")
        turn_done, lcos_ready, rope_ready = sem("turn_done"), sem("lcos_ready"), sem("rope_ready")
        sim_done, att_ready = sem("sim_done"), sem("att_ready")
        kT_done, k_ready, kv_done, kv_ready = sem("kT_done"), sem("k_ready"), sem("kv_done"), sem("kv_ready")
        g_done, g_ready, o_done, o_ready, y_done = (sem(n) for n in ("g_done", "g_ready", "o_done", "o_ready", "y_done"))
        y_moved, zn_ready, wz_ready = sem("y_moved"), sem("zn_ready"), sem("wz_ready")

        block = ctx.enter_context(nc.Block())

        @block.sync
        def _(sp):
            sp.dma_start(batch_of(x, 0), w["x"][0]).then_inc(x_first, 16)
            sp.dma_start(ident[:, :], w["ident"]).then_inc(w_early, 16)
            sp.dma_start(ln1[:, 0, :], w["ln1_wT"]).then_inc(w_early, 16)
            sp.dma_start(ln1[:, 1, :], w["ln1_bT"]).then_inc(w_early, 16)
            sp.dma_start(wqk[:, :, :], w["Wqk2T"].rearrange("(k p) n -> p k n", p=P)).then_inc(w_early, 16)
            sp.dma_start(bqk[:, :], w["bqk2"]).then_inc(w_early, 16)
            sp.dma_start(gamma[:, :], w["gammaT"]).then_inc(w_early, 16)
            sp.dma_start(beta[:, :], w["betaT"]).then_inc(w_early, 16)
            sp.dma_start(wv[:, :, :], w["WvT"].rearrange("(k p) n -> p k n", p=P)).then_inc(w_late, 16)
            sp.dma_start(wg[:, :, :], w["WgT"].rearrange("(k p) n -> p k n", p=P)).then_inc(w_late, 16)
            sp.dma_start(turn[:, :], w["turn"]).then_inc(w_late, 16)
            sp.dma_start(bg[:, :], w["bgT"]).then_inc(w_late, 16)
            sp.dma_start(wo[:, :, :], w["WoT"].rearrange("(k p) n -> p k n", p=P)).then_inc(w_late, 16)
            for b in range(1, B):
                sp.dma_start(batch_of(x, b), w["x"][b]).then_inc(x_rest, 16)

        W_EARLY, W_LATE, W_ROWS = 16 * 7, 16 * 5, 16 * 6

        @block.gpsimd
        def _(pool):
            pool.memset(nm.mhalf[:, :], -0.5).then_inc(fill, 1)
            pool.memset(att[:, :, :], 0.0).then_inc(fill, 1)
            pool.wait_ge(w_rows, W_ROWS)
            pool.wait_ge(fill, 2)
            pool.wait_ge(var_ready, 1)
            nm.root(pool, rstd_ready)

            def rest(b, at):
                pool.wait_ge(var_ready, at)
                nm.root(pool, rstd_ready)
                pool.wait_ge(zn_ready, TT * b + TT)
                pool.tensor_tensor(wz[:, :, :], zn[:, :, :], ln2[:, 0:1, :].to_broadcast([P, TT, D]), ALU.mult)\
                    .then_inc(wz_ready, 1)
                pool.wait_ge(var_ready, at + 1)
                nm.root(pool, rstd_ready)

            def body(b, first=False, last=False):
                for j in (1, 0):
                    pool.wait_ge(lin_ready, 2 * b + 2 - j)
                    pool.tensor_tensor(lcos[:, j, :], lin[:, j, :], cos[:, :], ALU.mult).then_inc(lcos_ready, 1)
                if not first:
                    rest(b - 1, 3 * b)
                if not last:
                    pool.wait_ge(var_ready, 3 * b + 2)
                    nm.root(pool, rstd_ready)

            body(0, first=True)
            with pool.Fori(1, B - 1) as b:
                body(b)
            body(B - 1, last=True)
            rest(B - 1, 3 * B - 1)

        @block.scalar
        def _(act):
            act.dma_start(pos_row[:, :], w["pos_emb"].rearrange("(a n) -> a n", a=1)).then_inc(pos_in, 16)
            act.dma_start(cos[:, :], w["cos"]).then_inc(w_rows, 16)
            act.dma_start(sin[:, :], w["sin"]).then_inc(w_rows, 16)
            act.dma_start(bv_row[:, :], w["bv"].partition_broadcast(P)).then_inc(w_rows, 16)
            act.dma_start(bo_row[:, :], w["bo"].partition_broadcast(P)).then_inc(w_rows, 16)
            act.dma_start(ln2[:, 0, :], w["ln2_w"].partition_broadcast(P)).then_inc(w_rows, 16)
            act.dma_start(ln2[:, 1, :], w["ln2_b"].partition_broadcast(P)).then_inc(w_rows, 16)
            act.wait_ge(dve_step, 3)
            act.dma_start(rel_dram, rel_row[0, :]).then_inc(rel_out, 16)
            act.wait_ge(rel_out, 16)
            for g in range(2):
                act.dma_start(rel_flip[g * GROUP:(g + 1) * GROUP, :],
                              bass.AP(tensor=rel_dram.tensor, offset=0, ap=[[1, GROUP], [1, GROUP]])).then_inc(rel_in, 16)
            act.wait_ge(w_early, W_EARLY)
            act.wait_ge(w_late, W_LATE)

            def body(b):
                for k in range(KC):
                    act.wait_ge(zT_done, KC * b + k + 1)
                    nc.scalar.activation(xnT[:, k, :], bank[k][:, :], ACT.Identity, bias=ln1[:, 1, k:k + 1],
                                         scale=ln1[:, 0, k:k + 1]).then_inc(xn_ready, 1)
                act.wait_ge(qk_done, b + 1)
                nc.scalar.activation(sT[:, :], bank[2][:, :], ACT.Silu, bias=bqk[:, :]).then_inc(s_ready, 1)
                for t in range(TT):
                    act.wait_ge(v_biased, TT * b + t + 1)
                    nc.scalar.activation(v[:, t, :], v[:, t, :], ACT.Silu).then_inc(v_ready, 1)
                for e in range(EC):
                    if e == 2:
                        act.wait_ge(kT_done, b + 1)
                        nc.scalar.activation(k_tok[:, :, :], bank[7][:, :].rearrange("p (t n) -> p t n", t=TT),
                                             ACT.Copy).then_inc(k_ready, 1)
                    act.wait_ge(g_done, EC * b + e + 1)
                    nc.scalar.activation(gT[:, e, :], bank[5 + e % 2][:, :], ACT.Silu, bias=bg[:, e:e + 1])\
                        .then_inc(g_ready, 1)
                act.wait_ge(kv_done, b + 1)
                nc.scalar.activation(kv[QK:P, :], bank[7][QK:P, :], ACT.Copy, scale=1.0 / T).then_inc(kv_ready, 1)

            with act.Fori(0, B) as b:
                body(b)

        @block.vector
        def _(dve):
            steps = Steps(dve, dve_step)
            dve.wait_ge(pos_in, 16)
            steps.did(nc.vector.tensor_copy(rel_row[:, :], pos_row[:, MAX_REL:MAX_REL + 1].to_broadcast([1, 2 * GROUP])))
            steps.settle()
            mid = GROUP - 1
            steps.did(nc.vector.tensor_copy(rel_row[:, mid:mid + MAX_REL], pos_row[:, 0:MAX_REL]))
            steps.did(nc.vector.tensor_copy(rel_row[:, mid - MAX_REL + 1:mid], pos_row[:, 1:MAX_REL][:, ::-1]))
            dve.wait_ge(rel_in, 32)
            steps.did(nc.vector.tensor_copy(rel[:, 0, :], rel_flip[:, ::-1]))
            dve.wait_ge(w_early, W_EARLY)
            dve.wait_ge(w_rows, W_ROWS)
            dve.wait_ge(fill, 2)

            def front(b, at):
                nm.stats(nc, steps, [tile_of(x, b, t) for t in range(TT)], var_ready, twice=True)
                dve.wait_ge(rstd_ready, at)
                for t in range(TT):
                    nm.apply(nc, z[:, t * D:(t + 1) * D], tile_of(x, b, t), t).then_inc(z_ready, 1)

            def rest(b, at):
                dve.wait_ge(y_moved, TT // 2 * (b + 1))
                nm.stats(nc, steps, [y[:, t, :] for t in range(TT)], var_ready)
                dve.wait_ge(rstd_ready, at)
                for t in range(TT):
                    nm.apply(nc, zn[:, t, :], y[:, t, :], t).then_inc(zn_ready, 1)
                dve.wait_ge(wz_ready, b + 1)
                steps.did(nc.vector.tensor_tensor(y[:, :, :], wz[:, :, :], ln2[:, 1:2, :].to_broadcast([P, TT, D]), ALU.add))
                steps.settle()
                nm.stats(nc, steps, [y[:, t, :] for t in range(TT)], var_ready)
                dve.wait_ge(rstd_ready, at + 1)
                for t in range(TT):
                    steps.did(nm.apply(nc, zn[:, t, :], y[:, t, :], t))
                steps.settle()
                steps.did(nc.vector.tensor_tensor(batch_of(x, b), batch_of(x, b),
                                                  zn[:, :, :].rearrange("p t c -> p (t c)"), ALU.add))

            REST = 2 * Norm.STATS_STEPS + TT + 2

            def body(b, first=False, last=False):
                dve.wait_ge(s_ready, b + 1)
                for j in (1, 0):
                    nc.vector.tensor_scalar(lin[:, j, :], sT[:, :], gamma[:, j:j + 1], beta[:, j:j + 1],
                                            ALU.mult, ALU.add).then_inc(lin_ready, 1)
                for t in range(TT):
                    dve.wait_ge(v_done, TT * b + t + 1)
                    nc.vector.tensor_tensor(v[:, t, :], bank[5 + t % 2][:, :], bv_row[:, :], ALU.add)\
                        .then_inc(v_biased, 1)
                for i, j in enumerate((1, 0)):
                    dve.wait_ge(turn_done, 2 * b + i + 1)
                    steps.did(nc.vector.tensor_tensor(lsin[:, j, :], bank[3 + j][:, :], sin[:, :], ALU.mult))
                steps.settle()
                for i, j in enumerate((1, 0)):
                    dve.wait_ge(lcos_ready, 2 * b + i + 1)
                    nc.vector.tensor_tensor(rope[:, j, :], lcos[:, j, :], lsin[:, j, :], ALU.add).then_inc(rope_ready, 1)
                dve.wait_ge(sim_done, b + 1)
                for g in range(2):
                    rows = slice(g * GROUP, (g + 1) * GROUP)
                    steps.did(nc.vector.scalar_tensor_tensor(
                        out=sim[rows, :, :], in0=bank[2][rows, :].rearrange("p (t i) -> p t i", t=TT)[:, :, rows],
                        scalar=1.0 / GROUP, in1=rel[rows, :, :].to_broadcast([GROUP, TT, GROUP]), op0=ALU.mult, op1=ALU.add))
                steps.settle()
                for g in range(2):
                    rows = slice(g * GROUP, (g + 1) * GROUP)
                    nc.vector.scalar_tensor_tensor(out=att[rows, :, rows], in0=sim[rows, :, :], scalar=0.0,
                                                   in1=sim[rows, :, :], op0=ALU.max, op1=ALU.mult).then_inc(att_ready, 1)
                if not first:
                    rest(b - 1, 3 * b)
                if not last:
                    front(b + 1, 3 * b + 2)
                for e in range(EC):
                    dve.wait_ge(o_done, EC * b + e + 1)
                    dve.wait_ge(g_ready, EC * b + e + 1)
                    nc.vector.tensor_tensor(oT[:, e, :], bank[3 + e % 2][:, :], gT[:, e, :], ALU.mult).then_inc(o_ready, 1)
                for i in range(TT // 2):
                    dve.wait_ge(y_done, TT // 2 * b + i + 1)
                    nc.vector.tensor_tensor(y[:, 2 * i:2 * i + 2, :], bank[i][:, :].rearrange("p (t c) -> p t c", t=2),
                                            bo_row[:, :].rearrange("p (a c) -> p a c", a=1).to_broadcast([P, 2, D]),
                                            ALU.add).then_inc(y_moved, 1)

            BODY = 4 + Norm.STATS_STEPS + REST
            dve.wait_ge(x_first, 16)
            front(0, 1)
            dve.wait_ge(x_rest, 16 * (B - 1))
            body(0, first=True)
            steps.loop(1, B - 1, body, BODY)
            body(B - 1, last=True)
            rest(B - 1, 3 * B - 1)

        @block.tensor
        def _(pe):
            pe.wait_ge(w_early, W_EARLY)
            pe.wait_ge(w_late, W_LATE)
            pe.wait_ge(fill, 2)

            def gate(b, e):
                pe.wait_ge(v_biased, TT * b + 3 + e) if e < 2 else pe.wait_ge(g_ready, EC * b + e - 1)
                for k in range(KC):
                    last = nc.tensor.matmul(bank[5 + e % 2][:, :], wg[:, k, e * P:(e + 1) * P], xnT[:, k, :],
                                            start=k == 0, stop=k == KC - 1)
                last.then_inc(g_done, 1)

            def body(b):
                pe.wait_ge(z_ready, TT * b + TT)
                pe.wait_ge(y_moved, TT // 2 * b)
                for k in range(KC):
                    for t in range(TT):
                        last = nc.tensor.transpose(bank[k][:, t * P:(t + 1) * P],
                                                   z[:, t * D + k * P:t * D + (k + 1) * P], ident[:, :])
                    last.then_inc(zT_done, 1)
                pe.wait_ge(xn_ready, KC * b + KC)
                for k in range(KC):
                    last = nc.tensor.matmul(bank[2][:, :], wqk[:, k, :], xnT[:, k, :], start=k == 0, stop=k == KC - 1)
                last.then_inc(qk_done, 1)
                for t in range(TT):
                    if t < 2:
                        pe.wait_ge(g_ready, EC * b)
                    else:
                        pe.wait_ge(v_biased, TT * b + t - 1)
                    for k in range(KC):
                        last = nc.tensor.matmul(bank[5 + t % 2][:, :], xnT[:, k, t * P:(t + 1) * P], wv[:, k, :],
                                                start=k == 0, stop=k == KC - 1)
                    last.then_inc(v_done, 1)
                for i, j in enumerate((1, 0)):
                    pe.wait_ge(lin_ready, 2 * b + i + 1)
                    pe.wait_ge(o_ready, EC * b)
                    nc.tensor.matmul(bank[3 + j][:, :], turn[:, :], lin[:, j, :], start=True, stop=True).then_inc(turn_done, 1)
                gate(b, 0)
                gate(b, 1)
                pe.wait_ge(rope_ready, 2 * b + 2)
                for t in range(TT):
                    ts = slice(t * P, (t + 1) * P)
                    last = nc.tensor.matmul(bank[2][:, ts], rope[0:QK, 1, ts], rope[0:QK, 0, ts], start=True, stop=True)
                last.then_inc(sim_done, 1)
                pe.wait_ge(kv_ready, b)
                for t in range(TT):
                    ts = slice(t * P, (t + 1) * P)
                    last = nc.tensor.transpose(bank[7][:, ts], rope[:, 1, ts], ident[:, :])
                last.then_inc(kT_done, 1)
                gate(b, 2)
                gate(b, 3)
                pe.wait_ge(k_ready, b + 1)
                pe.wait_ge(v_ready, TT * b + TT)
                for t in range(TT):
                    last = nc.tensor.matmul(bank[7][:, :], k_tok[:, t, :], v[:, t, :], start=t == 0, stop=t == TT - 1)
                last.then_inc(kv_done, 1)
                pe.wait_ge(kv_ready, b + 1)
                pe.wait_ge(att_ready, 2 * b + 2)
                for e in range(EC):
                    es = slice(e * P, (e + 1) * P)
                    if e >= 2:
                        pe.wait_ge(o_ready, EC * b + e - 1)
                    nc.tensor.matmul(bank[3 + e % 2][:, :], kv[QK:P, es], rope[QK:P, 0, :], start=True, stop=False)
                    for t in range(TT):
                        ts = slice(t * P, (t + 1) * P)
                        last = nc.tensor.matmul(bank[3 + e % 2][:, ts], v[:, t, es], att[:, t, :], start=False,
                                                stop=t == TT - 1)
                    last.then_inc(o_done, 1)
                pe.wait_ge(o_ready, EC * b + EC)
                for t in range(TT):
                    for e in range(EC):
                        last = nc.tensor.matmul(bank[t // 2][:, (t % 2) * D:(t % 2 + 1) * D],
                                                oT[:, e, t * P:(t + 1) * P], wo[:, e, :], start=e == 0, stop=e == EC - 1)
                    if t % 2:
                        last.then_inc(y_done, 1)

            with pe.Fori(0, B) as b:
                body(b)


def mix_layer(nc, s, w):
    x, nm, bank, ident = s.x, s.norm, s.bank, s.ident
    with ExitStack() as ctx:
        sb = lambda n, shape, d=F32: ctx.enter_context(nc.sbuf_tensor("mix_" + n, shape, d))
        sem = lambda n: ctx.enter_context(nc.semaphore("mix_" + n))
        wr, wk, wv = (sb(n, [P, KC, D]) for n in ("wr", "wk", "wv"))
        mu = sb("mu", [P, 2, KC])
        z = sb("z", [P, TT * D])
        zT = sb("zT", [P, KC, T + 1])
        dT = sb("dT", [P, KC, T])
        xrT, xkT = sb("xrT", [P, KC, T]), sb("xkT", [P, KC, T])
        kT = sb("kT", [P, KC, T])
        kaT = sb("kaT", [P, KC, T])
        r = sb("r", [P, TT, D])
        y = sb("y", [P, TT, D])
        zn = sb("zn", [P, TT, D])

        w_in, fill, dve_step = sem("w_in"), sem("fill"), sem("dve_step")
        var_ready, rstd_ready = sem("var_ready"), sem("rstd_ready")
        z_ready, zT_done, zT_ready = sem("z_ready"), sem("zT_done"), sem("zT_ready")
        d_ready, xk_ready, xr_ready = sem("d_ready"), sem("xk_ready"), sem("xr_ready")
        k_done, k_ready, ka_ready = sem("k_done"), sem("k_ready"), sem("ka_ready")
        r_done, r_ready, kv_done, y_ready = sem("r_done"), sem("r_ready"), sem("kv_done"), sem("y_ready")

        block = ctx.enter_context(nc.Block())
        W_IN = 16 * 5

        @block.sync
        def _(sp):
            for dst, src in ((wk, w["ffn_WkT"]), (wr, w["ffn_WrT"]), (wv, w["ffn_WvT"])):
                sp.dma_start(dst[:, :, :], src.rearrange("(k p) n -> p k n", p=P)).then_inc(w_in, 16)
            sp.dma_start(mu[:, 0, :], w["mu_rT"]).then_inc(w_in, 16)
            sp.dma_start(mu[:, 1, :], w["mu_kT"]).then_inc(w_in, 16)

        @block.gpsimd
        def _(pool):
            pool.memset(zT[:, :, 0:1], 0.0).then_inc(fill, 1)
            pool.wait_ge(fill, 1)

            def body(b, first=False, last=False):
                for m in range(KC):
                    pool.wait_ge(k_ready, KC * b + m + 1)
                    pool.tensor_tensor(kaT[:, m, :], kT[:, m, :], kT[:, m, :], ALU.mult).then_inc(ka_ready, 1)
                if not last:
                    pool.wait_ge(var_ready, 2 * b + 2)
                    nm.root(pool, rstd_ready)
                pool.wait_ge(var_ready, 2 * b + (2 if last else 3))
                nm.root(pool, rstd_ready)

            pool.wait_ge(var_ready, 1)
            nm.root(pool, rstd_ready)
            with pool.Fori(0, B - 1) as b:
                body(b)
            body(B - 1, last=True)

        @block.scalar
        def _(act):
            with act.Fori(0, B) as b:
                for k in range(KC):
                    act.wait_ge(zT_done, KC * b + k + 1)
                    nc.scalar.activation(zT[:, k, 1:T + 1], bank[k][:, :], ACT.Copy).then_inc(zT_ready, 1)
                for m in range(KC):
                    act.wait_ge(k_done, KC * b + m + 1)
                    nc.scalar.activation(kT[:, m, :], bank[2 + m][:, :], ACT.Relu).then_inc(k_ready, 1)
                for i in range(TT // 2):
                    act.wait_ge(r_done, TT // 2 * b + i + 1)
                    nc.scalar.activation(r[:, 2 * i:2 * i + 2, :], bank[4 + i][:, :].rearrange("p (t c) -> p t c", t=2),
                                         ACT.Sigmoid).then_inc(r_ready, 1)

        @block.vector
        def _(dve):
            steps = Steps(dve, dve_step)

            def front(b, at):
                nm.stats(nc, steps, [tile_of(x, b, t) for t in range(TT)], var_ready)
                dve.wait_ge(rstd_ready, at)
                for t in range(TT):
                    nm.apply(nc, z[:, t * D:(t + 1) * D], tile_of(x, b, t), t).then_inc(z_ready, 1)

            def body(b, last=False):
                for k in range(KC):
                    dve.wait_ge(zT_ready, KC * b + k + 1)
                    steps.did(nc.vector.tensor_tensor(dT[:, k, :], zT[:, k, 1:T + 1], zT[:, k, 0:T], ALU.subtract))
                steps.settle()
                for i, (dst, ready) in enumerate(((xkT, xk_ready), (xrT, xr_ready))):
                    for k in range(KC):
                        nc.vector.scalar_tensor_tensor(out=dst[:, k, :], in0=dT[:, k, :], scalar=mu[:, 1 - i, k:k + 1],
                                                       in1=zT[:, k, 0:T], op0=ALU.mult, op1=ALU.add).then_inc(ready, 1)
                if not last:
                    front(b + 1, 2 * b + 2)
                for i in range(TT // 2):
                    dve.wait_ge(kv_done, TT // 2 * b + i + 1)
                    dve.wait_ge(r_ready, TT // 2 * b + i + 1)
                    nc.vector.tensor_tensor(y[:, 2 * i:2 * i + 2, :], bank[6 + i][:, :].rearrange("p (t c) -> p t c", t=2),
                                            r[:, 2 * i:2 * i + 2, :], ALU.mult).then_inc(y_ready, 1)
                dve.wait_ge(y_ready, TT // 2 * b + TT // 2)
                nm.stats(nc, steps, [y[:, t, :] for t in range(TT)], var_ready)
                dve.wait_ge(rstd_ready, 2 * b + (2 if last else 3))
                for t in range(TT):
                    steps.did(nm.apply(nc, zn[:, t, :], y[:, t, :], t))
                steps.settle()
                steps.did(nc.vector.tensor_tensor(batch_of(x, b), batch_of(x, b),
                                                  zn[:, :, :].rearrange("p t c -> p (t c)"), ALU.add))

            front(0, 1)
            dve.wait_ge(w_in, W_IN)
            dve.wait_ge(fill, 1)
            steps.loop(0, B - 1, body, KC + 2 * Norm.STATS_STEPS + TT + 1)
            body(B - 1, last=True)

        @block.tensor
        def _(pe):
            pe.wait_ge(w_in, W_IN)
            with pe.Fori(0, B) as b:
                pe.wait_ge(z_ready, TT * b + TT)
                for k in range(KC):
                    for t in range(TT):
                        last = nc.tensor.transpose(bank[k][:, t * P:(t + 1) * P],
                                                   z[:, t * D + k * P:t * D + (k + 1) * P], ident[:, :])
                    last.then_inc(zT_done, 1)
                pe.wait_ge(xk_ready, KC * b + KC)
                for m in range(KC):
                    for k in range(KC):
                        last = nc.tensor.matmul(bank[2 + m][:, :], wk[:, k, m * P:(m + 1) * P], xkT[:, k, :],
                                                start=k == 0, stop=k == KC - 1)
                    last.then_inc(k_done, 1)
                pe.wait_ge(xr_ready, KC * b + KC)
                for t in range(TT):
                    for k in range(KC):
                        last = nc.tensor.matmul(bank[4 + t // 2][:, (t % 2) * D:(t % 2 + 1) * D],
                                                xrT[:, k, t * P:(t + 1) * P], wr[:, k, :], start=k == 0, stop=k == KC - 1)
                    if t % 2:
                        last.then_inc(r_done, 1)
                pe.wait_ge(ka_ready, KC * b + KC)
                pe.wait_ge(y_ready, TT // 2 * b)
                for t in range(TT):
                    for m in range(KC):
                        last = nc.tensor.matmul(bank[6 + t // 2][:, (t % 2) * D:(t % 2 + 1) * D],
                                                kaT[:, m, t * P:(t + 1) * P], wv[:, m, :], start=m == 0, stop=m == KC - 1)
                    if t % 2:
                        last.then_inc(kv_done, 1)


def hedgehog_layer(nc, s, w):
    x, nm, bank, ident = s.x, s.norm, s.bank, s.ident
    NF = 2 * HEADS * 2 * HD
    QW = NF // 2
    with ExitStack() as ctx:
        sb = lambda n, shape, d=F32: ctx.enter_context(nc.sbuf_tensor("hh_" + n, shape, d))
        sem = lambda n: ctx.enter_context(nc.semaphore("hh_" + n))
        rows = sb("rows", [P, 2 * KC, D])
        maps = sb("maps", [P, 2, P])
        wqk = sb("wqk", [P, KC, 2 * D])
        wv, wo = sb("wv", [P, KC, D]), sb("wo", [P, KC, D])
        bias = sb("bias", [P, 2, 1, HD])
        causal = sb("causal", [P, 1, P])
        z = sb("z", [P, TT * D])
        zT = sb("zT", [P, KC, T])
        p = sb("p", [P, 2 * HEADS, HD])
        pmax, pmin = sb("pmax", [P, 2 * HEADS, 1]), sb("pmin", [P, 2 * HEADS, 1])
        ex = sb("ex", [P, 2 * HEADS, 2, HD])
        tot, rtot = sb("tot", [P, 4 * HEADS, 1]), sb("rtot", [P, 4 * HEADS, 1])
        feat = sb("feat", [P, 2, NF])
        v1 = sb("v1", [P, 2, HEADS, VW])
        qT, kT = sb("qT", [P, FC * P]), sb("kT", [P, FC * P])
        att = sb("att", [P, HPC, FC, P])
        state = sb("state", [P, FC, HPC * VW])
        den, rden = sb("den", [P, HEADS]), sb("rden", [P, HEADS, 1])
        y = sb("y", [P, HEADS, HD])
        yT = sb("yT", [P, KC, P])
        o = sb("o", [P, TT, D])
        zn = sb("zn", [P, TT, D])
        b_y, b_st = bank[6], bank[7]
        YW = HEADS * VW

        w_in, fill, comp_done, comp_ready, dve_step = (sem(n) for n in ("w_in", "fill", "comp_done", "comp_ready", "dve_step"))
        map_in = sem("map_in")
        var_ready, rstd_ready = sem("var_ready"), sem("rstd_ready")
        z_ready, zT_done, zT_ready = sem("z_ready"), sem("zT_done"), sem("zT_ready")
        p_done, v_done, p_ready, v_ready = sem("p_done"), sem("v_done"), sem("p_ready"), sem("v_ready")
        max_ready, arg_ready, exp_ready, feat_ready = sem("max_ready"), sem("arg_ready"), sem("exp_ready"), sem("feat_ready")
        fT_done, fT_ready, sc_done = sem("fT_done"), sem("fT_ready"), sem("sc_done")
        even_ready, odd_moved, odd_ready = sem("even_ready"), sem("odd_moved"), sem("odd_ready")
        y_done, y_ready, st_done, st_ready = sem("y_done"), sem("y_ready"), sem("st_done"), sem("st_ready")
        yT_done, yT_ready, o_done, o_ready, o_read = (sem(n) for n in ("yT_done", "yT_ready", "o_done", "o_ready", "o_read"))

        block = ctx.enter_context(nc.Block())
        W_IN, MAP_IN = 16 * 4, 16 * 18

        @block.sync
        def _(sp):
            sp.dma_start(rows[:, :, :], w["w_qk"].rearrange("(m p) c -> p m c", p=P)).then_inc(w_in, 16)
            sp.dma_start(wv[:, :, :], w["w_vT"].rearrange("(k p) n -> p k n", p=P)).then_inc(w_in, 16)
            sp.dma_start(wo[:, :, :], w["w_outT"].rearrange("(k p) n -> p k n", p=P)).then_inc(w_in, 16)
            sp.dma_start(causal[:, 0, :], w["causal"]).then_inc(w_in, 16)
            sp.dma_start(bias[:, 0, 0, :], w["bq_map"].partition_broadcast(P)).then_inc(map_in, 16)
            sp.dma_start(bias[:, 1, 0, :], w["bk_map"].partition_broadcast(P)).then_inc(map_in, 16)
            sp.wait_ge(fill, 1)
            for m, src in ((0, w["wq_mapT"]), (1, w["wk_mapT"])):
                for h in range(P // HD):
                    hs = slice(h * HD, (h + 1) * HD)
                    sp.dma_start(maps[hs, m, hs], src).then_inc(map_in, 16)

        @block.gpsimd
        def _(pool):
            pool.memset(maps[:, :, :], 0.0).then_inc(fill, 1)
            pool.memset(v1[:, :, :, HD:VW], 1.0).then_inc(fill, 1)
            pool.memset(state[:, :, :], 0.0).then_inc(fill, 1)
            pool.wait_ge(fill, 3)
            pool.wait_ge(var_ready, 1)
            nm.root(pool, rstd_ready)

            def args(g):
                pool.wait_ge(max_ready, 2 * g + 1)
                pool.tensor_tensor(ex[:, :, 0, :], p[:, :, :], pmax[:, :, :].to_broadcast([P, 2 * HEADS, HD]),
                                   ALU.subtract).then_inc(arg_ready, 1)
                pool.wait_ge(max_ready, 2 * g + 2)
                pool.tensor_tensor(ex[:, :, 1, :], pmin[:, :, :].to_broadcast([P, 2 * HEADS, HD]), p[:, :, :],
                                   ALU.subtract).then_inc(arg_ready, 1)

            def body(b, first=False, last=False):
                for t in range(TT):
                    g = TT * b + t
                    for i in range(HPC // 2):
                        pool.wait_ge(odd_moved, HPC // 2 * g + i + 1)
                        pool.tensor_tensor(att[:, 2 * i + 1, :, :], att[:, 2 * i + 1, :, :],
                                           causal[:, :, :].to_broadcast([P, FC, P]), ALU.mult).then_inc(odd_ready, 1)
                    if not (last and t == TT - 1):
                        args(g + 1)
                    if t == 1 and not first:
                        pool.wait_ge(var_ready, 2 * b + 1)
                        nm.root(pool, rstd_ready)
                    if t == 1 and not last:
                        pool.wait_ge(var_ready, 2 * b + 2)
                        nm.root(pool, rstd_ready)

            args(0)
            body(0, first=True)
            with pool.Fori(1, B - 1) as b:
                body(b)
            body(B - 1, last=True)
            pool.wait_ge(var_ready, 2 * B)
            nm.root(pool, rstd_ready)

        @block.scalar
        def _(act):
            def copy(out, in_, ready):
                nc.scalar.activation(out, in_, ACT.Copy).then_inc(ready, 1)

            def move_zT(b):
                for k in range(KC):
                    act.wait_ge(zT_done, KC * b + k + 1)
                    copy(zT[:, k, :], bank[k][:, :], zT_ready)

            def move_v(g, par):
                act.wait_ge(v_done, g + 1)
                copy(v1[:, par, :, 0:HD], bank[3][:, 0:D].rearrange("p (h e) -> p h e", h=HEADS), v_ready)

            def exps(g):
                act.wait_ge(arg_ready, 2 * g + 2)
                nc.scalar.activation(ex[:, :, :, :], ex[:, :, :, :], ACT.Exp).then_inc(exp_ready, 1)

            def move_yT(g):
                act.wait_ge(yT_done, g + 1)
                for k in range(KC):
                    copy(yT[:, k, :], bank[6 + k][:, YW:YW + P], yT_ready)

            def move_o(g, t, b_read):
                if t == 0:
                    act.wait_ge(o_read, TT * b_read)
                act.wait_ge(o_done, g + 1)
                copy(o[:, t, :], bank[3][:, D:2 * D], o_ready)

            def body(b, first=False, last=False):
                for t in range(TT):
                    g = TT * b + t
                    before = not (first and t == 0)
                    for i, dst in enumerate((qT, kT)):
                        act.wait_ge(fT_done, 2 * g + i + 1)
                        copy(dst[:, :], bank[i][:, :], fT_ready)
                    if before:
                        move_yT(g - 1)
                    if not (last and t == TT - 1):
                        move_v(g + 1, (t + 1) % 2)
                    for i in range(HPC // 2):
                        act.wait_ge(sc_done, HPC * g + 2 * i + 2)
                        copy(att[:, 2 * i + 1, :, :], bank[5][:, :].rearrange("p (c i) -> p c i", c=FC), odd_moved)
                    if not (last and t == TT - 1):
                        exps(g + 1)
                    if before:
                        move_o(g - 1, (t - 1) % TT, b)
                    if t == 2 and not last:
                        move_zT(b + 1)

            act.wait_ge(comp_done, 2)
            for k in range(KC):
                copy(wqk[:, k, :], bank[4 + k][:, :], comp_ready)
            act.wait_ge(fill, 3)
            move_zT(0)
            move_v(0, 0)
            exps(0)
            body(0, first=True)
            with act.Fori(1, B - 1) as b:
                body(b)
            body(B - 1, last=True)
            move_yT(TT * B - 1)
            move_o(TT * B - 1, TT - 1, B)

        @block.vector
        def _(dve):
            steps = Steps(dve, dve_step)

            def front(b, at):
                nm.stats(nc, steps, [tile_of(x, b, t) for t in range(TT)], var_ready)
                dve.wait_ge(rstd_ready, at)
                for t in range(TT):
                    nm.apply(nc, z[:, t * D:(t + 1) * D], tile_of(x, b, t), t).then_inc(z_ready, 1)

            def rest(b, at):
                dve.wait_ge(o_ready, TT * b + TT)
                nm.stats(nc, steps, [o[:, t, :] for t in range(TT)], var_ready)
                dve.wait_ge(rstd_ready, at)
                for t in range(TT):
                    nm.apply(nc, zn[:, t, :], o[:, t, :], t).then_inc(o_read, 1)
                dve.wait_ge(o_read, TT * b + TT)
                steps.did(nc.vector.tensor_tensor(batch_of(x, b), batch_of(x, b),
                                                  zn[:, :, :].rearrange("p t c -> p (t c)"), ALU.add))

            def project(g):
                dve.wait_ge(p_done, g + 1)
                nc.vector.tensor_tensor(p[:, :, :].rearrange("p (m h) e -> p m h e", m=2),
                                        bank[2][:, :].rearrange("p (m h e) -> p m h e", m=2, h=HEADS),
                                        bias[:, :, :, :].to_broadcast([P, 2, HEADS, HD]), ALU.add).then_inc(p_ready, 1)
                dve.wait_ge(p_ready, g + 1)
                nc.vector.tensor_reduce(pmax[:, :, 0], p[:, :, :], AX.X, ALU.max).then_inc(max_ready, 1)
                nc.vector.tensor_reduce(pmin[:, :, 0], p[:, :, :], AX.X, ALU.min).then_inc(max_ready, 1)

            def softmax(g, par):
                dve.wait_ge(exp_ready, g + 1)
                e = ex[:, :, :, :].rearrange("p h s e -> p (h s) e")
                steps.did(nc.vector.tensor_reduce(tot[:, :, 0], e, AX.X, ALU.add))
                steps.settle()
                steps.did(nc.vector.reciprocal(rtot[:, :, :], tot[:, :, :]))
                steps.settle()
                nc.vector.tensor_tensor(feat[:, par, :].rearrange("p (h e) -> p h e", e=HD), e,
                                        rtot[:, :, :].to_broadcast([P, 4 * HEADS, HD]), ALU.mult).then_inc(feat_ready, 1)

            def body(b, first=False, last=False):
                for t in range(TT):
                    g = TT * b + t
                    nxt = not (last and t == TT - 1)
                    if nxt:
                        project(g + 1)
                    for i in range(HPC // 2):
                        dve.wait_ge(sc_done, HPC * g + 2 * i + 1)
                        nc.vector.tensor_tensor(att[:, 2 * i, :, :], bank[4][:, :].rearrange("p (c i) -> p c i", c=FC),
                                                causal[:, :, :].to_broadcast([P, FC, P]), ALU.mult).then_inc(even_ready, 1)
                    if t == 1 and not first:
                        rest(b - 1, 2 * b + 1)
                    if t == 1 and not last:
                        front(b + 1, 2 * b + 2)
                    if nxt:
                        softmax(g + 1, (t + 1) % 2)
                    dve.wait_ge(y_done, g + 1)
                    yv = b_y[:, 0:YW].rearrange("p (h e) -> p h e", e=VW)
                    steps.did(nc.vector.tensor_scalar(den[:, :], yv[:, :, HD], 1e-6, None, ALU.max))
                    steps.settle()
                    steps.did(nc.vector.reciprocal(rden[:, :, 0], den[:, :]))
                    steps.settle()
                    nc.vector.tensor_tensor(y[:, :, :], yv[:, :, 0:HD], rden[:, :, :].to_broadcast([P, HEADS, HD]),
                                            ALU.mult).then_inc(y_ready, 1)
                    if t < TT - 1:
                        dve.wait_ge(st_done, (TT - 1) * b + t + 1)
                        for r in range(HPC):
                            rs, cs = slice(r * 2 * HD, (r + 1) * 2 * HD), slice(r * VW, (r + 1) * VW)
                            blk = state[rs, :, cs]
                            nc.vector.tensor_tensor(blk, blk, b_st[rs, 0:YW].rearrange("p (c n) -> p c n", c=FC)[:, :, cs],
                                                    ALU.add).then_inc(st_ready, 1)
                    elif not last:
                        for r in range(HPC):
                            rs, cs = slice(r * 2 * HD, (r + 1) * 2 * HD), slice(r * VW, (r + 1) * VW)
                            nc.vector.memset(state[rs, :, cs], 0.0).then_inc(st_ready, 1)

            front(0, 1)
            dve.wait_ge(map_in, MAP_IN)
            dve.wait_ge(w_in, W_IN)
            project(0)
            softmax(0, 0)
            BODY = TT * 4 + 1 + 2 * Norm.STATS_STEPS
            dve.wait_ge(fill, 3)
            body(0, first=True)
            steps.loop(1, B - 1, body, BODY)
            body(B - 1, last=True)
            rest(B - 1, 2 * B)

        @block.tensor
        def _(pe):
            def trans_z(b):
                pe.wait_ge(z_ready, TT * b + TT)
                for k in range(KC):
                    for t in range(TT):
                        last = nc.tensor.transpose(bank[k][:, t * P:(t + 1) * P],
                                                   z[:, t * D + k * P:t * D + (k + 1) * P], ident[:, :])
                    last.then_inc(zT_done, 1)

            def qkv(g, t, par_free=None):
                for k in range(KC):
                    last = nc.tensor.matmul(bank[2][:, :], zT[:, k, t * P:(t + 1) * P], wqk[:, k, :],
                                            start=k == 0, stop=k == KC - 1)
                last.then_inc(p_done, 1)
                for k in range(KC):
                    last = nc.tensor.matmul(bank[3][:, 0:D], zT[:, k, t * P:(t + 1) * P], wv[:, k, :],
                                            start=k == 0, stop=k == KC - 1)
                last.then_inc(v_done, 1)

            def trans_y(g, n_state):
                pe.wait_ge(y_ready, g + 1)
                pe.wait_ge(st_ready, n_state)
                for k in range(KC):
                    last = nc.tensor.transpose(bank[6 + k][:, YW:YW + P],
                                               y[:, k * HEADS // KC:(k + 1) * HEADS // KC, :].rearrange("p h e -> p (h e)"),
                                               ident[:, :])
                last.then_inc(yT_done, 1)

            def out(g):
                pe.wait_ge(yT_ready, KC * g + KC)
                pe.wait_ge(o_ready, g)
                for k in range(KC):
                    last = nc.tensor.matmul(bank[3][:, D:2 * D], yT[:, k, :], wo[:, k, :], start=k == 0, stop=k == KC - 1)
                last.then_inc(o_done, 1)

            def body(b, first=False, last=False):
                for t in range(TT):
                    g, par = TT * b + t, t % 2
                    before = not (first and t == 0)
                    pe.wait_ge(feat_ready, g + 1)
                    if t == 3 and not last:
                        pe.wait_ge(zT_ready, KC * b + 2 * KC)
                    for i in range(2):
                        for c in range(FC):
                            f = i * QW + c * P
                            mm = nc.tensor.transpose(bank[i][:, c * P:(c + 1) * P], feat[:, par, f:f + P], ident[:, :])
                        mm.then_inc(fT_done, 1)
                    if before:
                        trans_y(g - 1, HPC * g)
                    nxt = not (last and t == TT - 1)
                    if nxt:
                        if before:
                            pe.wait_ge(o_ready, g - 1)
                        pe.wait_ge(v_ready, g + 1)
                        pe.wait_ge(p_ready, g + 1)
                        qkv(g + 1, (t + 1) % TT)
                    pe.wait_ge(fT_ready, 2 * g + 2)
                    for r in range(HPC):
                        rs = slice(r * 2 * HD, (r + 1) * 2 * HD)
                        if r % 2 == 0:
                            pe.wait_ge(even_ready, HPC // 2 * g + r // 2)
                        else:
                            pe.wait_ge(odd_moved, HPC // 2 * g + r // 2)
                        for c in range(FC):
                            cs = slice(c * P, (c + 1) * P)
                            mm = nc.tensor.matmul(bank[4 + r % 2][:, cs], kT[rs, cs], qT[rs, cs], start=True, stop=True)
                        mm.then_inc(sc_done, 1)
                    if before:
                        if nxt:
                            pe.wait_ge(v_ready, g + 2)
                        out(g - 1)
                    pe.wait_ge(st_ready, HPC * g)
                    for c in range(FC):
                        nc.tensor.matmul(b_y[:, c * HPC * VW:(c + 1) * HPC * VW], qT[:, c * P:(c + 1) * P],
                                         state[:, c, :], start=c == 0, stop=False)
                    for r in range(HPC):
                        if r % 2 == 0:
                            pe.wait_ge(even_ready, HPC // 2 * g + r // 2 + 1)
                        else:
                            pe.wait_ge(odd_ready, HPC // 2 * g + r // 2 + 1)
                        for c in range(FC):
                            h = HPC * c + r
                            mm = nc.tensor.matmul(b_y[:, h * VW:(h + 1) * VW], att[:, r, c, :], v1[:, par, h, :],
                                                  start=False, stop=r == HPC - 1 and c == FC - 1)
                    mm.then_inc(y_done, 1)
                    if t < TT - 1:
                        for c in range(FC):
                            mm = nc.tensor.matmul(b_st[:, c * HPC * VW:(c + 1) * HPC * VW],
                                                  feat[:, par, QW + c * P:QW + (c + 1) * P],
                                                  v1[:, par, c * HPC:(c + 1) * HPC, :].rearrange("p h e -> p (h e)"),
                                                  start=True, stop=True)
                        mm.then_inc(st_done, 1)
                    if t == 2 and not last:
                        trans_z(b + 1)

            pe.wait_ge(w_in, W_IN)
            pe.wait_ge(map_in, MAP_IN)
            for k in range(KC):
                for m in range(2 * KC):
                    mm = nc.tensor.matmul(bank[4 + k][:, m * P:(m + 1) * P], rows[:, m, k * P:(k + 1) * P],
                                          maps[:, m // KC, :], start=True, stop=True)
                mm.then_inc(comp_done, 1)
            trans_z(0)
            pe.wait_ge(comp_ready, 2)
            pe.wait_ge(zT_ready, KC)
            qkv(0, 0)
            pe.wait_ge(fill, 3)
            body(0, first=True)
            with pe.Fori(1, B - 1) as b:
                body(b)
            body(B - 1, last=True)
            trans_y(TT * B - 1, HPC * (TT * B - 1))
            out(TT * B - 1)


G_TILES = B * TT
ZW = D + NE
BLK = CAP // P
BITS = 30


def route(nc, s, w):
    x, nm, bank, ident = s.x, s.norm, s.bank, s.ident
    GE = G_TILES * NE
    with ExitStack() as ctx:
        sb = lambda n, shape, d=F32: ctx.enter_context(nc.sbuf_tensor("rt_" + n, shape, d))
        sem = lambda n: ctx.enter_context(nc.semaphore("rt_" + n))
        wg = sb("wg", [P, KC, NE])
        z = sb("z", [P, 2, TT * D])
        zT = sb("zT", [P, KC, T])
        ones, below = sb("ones", [P, P], BF16), sb("below", [P, P], BF16)
        lo_row = sb("lo_row", [P, P], BF16)
        hi_row = sb("hi_row", [P, 1, BLK])
        tile_no = sb("tile_no", [P, GE, 1])
        lane_no = sb("lane_no", [P, 1])
        carry_on = sb("carry_on", [P, GE])
        bit, next_bit = sb("bit", [P, BITS]), sb("next_bit", [P, BITS], I32)
        zeros = sb("zeros", [P, TT * D])
        top, rsum, esum = sb("top", [P, G_TILES, 1]), sb("rsum", [P, G_TILES, 1]), sb("esum", [P, G_TILES, 1])
        score = sb("score", [P, G_TILES, NE])
        by_exp = sb("by_exp", [P, NE, G_TILES])
        flag, take = sb("flag", [P, NE, G_TILES], BF16), sb("take", [P, NE, G_TILES], BF16)
        chosen = sb("chosen", [P, NE, G_TILES], BF16)
        part = sb("part", [P, NE], BF16)
        inc, low, cand = (sb(n, [P, NE, 1], I32) for n in ("inc", "low", "cand"))
        need = sb("need", [P, NE, 1])
        total, upto, rank = sb("total", [P, GE]), sb("upto", [P, GE]), sb("rank", [P, GE])
        slot, lo_i, hi_i = (sb(n, [P, GE], I32) for n in ("slot", "lo_i", "hi_i"))
        lo, hi = sb("lo", [P, GE]), sb("hi", [P, GE, 1])
        hot_hi = sb("hot_hi", [P, GE, BLK])
        number = sb("number", [P, GE, 2, BLK], BF16)
        hot_lo = sb("hot_lo", [P, 2, G_TILES, P], BF16)
        pair = sb("pair", [P, NE, 2, BLK])

        w_in, c_in, fill, dve_step = sem("w_in"), sem("c_in"), sem("fill"), sem("dve_step")
        var_ready, rstd_ready, z_ready = sem("var_ready"), sem("rstd_ready"), sem("z_ready")
        zT_done, zT_ready, logits_done = sem("zT_done"), sem("zT_ready"), sem("logits_done")
        z_out, zero_out, score_out = [sem("z_out0"), sem("z_out1")], sem("zero_out"), sem("score_out")
        shifted, exp_ready, score_ready = sem("shifted"), sem("exp_ready"), sem("score_ready")
        part_ready, count_done, flags_ready, ranks_done = sem("part_ready"), sem("count_done"), sem("flags_ready"), sem("ranks_done")
        number_ready = sem("number_ready")
        hot_ready, hot_used = [sem("hot_ready0"), sem("hot_ready1")], [sem("hot_used0"), sem("hot_used1")]
        block = ctx.enter_context(nc.Block())
        C_IN = 16 * 9
        z_rows = s.z_dram.rearrange("(g p) c -> p g c", p=P)
        acc_rows = s.acc_dram.rearrange("(g p) c -> p g c", p=P)

        @block.sync
        def _(sp):
            sp.dma_start(wg[:, :, :], w["wg"].rearrange("(k p) n -> p k n", p=P)).then_inc(w_in, 16)
            for dst, src in ((ones[:, :], w["ones"]), (below[:, :], w["below"]), (lo_row[:, :], w["lo_row"]),
                             (hi_row[:, 0, :], w["hi_row"]), (tile_no[:, :, 0], w["tile_no"]), (lane_no[:, :], w["lane_no"]),
                             (carry_on[:, :], w["carry_on"]), (bit[:, :], w["bit"]), (next_bit[:, :], w["next_bit"])):
                sp.dma_start(dst, src).then_inc(c_in, 16)
            sp.wait_ge(fill, 1)
            with sp.Fori(0, B // 2) as i:
                for par in range(2):
                    b = 2 * i + par
                    sp.wait_ge(z_ready, TT * b + TT)
                    sp.dma_start(z_rows[:, bass.ds(TT * b, TT), 0:D], z[:, par, :].rearrange("p (t c) -> p t c", t=TT))\
                        .then_inc(z_out[par], 16)
                    sp.dma_start(acc_rows[:, bass.ds(TT * b, TT), :], zeros[:, :].rearrange("p (t c) -> p t c", t=TT))\
                        .then_inc(zero_out, 16)
            sp.wait_ge(score_ready, 1)
            sp.dma_start(z_rows[:, :, D:ZW], score[:, :, :]).then_inc(score_out, 16)
            for par in range(2):
                sp.wait_ge(z_out[par], 16 * B // 2)
            sp.wait_ge(zero_out, 16 * B)
            sp.wait_ge(score_out, 16)

        @block.gpsimd
        def _(pool):
            pool.memset(zeros[:, :], 0.0).then_inc(fill, 1)
            with pool.Fori(0, B) as b:
                pool.wait_ge(var_ready, b + 1)
                nm.root(pool, rstd_ready)

        @block.scalar
        def _(act):
            with act.Fori(0, B) as b:
                for k in range(KC):
                    act.wait_ge(zT_done, KC * b + k + 1)
                    nc.scalar.activation(zT[:, k, :], bank[k][:, :], ACT.Copy).then_inc(zT_ready, 1)
            act.wait_ge(shifted, 1)
            nc.scalar.activation(score[:, :, :], score[:, :, :], ACT.Exp).then_inc(exp_ready, 1)

        @block.vector
        def _(dve):
            steps = Steps(dve, dve_step)

            def norm_pair(i):
                for par in range(2):
                    b = 2 * i + par
                    nm.stats(nc, steps, [tile_of(x, b, t) for t in range(TT)], var_ready)
                    dve.wait_ge(rstd_ready, b + 1)
                    dve.wait_ge(z_out[par], 16 * i)
                    dve.wait_ge(zT_done, 2 * KC * i)
                    for t in range(TT):
                        nm.apply(nc, z[:, par, t * D:(t + 1) * D], tile_of(x, b, t), t).then_inc(z_ready, 1)

            steps.loop(0, B // 2, norm_pair, 2 * Norm.STATS_STEPS)
            logits = bank[2][:, 0:GE].rearrange("p (g e) -> p g e", e=NE)
            wide = [P, G_TILES, NE]
            dve.wait_ge(logits_done, B)
            steps.did(nc.vector.tensor_reduce(top[:, :, 0], logits, AX.X, ALU.max))
            steps.settle()
            nc.vector.tensor_tensor(score[:, :, :], logits, top[:, :, :].to_broadcast(wide), ALU.subtract).then_inc(shifted, 1)
            dve.wait_ge(exp_ready, 1)
            steps.did(nc.vector.tensor_reduce(esum[:, :, 0], score[:, :, :], AX.X, ALU.add))
            steps.settle()
            steps.did(nc.vector.reciprocal(rsum[:, :, :], esum[:, :, :]))
            steps.settle()
            nc.vector.tensor_tensor(score[:, :, :], score[:, :, :], rsum[:, :, :].to_broadcast(wide), ALU.mult)\
                .then_inc(score_ready, 1)
            dve.wait_ge(score_ready, 1)
            steps.did(nc.vector.tensor_copy(by_exp[:, :, :], score[:, :, :].rearrange("p g e -> p e g")))
            dve.wait_ge(c_in, C_IN)
            steps.did(nc.vector.memset(low[:, :, :], 0))
            steps.did(nc.vector.memset(cand[:, :, :], 1 << (BITS - 1)))
            steps.settle()
            tall = [P, NE, G_TILES]
            count = bank[3][:, 0:NE].rearrange("p (e a) -> p e a", a=1)

            def search(i):
                steps.did(nc.vector.tensor_tensor(flag[:, :, :], by_exp[:, :, :], cand[:, :, :].bitcast(F32).to_broadcast(tall),
                                                  ALU.is_ge))
                steps.settle()
                with nc.allow_low_precision(reason="counts up to 32 are exact in bfloat16"):
                    nc.vector.tensor_reduce(part[:, :], flag[:, :, :], AX.X, ALU.add).then_inc(part_ready, 1)
                dve.wait_ge(count_done, i + 1)
                steps.did(nc.vector.scalar_tensor_tensor(
                    out=inc[:, :, :], in0=count, scalar=float(CAP),
                    in1=bit[:, bass.ds(i, 1)].rearrange("p (a o) -> p a o", a=1).to_broadcast([P, NE, 1]),
                    op0=ALU.is_ge, op1=ALU.mult))
                steps.settle()
                steps.did(nc.vector.scalar_tensor_tensor(out=cand[:, :, :], in0=low[:, :, :], scalar=next_bit[:, bass.ds(i, 1)],
                                                         in1=inc[:, :, :], op0=ALU.bitwise_or, op1=ALU.bitwise_or))
                steps.settle()
                steps.did(nc.vector.tensor_tensor(low[:, :, :], low[:, :, :], inc[:, :, :], ALU.bitwise_or))

            steps.loop(0, BITS, search, 4)
            steps.settle()
            edge = low[:, :, :].bitcast(F32).to_broadcast(tall)
            steps.did(nc.vector.tensor_tensor(flag[:, :, :], by_exp[:, :, :], edge, ALU.is_gt))
            nc.vector.tensor_tensor(take[:, :, :], by_exp[:, :, :], edge, ALU.is_equal).then_inc(flags_ready, 1)
            steps.settle()
            with nc.allow_low_precision(reason="counts up to 32 are exact in bfloat16"):
                nc.vector.tensor_reduce(part[:, :], flag[:, :, :], AX.X, ALU.add).then_inc(part_ready, 1)
            dve.wait_ge(count_done, BITS + 1)
            steps.did(nc.vector.tensor_scalar(need[:, :, :], count, -1.0, float(CAP), ALU.mult, ALU.add))

            def ranks(n, out):
                dve.wait_ge(ranks_done, n)
                steps.did(nc.vector.tensor_copy(total[:, :], bank[5][:, 0:GE]))
                steps.settle()
                steps.did(nc.vector.tensor_tensor_scan(upto[:, :], carry_on[:, :], total[:, :], 0.0, ALU.mult, ALU.add))
                steps.settle()
                steps.did(nc.vector.tensor_tensor(upto[:, :], upto[:, :], total[:, :], ALU.subtract))
                steps.settle()
                steps.did(nc.vector.tensor_tensor(out, bank[4][:, 0:GE], upto[:, :], ALU.add))
                steps.settle()

            ranks(1, rank[:, :])
            steps.did(nc.vector.tensor_tensor(chosen[:, :, :], rank[:, :].rearrange("p (e g) -> p e g", e=NE),
                                              need[:, :, :].to_broadcast(tall), ALU.is_lt))
            steps.settle()
            steps.did(nc.vector.tensor_tensor(take[:, :, :], chosen[:, :, :], take[:, :, :], ALU.mult))
            steps.settle()
            nc.vector.tensor_tensor(chosen[:, :, :], flag[:, :, :], take[:, :, :], ALU.add).then_inc(flags_ready, 1)
            ranks(2, slot[:, :])
            steps.did(nc.vector.tensor_scalar(lo_i[:, :], slot[:, :], P - 1, None, ALU.bitwise_and))
            steps.did(nc.vector.tensor_scalar(hi_i[:, :], slot[:, :], P.bit_length() - 1, None, ALU.logical_shift_right))
            steps.settle()
            steps.did(nc.vector.scalar_tensor_tensor(out=lo[:, :], in0=lo_i[:, :], scalar=1.0,
                                                     in1=chosen[:, :, :].rearrange("p e g -> p (e g)"),
                                                     op0=ALU.add, op1=ALU.mult))
            steps.did(nc.vector.tensor_copy(hi[:, :, 0], hi_i[:, :]))
            steps.settle()
            steps.did(nc.vector.tensor_tensor(hot_hi[:, :, :], hi[:, :, :].to_broadcast([P, GE, BLK]),
                                              hi_row[:, :, :].to_broadcast([P, GE, BLK]), ALU.is_equal))
            steps.settle()
            nc.vector.tensor_tensor(number[:, :, 0, :], hot_hi[:, :, :], tile_no[:, :, :].to_broadcast([P, GE, BLK]),
                                    ALU.mult).then_inc(number_ready, 1)
            nc.vector.tensor_scalar(number[:, :, 1, :], hot_hi[:, :, :], lane_no[:, :], None, ALU.mult).then_inc(number_ready, 1)
            with dve.Fori(0, NE // 2) as i:
                for par in range(2):
                    for g in range(G_TILES):
                        if g == 0:
                            dve.wait_ge(hot_used[par], i)
                        hot = nc.vector.tensor_scalar(hot_lo[:, par, g, :], lo_row[:, :],
                                                      lo[:, bass.ds((2 * i + par) * G_TILES + g, 1)], None, ALU.is_equal)
                        if g % 8 == 7:
                            hot.then_inc(hot_ready[par], 1)
            dve.wait_ge(hot_used[0], NE // 2)
            dve.wait_ge(hot_used[1], NE // 2)
            steps.did(nc.vector.tensor_copy(pair[:, :, :, :], bank[6][:, 0:NE * 2 * BLK]
                                            .rearrange("p (e a h) -> p e a h", e=NE, a=2)))
            steps.settle()
            steps.did(nc.vector.scalar_tensor_tensor(out=s.token[:, :, :], in0=pair[:, :, 0, :], scalar=float(P),
                                                     in1=pair[:, :, 1, :], op0=ALU.mult, op1=ALU.add))
            steps.settle()

        @block.tensor
        def _(pe):
            pe.wait_ge(w_in, 16)
            with pe.Fori(0, B // 2) as i:
                for par in range(2):
                    b = 2 * i + par
                    pe.wait_ge(z_ready, TT * b + TT)
                    for k in range(KC):
                        for t in range(TT):
                            last = nc.tensor.transpose(bank[k][:, t * P:(t + 1) * P],
                                                       z[:, par, t * D + k * P:t * D + (k + 1) * P], ident[:, :])
                        last.then_inc(zT_done, 1)
                    pe.wait_ge(zT_ready, KC * b + KC)
                    for t in range(TT):
                        for k in range(KC):
                            last = nc.tensor.matmul(bank[2][:, bass.ds((TT * b + t) * NE, NE)], zT[:, k, t * P:(t + 1) * P],
                                                    wg[:, k, :], start=k == 0, stop=k == KC - 1)
                    last.then_inc(logits_done, 1)
            pe.wait_ge(c_in, C_IN)
            with pe.Fori(0, BITS + 1) as i:
                pe.wait_ge(part_ready, i + 1)
                nc.tensor.matmul(bank[3][:, 0:NE], ones[:, :], part[:, :], start=True, stop=True).then_inc(count_done, 1)
            for n, src in enumerate((take, chosen)):
                pe.wait_ge(flags_ready, n + 1)
                v = src[:, :, :].rearrange("p e g -> p (e g)")
                nc.tensor.matmul(bank[4][:, 0:GE], below[:, :], v, start=True, stop=True)
                nc.tensor.matmul(bank[5][:, 0:GE], ones[:, :], v, start=True, stop=True).then_inc(ranks_done, 1)
            pe.wait_ge(number_ready, 2)
            W = 2 * BLK
            flat = number[:, :, :, :].rearrange("p n a h -> p (n a h)")
            with pe.Fori(0, NE // 2) as i:
                for par in range(2):
                    for g in range(G_TILES):
                        if g % 8 == 0:
                            pe.wait_ge(hot_ready[par], G_TILES // 8 * i + g // 8 + 1)
                        last = nc.tensor.matmul(bank[6][:, bass.ds((2 * i + par) * W, W)], hot_lo[:, par, g, :],
                                                flat[:, bass.ds(((2 * i + par) * G_TILES + g) * W, W)],
                                                start=g == 0, stop=g == G_TILES - 1)
                    last.then_inc(hot_used[par], 1)


def experts(nc, s, w):
    bank, ident = s.bank, s.ident
    HC = HID // P
    HB = BLK // 2
    with ExitStack() as ctx:
        sb = lambda n, shape, d=F32: ctx.enter_context(nc.sbuf_tensor("ex_" + n, shape, d))
        sem = lambda n: ctx.enter_context(nc.semaphore("ex_" + n))
        both = lambda n: [sem(n + "0"), sem(n + "1")]
        w1, w3 = sb("w1", [P, 2, KC, HID]), sb("w3", [P, 2, KC, HID])
        w2 = sb("w2", [P, 2, HC, D])
        mine = [sb(f"mine{par}", [P, BLK], I32) for par in range(2)]
        got = sb("got", [P, 2, BLK, ZW])
        rT = sb("rT", [P, KC, CAP])
        gate = sb("gate", [P, 2, T])
        hT = sb("hT", [P, 2, HC, T])
        o = sb("o", [P, BLK, D])
        nil, tick = sb("nil", [P, 1]), sb("tick", [P, 1])

        w_in = [sem("w_in0"), sem("w_in1")]
        gathered = [sem("gathered0"), sem("gathered1")]
        fill, ticked, mine_ready = sem("fill"), sem("ticked"), sem("mine_ready")
        scaled, rT_done, rT_ready = sem("scaled"), sem("rT_done"), sem("rT_ready")
        h1_done, h3_done, gate_ready, h_ready = sem("h1_done"), sem("h3_done"), sem("gate_ready"), sem("h_ready")
        o_done, o_ready, added = sem("o_done"), sem("o_ready"), sem("added")
        block = ctx.enter_context(nc.Block())
        NH, NT, NO, ADDS = 2 * HC, 2 * KC, BLK // 2, 16 * BLK

        def each(eng, body):
            with eng.Fori(0, NE // 2 - 1) as i:
                body(2 * i, 0, i, False)
                body(2 * i + 1, 1, i, False)
            body(NE - 2, 0, NE // 2 - 1, False)
            body(NE - 1, 1, NE // 2 - 1, True)

        @block.sync
        def _(sp):
            def load(e, par):
                for dst, src in ((w1, w["w1"]), (w3, w["w3"]), (w2, w["w2"])):
                    sp.dma_start(dst[:, par, :, :], src[bass.ds(e, 1), :, :].rearrange("a (k p) n -> p (a k) n", p=P))\
                        .then_inc(w_in[par], 16)
            load(0, 0)
            load(1, 1)
            with sp.Fori(0, NE // 2 - 1) as i:
                for par in range(2):
                    e = 2 * i + par
                    sp.wait_ge(o_done, NO * e + NO)
                    load(e + 2, par)

        @block.gpsimd
        def _(pool):
            TICKS = 3 + NO

            def wait_ahead(sem, value, e, n):
                pool.wait_ge(ticked, TICKS * e + n)
                pool.wait_ge(sem, value)
                pool.tensor_tensor(tick[:, :], nil[:, :], nil[:, :], ALU.add).then_inc(ticked, 1)

            def gather(e, par, i):
                for j in range(BLK):
                    pool.indirect_dma_start(got[:, par, j, :], None, s.z_dram, bass.IndirectOffsetOnAxis(
                        ap=mine[par][:, j:j + 1], axis=0)).then_inc(gathered[par], 16)

            def body(e, par, i, last):
                if not last:
                    wait_ahead(rT_done, NT * e + NT, e, 0)
                    wait_ahead(mine_ready, e + 2, e, 1)
                    gather(e + 1, 1 - par, i)
                n = 0 if last else 2
                wait_ahead(added, ADDS * e, e, n)
                for j in range(BLK):
                    if j % 2 == 0:
                        wait_ahead(o_ready, NO * e + j // 2 + 1, e, n + 1 + j // 2)
                    pool.indirect_dma_start(s.acc_dram, bass.IndirectOffsetOnAxis(ap=mine[par][:, j:j + 1], axis=0),
                                            o[:, j, :], None, compute_op=ALU.add).then_inc(added, 16)

            pool.memset(nil[:, :], 0.0).then_inc(fill, 1)
            pool.wait_ge(fill, 1)
            pool.wait_ge(mine_ready, 1)
            gather(0, 0, 0)
            each(pool, body)
            pool.wait_ge(added, ADDS * NE)

        @block.scalar
        def _(act):
            def move_rT(e):
                for n in range(NT):
                    half, k = n // KC, n % KC
                    act.wait_ge(rT_done, NT * e + n + 1)
                    nc.scalar.activation(rT[:, k, half * T:(half + 1) * T], bank[n][:, :], ACT.Copy).then_inc(rT_ready, 1)

            def move_o(e, half):
                if half == 0:
                    act.wait_ge(added, ADDS * e)
                for n in range(2 * half, 2 * half + 2):
                    act.wait_ge(o_done, NO * e + n + 1)
                    nc.scalar.activation(o[:, 2 * n:2 * n + 2, :], bank[6 + n % 2][:, :].rearrange("p (a c) -> p a c", a=2),
                                         ACT.Copy).then_inc(o_ready, 1)

            def body(e, par, i, last):
                for q in range(NH):
                    act.wait_ge(h1_done, NH * e + q + 1)
                    act.wait_ge(h_ready, NH * e + max(q - 1, 0))
                    nc.scalar.activation(gate[:, q % 2, :], bank[2 + q % 2][:, :], ACT.Silu).then_inc(gate_ready, 1)
                move_o(e, 0)
                if not last:
                    move_rT(e + 1)
                move_o(e, 1)

            nc.scalar.preload_act_table(ACT.Silu)
            move_rT(0)
            each(act, body)

        @block.vector
        def _(dve):
            def name(e, par):
                nc.vector.tensor_scalar(mine[par][:, :], s.token[:, bass.ds(e, 1), :].rearrange("p a h -> p (a h)"),
                                        0.0, None, ALU.add).then_inc(mine_ready, 1)

            def scale(e, par, i):
                dve.wait_ge(gathered[par], ADDS * (i + 1))
                for j in range(BLK):
                    row = got[:, par, :, :].rearrange("p b c -> p (b c)")
                    nc.vector.tensor_scalar(got[:, par, j, 0:D], got[:, par, j, 0:D], row[:, bass.ds(j * ZW + D + e, 1)],
                                            None, ALU.mult).then_inc(scaled, 1)

            def body(e, par, i, last):
                for q in range(NH):
                    if q == HC and not last:
                        dve.wait_ge(added, ADDS * e)
                        name(e + 1, 1 - par)
                    dve.wait_ge(h3_done, NH * e + q + 1)
                    dve.wait_ge(gate_ready, NH * e + q + 1)
                    nc.vector.tensor_tensor(hT[:, q // HC, q % HC, :], bank[4 + q % 2][:, :], gate[:, q % 2, :], ALU.mult)\
                        .then_inc(h_ready, 1)
                if not last:
                    scale(e + 1, 1 - par, i + par)

            name(0, 0)
            scale(0, 0, 0)
            each(dve, body)

        @block.tensor
        def _(pe):
            def trans(e, par):
                pe.wait_ge(scaled, BLK * e + BLK)
                for n in range(NT):
                    half, k = n // KC, n % KC
                    for j in range(BLK // 2):
                        last = nc.tensor.transpose(bank[n][:, j * P:(j + 1) * P],
                                                   got[:, par, half * BLK // 2 + j, k * P:(k + 1) * P], ident[:, :])
                    last.then_inc(rT_done, 1)

            def out(e, par, half):
                for j in range(BLK // 2):
                    if j % 2 == 0:
                        pe.wait_ge(o_ready, NO * e + (j // 2 + 1 if half else 0))
                    for c in range(HC):
                        last = nc.tensor.matmul(bank[6 + j // 2][:, (j % 2) * D:(j % 2 + 1) * D],
                                                hT[:, half, c, j * P:(j + 1) * P], w2[:, par, c, :],
                                                start=c == 0, stop=c == HC - 1)
                    if j % 2:
                        last.then_inc(o_done, 1)

            def body(e, par, i, last):
                pe.wait_ge(w_in[par], 48 * (i + 1))
                pe.wait_ge(rT_ready, NT * e + NT)
                for q in range(NH):
                    half, c = q // HC, q % HC
                    for ws, b0, done, free in ((w1, 2, h1_done, gate_ready), (w3, 4, h3_done, h_ready)):
                        pe.wait_ge(free, NH * e + max(q - 1, 0))
                        for k in range(KC):
                            mm = nc.tensor.matmul(bank[b0 + q % 2][:, :], ws[:, par, k, c * P:(c + 1) * P],
                                                    rT[:, k, half * T:(half + 1) * T], start=k == 0, stop=k == KC - 1)
                        mm.then_inc(done, 1)
                pe.wait_ge(h_ready, NH * e + HC)
                out(e, par, 0)
                if not last:
                    pe.wait_ge(gate_ready, NH * e + NH)
                    trans(e + 1, 1 - par)
                pe.wait_ge(h_ready, NH * e + NH)
                out(e, par, 1)

            trans(0, 0)
            each(pe, body)


def close(nc, s, w, out):
    x, nm = s.x, s.norm
    with ExitStack() as ctx:
        sb = lambda n, shape, d=F32: ctx.enter_context(nc.sbuf_tensor("cl_" + n, shape, d))
        sem = lambda n: ctx.enter_context(nc.semaphore("cl_" + n))
        y = sb("y", [P, 2, TT, D])
        zn = sb("zn", [P, 2, TT, D])
        y_in, x_out = [sem("y_in0"), sem("y_in1")], [sem("x_out0"), sem("x_out1")]
        dve_step, var_ready, rstd_ready, y_read, x_ready = (sem(n) for n in ("dve_step", "var_ready", "rstd_ready", "y_read", "x_ready"))
        block = ctx.enter_context(nc.Block())
        acc_rows = s.acc_dram.rearrange("(g p) c -> p g c", p=P)
        out_rows = out.rearrange("b (t p) c -> p (b t) c", p=P)

        @block.sync
        def _(sp):
            with sp.Fori(0, B // 2) as i:
                for par in range(2):
                    sp.wait_ge(y_read, TT * 2 * i)
                    sp.dma_start(y[:, par, :, :], acc_rows[:, bass.ds(TT * (2 * i + par), TT), :]).then_inc(y_in[par], 16)

        @block.scalar
        def _(act):
            with act.Fori(0, B // 2) as i:
                for par in range(2):
                    act.wait_ge(x_ready, 2 * i + par + 1)
                    act.dma_start(out_rows[:, bass.ds(TT * (2 * i + par), TT), :], zn[:, par, :, :]).then_inc(x_out[par], 16)
            act.wait_ge(x_out[0], 16 * B // 2)
            act.wait_ge(x_out[1], 16 * B // 2)

        @block.gpsimd
        def _(pool):
            with pool.Fori(0, B) as b:
                pool.wait_ge(var_ready, b + 1)
                nm.root(pool, rstd_ready)

        @block.vector
        def _(dve):
            steps = Steps(dve, dve_step)

            def body(i):
                for par in range(2):
                    b = 2 * i + par
                    dve.wait_ge(y_in[par], 16 * i + 16)
                    nm.stats(nc, steps, [y[:, par, t, :] for t in range(TT)], var_ready)
                    dve.wait_ge(x_out[par], 16 * i)
                    dve.wait_ge(rstd_ready, b + 1)
                    for t in range(TT):
                        nm.apply(nc, zn[:, par, t, :], y[:, par, t, :], t).then_inc(y_read, 1)
                    dve.wait_ge(y_read, TT * b + TT)
                    flat = zn[:, par, :, :].rearrange("p t c -> p (t c)")
                    nc.vector.tensor_tensor(flat, flat, batch_of(x, b), ALU.add).then_inc(x_ready, 1)

            steps.loop(0, B // 2, body, 2 * Norm.STATS_STEPS)


class Shared:
    pass


def build(nc, ins, out):
    w = dict(ins)
    pos = np.arange(T, dtype=np.float32)
    freq = (np.float32(10000.0) ** (-np.arange(QK // 2, dtype=np.float32) / np.float32(QK // 2))).astype(np.float32)
    angle = (pos[:, None] * freq[None, :]).astype(np.float32)
    turn = np.zeros((P, P), np.float32)
    for i in range(P):
        if i % QK < QK // 2:
            turn[i + QK // 2, i] = -1.0
        else:
            turn[i - QK // 2, i] = 1.0
    for name, a in (("ident", np.eye(P)), ("turn", turn), ("cos", np.tile(np.cos(angle).T, (4, 1))),
                    ("sin", np.tile(np.sin(angle).T, (4, 1))), ("causal", np.triu(np.ones((P, P)))),
                    ("hi_row", np.tile(np.arange(BLK), (P, 1))),
                    ("tile_no", np.tile(np.arange(G_TILES), (P, NE))), ("lane_no", np.arange(P)[:, None]),
                    ("carry_on", np.tile(np.arange(G_TILES) > 0, (P, NE))),
                    ("bit", np.tile(2.0 ** np.arange(BITS - 1, -1, -1), (P, 1)))):
        w[name] = nc.inline_tensor(np.ascontiguousarray(a, dtype=np.float32), "const_" + name).ap()
    half = mybir.dt.np(BF16)
    for name, a, dt in (("ones", np.ones((P, P)), half), ("below", np.triu(np.ones((P, P)), 1), half),
                        ("lo_row", np.tile(np.arange(1, P + 1), (P, 1)), half),
                        ("next_bit", np.tile((1 << np.arange(BITS - 1, -1, -1)) >> 1, (P, 1)), np.int32)):
        w[name] = nc.inline_tensor(np.ascontiguousarray(a.astype(dt)), "const_" + name).ap()
    with ExitStack() as ctx:
        s = Shared()
        sb = lambda n, shape, d=F32: ctx.enter_context(nc.sbuf_tensor(n, shape, d))
        s.x = sb("x", [P, B * TT * D])
        s.ident = sb("ident", [P, P])
        s.token = sb("token", [P, NE, BLK])
        s.z_dram = nc.dram_tensor("z_dram", (NTOK, ZW), F32, kind="Internal").ap()
        s.acc_dram = nc.dram_tensor("acc_dram", (NTOK, D), F32, kind="Internal").ap()
        s.norm = Norm(sb)
        s.bank = [ctx.enter_context(nc.psum_tensor(f"bank{i}", [P, 512], F32)) for i in range(8)]
        gau_layer(nc, s, w)
        mix_layer(nc, s, w)
        hedgehog_layer(nc, s, w)
        route(nc, s, w)
        experts(nc, s, w)
        close(nc, s, w, out)


def laid_out(i):
    flip = lambda a: a.T
    cols = lambda a: a.reshape(-1, P).T
    g = lambda n: i[n]
    return {
        "x": g("L0_attn_x").reshape(B, TT, P, D).transpose(0, 2, 1, 3).reshape(B, P, TT * D),
        "Wqk2T": np.concatenate([g("L0_attn_Wqk"), g("L0_attn_Wqk")]).T,
        "WvT": flip(g("L0_attn_Wv")), "WgT": flip(g("L0_attn_Wg")), "WoT": flip(g("L0_attn_Wo")),
        "ln1_wT": cols(g("L0_attn_ln1_w")), "ln1_bT": cols(g("L0_attn_ln1_b")),
        "bqk2": np.concatenate([g("L0_attn_bqk"), g("L0_attn_bqk")]).reshape(P, 1),
        "gammaT": cols(g("L0_attn_gamma")), "betaT": cols(g("L0_attn_beta")), "bgT": cols(g("L0_attn_bg")),
        "bv": g("L0_attn_bv"), "bo": g("L0_attn_bo"), "ln2_w": g("L0_attn_ln2_w"), "ln2_b": g("L0_attn_ln2_b"),
        "pos_emb": g("L0_attn_pos_emb"),
        "ffn_WrT": flip(g("L0_ffn_W_r")), "ffn_WkT": flip(g("L0_ffn_W_k")), "ffn_WvT": flip(g("L0_ffn_W_v")),
        "mu_rT": cols(g("L0_ffn_mu_r")), "mu_kT": cols(g("L0_ffn_mu_k")),
        "w_qk": g("L1_attn_w_qkv")[:2 * D], "w_vT": flip(g("L1_attn_w_qkv")[2 * D:]),
        "wq_mapT": flip(g("L1_attn_wq_map")), "wk_mapT": flip(g("L1_attn_wk_map")),
        "bq_map": g("L1_attn_bq_map"), "bk_map": g("L1_attn_bk_map"), "w_outT": flip(g("L1_attn_w_out")),
        "wg": g("L1_ffn_wg"), "w1": g("L1_ffn_w1"), "w3": g("L1_ffn_w3"), "w2": g("L1_ffn_w2"),
    }


def kernel(**inputs):
    import concourse.bacc as bacc
    from concourse.bass_utils import run_bass_kernel_spmd

    nc = bacc.Bacc("TRN2", target_bir_lowering=False, num_devices=1)
    arrays, ins = {}, {}
    for name, a in laid_out({n: np.asarray(a) for n, a in inputs.items()}).items():
        arrays["in_" + name] = np.ascontiguousarray(a)
        ins[name] = nc.dram_tensor("in_" + name, a.shape, mybir.dt.from_np(a.dtype), kind="ExternalInput").ap()
    out = nc.dram_tensor("out_0", (B, T, D), F32, kind="ExternalOutput").ap()
    build(nc, ins, out)
    r = run_bass_kernel_spmd(nc, [arrays], core_ids=[0])
    return r.results[0]["out_0"]
```

```python
import numpy as np
from contextlib import ExitStack

import concourse.bass as bass
from concourse import mybir

F32 = mybir.dt.float32
F32R = mybir.dt.float32r
BF16 = mybir.dt.bfloat16
I32 = mybir.dt.int32
ALU = mybir.AluOpType
ACT = mybir.ActivationFunctionType
AX = mybir.AxisListType

B, T, D = 8, 512, 256
P = 128
TT = T // P
KC = D // P
NTOK = B * T
EPS = 1e-5
QK, H = 64, 512
EC = H // P
GROUP, MAX_REL = 64, 32
HEADS, HD = 16, 16
HPC = 4
FC = HEADS // HPC
VW = HD + 1
NE, CAP, HID = 8, 1024, 512


class Steps:

    def __init__(self, eng, sem):
        self.eng, self.sem, self.count, self.reg = eng, sem, 0, None

    def did(self, ins):
        ins.then_inc(self.sem, 1)
        self.count += 1

    def settle(self):
        if self.reg is None:
            self.eng.wait_ge(self.sem, self.count)
        else:
            self.eng.wait_ge(self.sem, self.reg * self.per + (self.count - self.lo * self.per))

    def loop(self, lo, hi, body, per):
        first = self.count
        with self.eng.Fori(lo, hi) as i:
            self.reg, self.per, self.lo = i, per, lo
            body(i)
        assert self.count - first == per, (self.count - first, per)
        self.reg, self.count = None, first + per * (hi - lo)


def tile_of(x, b, t):
    return x[:, bass.ds(b * (TT * D) + t * D, D)]


def batch_of(x, b):
    return x[:, bass.ds(b * (TT * D), TT * D)]


class Norm:

    def __init__(self, sb, tag=""):
        sb = lambda n, shape, sb=sb: sb(n + tag, shape)
        self.st = sb("ln_stats", [P, TT, 6])
        self.sum = sb("ln_sum", [P, TT])
        self.dif = sb("ln_dif", [P, TT])
        self.cv = sb("ln_cv", [P, TT])
        self.sq = sb("ln_sq", [P, TT])
        self.v = sb("ln_v", [P, TT])
        self.mean = sb("ln_mean", [P, TT])
        self.var = sb("ln_var", [P, TT])
        self.rstd = sb("ln_rstd", [P, TT])
        self.mhalf = sb("ln_mhalf", [P, TT])
        self.shift = sb("ln_shift", [P, TT])

    def stats(self, nc, steps, tiles, var_ready, twice=False, minus=False):
        for t in range(len(tiles)):
            steps.did(nc.vector.bn_stats(self.st[:, t, :], tiles[t]))
        steps.settle()
        steps.did(nc.vector.tensor_tensor(self.dif[:, :], self.st[:, :, 1], self.st[:, :, 4], ALU.subtract))
        steps.did(nc.vector.tensor_tensor(self.sum[:, :], self.st[:, :, 1], self.st[:, :, 4], ALU.add))
        steps.did(nc.vector.tensor_tensor(self.cv[:, :], self.st[:, :, 2], self.st[:, :, 5], ALU.add))
        steps.settle()
        steps.did(nc.vector.tensor_tensor(self.sq[:, :], self.dif[:, :], self.dif[:, :], ALU.mult))
        steps.did(nc.vector.tensor_scalar(self.mean[:, :], self.sum[:, :], -0.5 if minus else 0.5, None, ALU.mult))
        steps.settle()
        steps.did(nc.vector.scalar_tensor_tensor(out=self.v[:, :], in0=self.sq[:, :], scalar=D / 4.0,
                                                 in1=self.cv[:, :], op0=ALU.mult, op1=ALU.add))
        steps.settle()
        a, e = (1 + EPS, EPS * EPS) if twice else (1.0, EPS)
        nc.vector.tensor_scalar(self.var[:, :], self.v[:, :], a / D, e, ALU.mult, ALU.add).then_inc(var_ready, 1)

    STATS_STEPS = TT + 6

    def root(self, pool, rstd_ready):
        pool.tensor_tensor(self.rstd[:, :], self.var[:, :], self.mhalf[:, :], ALU.pow).then_inc(rstd_ready, 1)

    def root_shift(self, pool, rstd_ready, at, shift_ready):
        self.root(pool, rstd_ready)
        pool.wait_ge(rstd_ready, at)
        pool.tensor_tensor(self.shift[:, :], self.mean[:, :], self.rstd[:, :], ALU.mult).then_inc(shift_ready, 1)

    def scaled(self, nc, out, in_, t):
        return nc.scalar.activation(out, in_, ACT.Identity, bias=self.shift[:, t:t + 1], scale=self.rstd[:, t:t + 1])

    def apply(self, nc, out, in_, t):
        return nc.vector.tensor_scalar(out, in_, self.mean[:, t:t + 1], self.rstd[:, t:t + 1],
                                       ALU.subtract, ALU.mult)


def gau_layer(nc, s, w):
    x, nm, bank, ident = s.x, s.norm, s.bank, s.ident
    with ExitStack() as ctx:
        sb = lambda n, shape, d=F32: ctx.enter_context(nc.sbuf_tensor("gau_" + n, shape, d))
        sem = lambda n: ctx.enter_context(nc.semaphore("gau_" + n))
        wqk = sb("wqk", [P, KC, 2 * QK])
        wv = sb("wv", [P, KC, H])
        wg = sb("wg", [P, KC, H])
        wo = sb("wo", [P, EC, D])
        cos, sin = sb("cos", [P, T]), sb("sin", [P, T])
        turn = sb("turn", [P, P])
        ln1 = sb("ln1", [P, 2, KC])
        bqk = sb("bqk", [P, 1])
        gamma, beta = sb("gamma", [P, 2]), sb("beta", [P, 2])
        bg = sb("bg", [P, EC])
        bv_row = sb("bv_row", [P, H])
        bo_row = sb("bo_row", [P, D])
        ln2 = sb("ln2", [P, 2, D])
        pos_row = sb("pos_row", [1, 2 * MAX_REL + 1])
        rel_row = sb("rel_row", [1, 2 * GROUP])
        rel_flip = sb("rel_flip", [P, GROUP])
        rel = sb("rel", [P, 1, GROUP])
        z = sb("z", [P, TT * D])
        xnT = sb("xnT", [P, KC, T])
        sT = sb("sT", [P, T])
        lin = sb("lin", [P, 2, T])
        lcos = sb("lcos", [P, 2, T])
        lsin = sb("lsin", [P, 2, T])
        rope = sb("rope", [P, 2, T])
        v = sb("v", [P, TT, H])
        k_tok = sb("k_tok", [P, TT, P])
        sim = sb("sim", [P, TT, GROUP])
        att = sb("att", [P, TT, P])
        kv = sb("kv", [P, H])
        gT = sb("gT", [P, EC, T])
        oT = sb("oT", [P, EC, T])
        y = sb("y", [P, TT, D])
        zn = sb("zn", [P, TT, D])
        wz = sb("wz", [P, TT, D])
        rel_dram = nc.dram_tensor("rel_dram", (2 * GROUP,), F32, kind="Internal").ap()

        w_early, w_late, w_rows = sem("w_early"), sem("w_late"), sem("w_rows")
        pos_in, rel_out, rel_in = sem("pos_in"), sem("rel_out"), sem("rel_in")
        x_first, x_rest = sem("x_first"), sem("x_rest")
        fill = sem("fill")
        dve_step, pool_step = sem("dve_step"), sem("pool_step")
        var_ready, rstd_ready = sem("var_ready"), sem("rstd_ready")
        z_ready, zT_done, xn_ready = sem("z_ready"), sem("zT_done"), sem("xn_ready")
        qk_done, s_ready, lin_ready = sem("qk_done"), sem("s_ready"), sem("lin_ready")
        v_done, v_biased, v_ready = sem("v_done"), sem("v_biased"), sem("v_ready")
        turn_done, lcos_ready, rope_ready = sem("turn_done"), sem("lcos_ready"), sem("rope_ready")
        sim_done, att_ready = sem("sim_done"), sem("att_ready")
        kT_done, k_ready, kv_done, kv_ready = sem("kT_done"), sem("k_ready"), sem("kv_done"), sem("kv_ready")
        g_done, g_ready, o_done, o_ready, y_done = (sem(n) for n in ("g_done", "g_ready", "o_done", "o_ready", "y_done"))
        y_moved, zn_ready, wz_ready = sem("y_moved"), sem("zn_ready"), sem("wz_ready")

        block = ctx.enter_context(nc.Block())

        @block.sync
        def _(sp):
            sp.dma_start(batch_of(x, 0), w["x"][0]).then_inc(x_first, 16)
            sp.dma_start(ident[:, :], w["ident"]).then_inc(w_early, 16)
            sp.dma_start(ln1[:, 0, :], w["ln1_wT"]).then_inc(w_early, 16)
            sp.dma_start(ln1[:, 1, :], w["ln1_bT"]).then_inc(w_early, 16)
            sp.dma_start(wqk[:, :, :], w["Wqk2T"].rearrange("(k p) n -> p k n", p=P)).then_inc(w_early, 16)
            sp.dma_start(bqk[:, :], w["bqk2"]).then_inc(w_early, 16)
            sp.dma_start(gamma[:, :], w["gammaT"]).then_inc(w_early, 16)
            sp.dma_start(beta[:, :], w["betaT"]).then_inc(w_early, 16)
            sp.dma_start(wv[:, :, :], w["WvT"].rearrange("(k p) n -> p k n", p=P)).then_inc(w_late, 16)
            sp.dma_start(wg[:, :, :], w["WgT"].rearrange("(k p) n -> p k n", p=P)).then_inc(w_late, 16)
            sp.dma_start(turn[:, :], w["turn"]).then_inc(w_late, 16)
            sp.dma_start(bg[:, :], w["bgT"]).then_inc(w_late, 16)
            sp.dma_start(wo[:, :, :], w["WoT"].rearrange("(k p) n -> p k n", p=P)).then_inc(w_late, 16)
            for b in range(1, B):
                sp.dma_start(batch_of(x, b), w["x"][b]).then_inc(x_rest, 16)
            sp.wait_ge(dve_step, Norm.STATS_STEPS + 3)
            sp.dma_start(rel_dram, rel_row[0, :]).then_inc(rel_out, 16)
            sp.wait_ge(rel_out, 16)
            for g in range(2):
                sp.dma_start(rel_flip[g * GROUP:(g + 1) * GROUP, :],
                             bass.AP(tensor=rel_dram.tensor, offset=0, ap=[[1, GROUP], [1, GROUP]])).then_inc(rel_in, 16)

        W_EARLY, W_LATE, W_ROWS = 16 * 7, 16 * 5, 16 * 6

        @block.gpsimd
        def _(pool):
            pool.memset(nm.mhalf[:, :], -0.5).then_inc(fill, 1)
            pool.memset(s.norm2.mhalf[:, :], -0.5).then_inc(fill, 1)
            pool.memset(att[:, :, :], 0.0).then_inc(fill, 1)
            pool.wait_ge(w_rows, W_ROWS)
            pool.wait_ge(fill, 3)
            pool.wait_ge(var_ready, 1)
            nm.root(pool, rstd_ready)

            def rest(b, at):
                pool.wait_ge(var_ready, at)
                nm.root(pool, rstd_ready)
                pool.wait_ge(zn_ready, TT * b + TT)
                pool.tensor_tensor(wz[:, :, :], zn[:, :, :], ln2[:, 0:1, :].to_broadcast([P, TT, D]), ALU.mult)\
                    .then_inc(wz_ready, 1)
                pool.wait_ge(var_ready, at + 1)
                nm.root(pool, rstd_ready)

            def body(b, first=False, last=False):
                for j in (1, 0):
                    pool.wait_ge(lin_ready, 2 * b + 2 - j)
                    pool.tensor_tensor(lcos[:, j, :], lin[:, j, :], cos[:, :], ALU.mult).then_inc(lcos_ready, 1)
                if not first:
                    rest(b - 1, 3 * b)
                if not last:
                    pool.wait_ge(var_ready, 3 * b + 2)
                    nm.root(pool, rstd_ready)

            body(0, first=True)
            with pool.Fori(1, B - 1) as b:
                body(b)
            body(B - 1, last=True)
            rest(B - 1, 3 * B - 1)

        @block.scalar
        def _(act):
            act.dma_start(pos_row[:, :], w["pos_emb"].rearrange("(a n) -> a n", a=1)).then_inc(pos_in, 16)
            act.dma_start(cos[:, :], w["cos"]).then_inc(w_rows, 16)
            act.dma_start(sin[:, :], w["sin"]).then_inc(w_rows, 16)
            act.dma_start(bv_row[:, :], w["bv"].partition_broadcast(P)).then_inc(w_rows, 16)
            act.dma_start(bo_row[:, :], w["bo"].partition_broadcast(P)).then_inc(w_rows, 16)
            act.dma_start(ln2[:, 0, :], w["ln2_w"].partition_broadcast(P)).then_inc(w_rows, 16)
            act.dma_start(ln2[:, 1, :], w["ln2_b"].partition_broadcast(P)).then_inc(w_rows, 16)
            act.wait_ge(w_early, W_EARLY)
            act.wait_ge(w_late, W_LATE)

            def move_xn(b):
                for k in range(KC):
                    act.wait_ge(zT_done, KC * b + k + 1)
                    nc.scalar.activation(xnT[:, k, :], bank[k][:, :], ACT.Identity, bias=ln1[:, 1, k:k + 1],
                                         scale=ln1[:, 0, k:k + 1]).then_inc(xn_ready, 1)

            def body(b, last=False):
                act.wait_ge(qk_done, b + 1)
                nc.scalar.activation(sT[:, :], bank[2][:, :], ACT.Silu, bias=bqk[:, :]).then_inc(s_ready, 1)
                for t in range(TT):
                    act.wait_ge(v_biased, TT * b + t + 1)
                    nc.scalar.activation(v[:, t, :], v[:, t, :], ACT.Silu).then_inc(v_ready, 1)
                for e in range(EC):
                    if e == 3:
                        act.wait_ge(kv_done, b + 1)
                        nc.scalar.activation(kv[QK:P, :], bank[7][QK:P, :], ACT.Copy, scale=1.0 / T).then_inc(kv_ready, 1)
                    if e == 2:
                        act.wait_ge(kT_done, b + 1)
                        nc.scalar.activation(k_tok[:, :, :], bank[7][:, :].rearrange("p (t n) -> p t n", t=TT),
                                             ACT.Copy).then_inc(k_ready, 1)
                    act.wait_ge(g_done, EC * b + e + 1)
                    nc.scalar.activation(gT[:, e, :], bank[5 + e % 2][:, :], ACT.Silu, bias=bg[:, e:e + 1])\
                        .then_inc(g_ready, 1)
                if not last:
                    move_xn(b + 1)

            nc.scalar.preload_act_table(ACT.Silu)
            move_xn(0)
            with act.Fori(0, B - 1) as b:
                body(b)
            body(B - 1, last=True)

        @block.vector
        def _(dve):
            steps = Steps(dve, dve_step)
            def front_stats(b):
                nm.stats(nc, steps, [tile_of(x, b, t) for t in range(TT)], var_ready, twice=True)

            def front_norm(b, at):
                dve.wait_ge(rstd_ready, at)
                for t in range(TT):
                    nm.apply(nc, z[:, t * D:(t + 1) * D], tile_of(x, b, t), t).then_inc(z_ready, 1)

            def rest_stats(b):
                dve.wait_ge(y_moved, TT // 2 * (b + 1))
                nm.stats(nc, steps, [y[:, t, :] for t in range(TT)], var_ready)

            def rest_norm(at):
                dve.wait_ge(rstd_ready, at)
                for t in range(TT):
                    nm.apply(nc, zn[:, t, :], y[:, t, :], t).then_inc(zn_ready, 1)

            def rest_affine(b):
                dve.wait_ge(wz_ready, b + 1)
                steps.did(nc.vector.tensor_tensor(y[:, :, :], wz[:, :, :], ln2[:, 1:2, :].to_broadcast([P, TT, D]), ALU.add))
                steps.settle()
                nm.stats(nc, steps, [y[:, t, :] for t in range(TT)], var_ready)

            def rest_add(b, at):
                dve.wait_ge(rstd_ready, at)
                for t in range(TT):
                    steps.did(nm.apply(nc, zn[:, t, :], y[:, t, :], t))
                steps.settle()
                steps.did(nc.vector.tensor_tensor(batch_of(x, b), batch_of(x, b),
                                                  zn[:, :, :].rearrange("p t c -> p (t c)"), ALU.add))

            REST = 2 * Norm.STATS_STEPS + TT + 2

            def body(b, first=False, last=False):
                dve.wait_ge(s_ready, b + 1)
                for j in (1, 0):
                    nc.vector.tensor_scalar(lin[:, j, :], sT[:, :], gamma[:, j:j + 1], beta[:, j:j + 1],
                                            ALU.mult, ALU.add).then_inc(lin_ready, 1)
                for t in range(TT):
                    dve.wait_ge(v_done, TT * b + t + 1)
                    nc.vector.tensor_tensor(v[:, t, :], bank[5 + t % 2][:, :], bv_row[:, :], ALU.add)\
                        .then_inc(v_biased, 1)
                    if not first:
                        (lambda: rest_stats(b - 1), lambda: rest_norm(3 * b), lambda: None,
                         lambda: rest_affine(b - 1))[t]()
                for i, j in enumerate((1, 0)):
                    dve.wait_ge(turn_done, 2 * b + i + 1)
                    steps.did(nc.vector.tensor_tensor(lsin[:, j, :], bank[3 + j][:, :], sin[:, :], ALU.mult))
                steps.settle()
                for i, j in enumerate((1, 0)):
                    dve.wait_ge(lcos_ready, 2 * b + i + 1)
                    nc.vector.tensor_tensor(rope[:, j, :], lcos[:, j, :], lsin[:, j, :], ALU.add).then_inc(rope_ready, 1)
                if first:
                    dve.wait_ge(rel_in, 32)
                    steps.did(nc.vector.tensor_copy(rel[:, 0, :], rel_flip[:, ::-1]))
                    steps.settle()
                dve.wait_ge(sim_done, b + 1)
                for g in range(2):
                    rows = slice(g * GROUP, (g + 1) * GROUP)
                    steps.did(nc.vector.scalar_tensor_tensor(
                        out=sim[rows, :, :], in0=bank[2][rows, :].rearrange("p (t i) -> p t i", t=TT)[:, :, rows],
                        scalar=1.0 / GROUP, in1=rel[rows, :, :].to_broadcast([GROUP, TT, GROUP]), op0=ALU.mult, op1=ALU.add))
                steps.settle()
                for g in range(2):
                    rows = slice(g * GROUP, (g + 1) * GROUP)
                    nc.vector.scalar_tensor_tensor(out=att[rows, :, rows], in0=sim[rows, :, :], scalar=0.0,
                                                   in1=sim[rows, :, :], op0=ALU.max, op1=ALU.mult).then_inc(att_ready, 1)
                if not first:
                    rest_add(b - 1, 3 * b + 1)
                if not last:
                    front_stats(b + 1)
                for e in range(EC):
                    if e == 1 and not last:
                        front_norm(b + 1, 3 * b + 2)
                    dve.wait_ge(o_done, EC * b + e + 1)
                    dve.wait_ge(g_ready, EC * b + e + 1)
                    nc.vector.tensor_tensor(oT[:, e, :], bank[3 + e % 2][:, :], gT[:, e, :], ALU.mult).then_inc(o_ready, 1)
                for i in range(TT // 2):
                    dve.wait_ge(y_done, TT // 2 * b + i + 1)
                    nc.vector.tensor_tensor(y[:, 2 * i:2 * i + 2, :], bank[5 + i][:, :].rearrange("p (t c) -> p t c", t=2),
                                            bo_row[:, :].rearrange("p (a c) -> p a c", a=1).to_broadcast([P, 2, D]),
                                            ALU.add).then_inc(y_moved, 1)

            BODY = 4 + Norm.STATS_STEPS + REST
            dve.wait_ge(x_first, 16)
            front_stats(0)
            front_norm(0, 1)
            dve.wait_ge(pos_in, 16)
            steps.did(nc.vector.tensor_copy(rel_row[:, :], pos_row[:, MAX_REL:MAX_REL + 1].to_broadcast([1, 2 * GROUP])))
            steps.settle()
            mid = GROUP - 1
            steps.did(nc.vector.tensor_copy(rel_row[:, mid:mid + MAX_REL], pos_row[:, 0:MAX_REL]))
            steps.did(nc.vector.tensor_copy(rel_row[:, mid - MAX_REL + 1:mid], pos_row[:, 1:MAX_REL][:, ::-1]))
            dve.wait_ge(w_early, W_EARLY)
            dve.wait_ge(w_rows, W_ROWS)
            dve.wait_ge(fill, 3)
            dve.wait_ge(x_rest, 16 * (B - 1))
            body(0, first=True)
            steps.loop(1, B - 1, body, BODY)
            body(B - 1, last=True)
            rest_stats(B - 1)
            rest_norm(3 * B - 1)
            rest_affine(B - 1)
            rest_add(B - 1, 3 * B)

        @block.tensor
        def _(pe):
            pe.wait_ge(w_early, W_EARLY)

            def gate(b, e):
                pe.wait_ge(v_biased, TT * b + 3 + e) if e < 2 else pe.wait_ge(g_ready, EC * b + e - 1)
                for k in range(KC):
                    last = nc.tensor.matmul(bank[5 + e % 2][:, :], wg[:, k, e * P:(e + 1) * P], xnT[:, k, :],
                                            start=k == 0, stop=k == KC - 1)
                last.then_inc(g_done, 1)

            def trans_z(b):
                pe.wait_ge(z_ready, TT * b + TT)
                for k in range(KC):
                    for t in range(TT):
                        last = nc.tensor.transpose(bank[k][:, t * P:(t + 1) * P],
                                                   z[:, t * D + k * P:t * D + (k + 1) * P], ident[:, :])
                    last.then_inc(zT_done, 1)

            def body(b, final=False):
                pe.wait_ge(xn_ready, KC * b + KC)
                for k in range(KC):
                    last = nc.tensor.matmul(bank[2][:, :], wqk[:, k, :], xnT[:, k, :], start=k == 0, stop=k == KC - 1)
                last.then_inc(qk_done, 1)
                for t in range(TT):
                    if t < 2:
                        pe.wait_ge(y_moved, TT // 2 * b)
                    else:
                        pe.wait_ge(v_biased, TT * b + t - 1)
                    for k in range(KC):
                        last = nc.tensor.matmul(bank[5 + t % 2][:, :], xnT[:, k, t * P:(t + 1) * P], wv[:, k, :],
                                                start=k == 0, stop=k == KC - 1)
                    last.then_inc(v_done, 1)
                for i, j in enumerate((1, 0)):
                    pe.wait_ge(lin_ready, 2 * b + i + 1)
                    pe.wait_ge(o_ready, EC * b)
                    nc.tensor.matmul(bank[3 + j][:, :], turn[:, :], lin[:, j, :], start=True, stop=True).then_inc(turn_done, 1)
                gate(b, 0)
                gate(b, 1)
                pe.wait_ge(rope_ready, 2 * b + 2)
                for t in range(TT):
                    ts = slice(t * P, (t + 1) * P)
                    last = nc.tensor.matmul(bank[2][:, ts], rope[0:QK, 1, ts], rope[0:QK, 0, ts], start=True, stop=True)
                last.then_inc(sim_done, 1)
                pe.wait_ge(kv_ready, b)
                for t in range(TT):
                    ts = slice(t * P, (t + 1) * P)
                    last = nc.tensor.transpose(bank[7][:, ts], rope[:, 1, ts], ident[:, :])
                last.then_inc(kT_done, 1)
                gate(b, 2)
                pe.wait_ge(k_ready, b + 1)
                pe.wait_ge(v_ready, TT * b + TT)
                for t in range(TT):
                    last = nc.tensor.matmul(bank[7][:, :], k_tok[:, t, :], v[:, t, :], start=t == 0, stop=t == TT - 1)
                last.then_inc(kv_done, 1)
                gate(b, 3)
                pe.wait_ge(kv_ready, b + 1)
                pe.wait_ge(att_ready, 2 * b + 2)
                for e in range(EC):
                    es = slice(e * P, (e + 1) * P)
                    if e >= 2:
                        pe.wait_ge(o_ready, EC * b + e - 1)
                    nc.tensor.matmul(bank[3 + e % 2][:, :], kv[QK:P, es], rope[QK:P, 0, :], start=True, stop=False)
                    for t in range(TT):
                        ts = slice(t * P, (t + 1) * P)
                        last = nc.tensor.matmul(bank[3 + e % 2][:, ts], v[:, t, es], att[:, t, :], start=False,
                                                stop=t == TT - 1)
                    last.then_inc(o_done, 1)
                if not final:
                    trans_z(b + 1)
                pe.wait_ge(g_ready, EC * b + EC)
                pe.wait_ge(o_ready, EC * b + EC)
                for t in range(TT):
                    for e in range(EC):
                        last = nc.tensor.matmul(bank[5 + t // 2][:, (t % 2) * D:(t % 2 + 1) * D],
                                                oT[:, e, t * P:(t + 1) * P], wo[:, e, :], start=e == 0, stop=e == EC - 1)
                    if t % 2:
                        last.then_inc(y_done, 1)

            trans_z(0)
            pe.wait_ge(w_late, W_LATE)
            pe.wait_ge(fill, 3)
            with pe.Fori(0, B - 1) as b:
                body(b)
            body(B - 1, final=True)


def mix_layer(nc, s, w):
    x, nm, nm2, bank, ident = s.x, s.norm, s.norm2, s.bank, s.ident
    with ExitStack() as ctx:
        sb = lambda n, shape, d=F32: ctx.enter_context(nc.sbuf_tensor("mix_" + n, shape, d))
        sem = lambda n: ctx.enter_context(nc.semaphore("mix_" + n))
        wr, wk, wv = (sb(n, [P, KC, D]) for n in ("wr", "wk", "wv"))
        mu = sb("mu", [P, 2, KC])
        z = sb("z", [P, TT * D])
        zT = sb("zT", [P, KC, T + 1])
        dT = sb("dT", [P, KC, T])
        xrT, xkT = sb("xrT", [P, KC, T]), sb("xkT", [P, KC, T])
        kT = sb("kT", [P, KC, T])
        kaT = sb("kaT", [P, KC, T])
        r = sb("r", [P, TT, D])
        y = sb("y", [P, TT, D])
        zn = sb("zn", [P, TT, D])

        w_in, fill, dve_step = sem("w_in"), sem("fill"), sem("dve_step")
        var_ready, rstd_ready = sem("var_ready"), sem("rstd_ready")
        yvar_ready, yrstd_ready, yshift_ready = sem("yvar_ready"), sem("yrstd_ready"), sem("yshift_ready")
        zn_ready, sum_ready = sem("zn_ready"), sem("sum_ready")
        z_ready, zT_done, zT_ready = sem("z_ready"), sem("zT_done"), sem("zT_ready")
        xk_ready, xr_ready = sem("xk_ready"), sem("xr_ready")
        k_done, k_ready, ka_ready = sem("k_done"), sem("k_ready"), sem("ka_ready")
        r_done, r_ready, kv_done, y_ready = sem("r_done"), sem("r_ready"), sem("kv_done"), sem("y_ready")

        block = ctx.enter_context(nc.Block())
        W_IN = 16 * 5

        @block.sync
        def _(sp):
            sp.dma_start(mu[:, 0, :], w["mu_rT"]).then_inc(w_in, 16)
            sp.dma_start(mu[:, 1, :], w["mu_kT"]).then_inc(w_in, 16)
            for dst, src in ((wk, w["ffn_WkT"]), (wr, w["ffn_WrT"]), (wv, w["ffn_WvT"])):
                sp.dma_start(dst[:, :, :], src.rearrange("(k p) n -> p k n", p=P)).then_inc(w_in, 16)

        @block.gpsimd
        def _(pool):
            pool.memset(zT[:, :, 0:1], 0.0).then_inc(fill, 1)
            pool.wait_ge(fill, 1)

            def root_z(b):
                pool.wait_ge(var_ready, b + 1)
                nm.root(pool, rstd_ready)

            def body(b, last=False):
                if not last:
                    root_z(b + 1)
                for m in range(KC):
                    pool.wait_ge(k_ready, KC * b + m + 1)
                    pool.tensor_tensor(kaT[:, m, :], kT[:, m, :], kT[:, m, :], ALU.mult).then_inc(ka_ready, 1)
                pool.wait_ge(yvar_ready, b + 1)
                nm2.root_shift(pool, yrstd_ready, b + 1, yshift_ready)

            root_z(0)
            with pool.Fori(0, B - 1) as b:
                body(b)
            body(B - 1, last=True)

        @block.scalar
        def _(act):
            def move_zT(b):
                for k in range(KC):
                    act.wait_ge(zT_done, KC * b + k + 1)
                    nc.scalar.activation(zT[:, k, 1:T + 1], bank[k][:, :], ACT.Copy).then_inc(zT_ready, 1)

            def body(b, first=False, last=False):
                if not first:
                    norm_y(b - 1)
                for m in range(KC):
                    act.wait_ge(k_done, KC * b + m + 1)
                    nc.scalar.activation(kT[:, m, :], bank[2 + m][:, :], ACT.Relu).then_inc(k_ready, 1)
                for i in range(TT // 2):
                    act.wait_ge(r_done, TT // 2 * b + i + 1)
                    if not first:
                        act.wait_ge(y_ready, TT // 2 * b)
                    nc.scalar.activation(r[:, 2 * i:2 * i + 2, :], bank[4 + i][:, :].rearrange("p (t c) -> p t c", t=2),
                                         ACT.Sigmoid).then_inc(r_ready, 1)
                if not last:
                    move_zT(b + 1)

            def norm_y(b):
                act.wait_ge(yshift_ready, b + 1)
                for t in range(TT):
                    nm2.scaled(nc, zn[:, t, :], y[:, t, :], t).then_inc(zn_ready, 1)

            nc.scalar.preload_act_table(ACT.Sigmoid)
            move_zT(0)
            body(0, first=True)
            with act.Fori(1, B - 1) as b:
                body(b)
            body(B - 1, last=True)
            norm_y(B - 1)

        @block.vector
        def _(dve):
            steps = Steps(dve, dve_step)

            def front_stats(b):
                nm.stats(nc, steps, [tile_of(x, b, t) for t in range(TT)], var_ready)

            def front_norm(b):
                dve.wait_ge(rstd_ready, b + 1)
                for t in range(TT):
                    nm.apply(nc, z[:, t * D:(t + 1) * D], tile_of(x, b, t), t).then_inc(z_ready, 1)

            def shift(b):
                for k in range(KC):
                    dve.wait_ge(zT_ready, KC * b + k + 1)
                    steps.did(nc.vector.tensor_tensor(dT[:, k, :], zT[:, k, 1:T + 1], zT[:, k, 0:T], ALU.subtract))
                steps.settle()
                for i, (dst, ready) in enumerate(((xkT, xk_ready), (xrT, xr_ready))):
                    for k in range(KC):
                        nc.vector.scalar_tensor_tensor(out=dst[:, k, :], in0=dT[:, k, :], scalar=mu[:, 1 - i, k:k + 1],
                                                       in1=zT[:, k, 0:T], op0=ALU.mult, op1=ALU.add).then_inc(ready, 1)

            def gate(b):
                for i in range(TT // 2):
                    dve.wait_ge(kv_done, TT // 2 * b + i + 1)
                    dve.wait_ge(r_ready, TT // 2 * b + i + 1)
                    nc.vector.tensor_tensor(y[:, 2 * i:2 * i + 2, :], bank[6 + i][:, :].rearrange("p (t c) -> p t c", t=2),
                                            r[:, 2 * i:2 * i + 2, :], ALU.mult).then_inc(y_ready, 1)
                dve.wait_ge(y_ready, TT // 2 * b + TT // 2)
                nm2.stats(nc, steps, [y[:, t, :] for t in range(TT)], yvar_ready, minus=True)

            def rest(b):
                dve.wait_ge(zn_ready, TT * b + TT)
                nc.vector.tensor_tensor(batch_of(x, b), batch_of(x, b),
                                        zn[:, :, :].rearrange("p t c -> p (t c)"), ALU.add).then_inc(sum_ready, 1)

            def body(b, first=False, last=False):
                if not last:
                    front_stats(b + 1)
                    front_norm(b + 1)
                if not first:
                    rest(b - 1)
                if not last:
                    shift(b + 1)
                gate(b)

            front_stats(0)
            front_norm(0)
            dve.wait_ge(w_in, W_IN)
            dve.wait_ge(fill, 1)
            shift(0)
            body(0, first=True)
            steps.loop(1, B - 1, body, KC + 2 * Norm.STATS_STEPS)
            body(B - 1, last=True)
            rest(B - 1)

        @block.tensor
        def _(pe):
            def trans_z(b):
                pe.wait_ge(z_ready, TT * b + TT)
                for k in range(KC):
                    for t in range(TT):
                        last = nc.tensor.transpose(bank[k][:, t * P:(t + 1) * P],
                                                   z[:, t * D + k * P:t * D + (k + 1) * P], ident[:, :])
                    last.then_inc(zT_done, 1)

            def body(b, first=False, last=False):
                pe.wait_ge(xk_ready, KC * b + KC)
                for m in range(KC):
                    for k in range(KC):
                        mm = nc.tensor.matmul(bank[2 + m][:, :], wk[:, k, m * P:(m + 1) * P], xkT[:, k, :],
                                              start=k == 0, stop=k == KC - 1)
                    mm.then_inc(k_done, 1)
                pe.wait_ge(xr_ready, KC * b + KC)
                for t in range(TT):
                    for k in range(KC):
                        mm = nc.tensor.matmul(bank[4 + t // 2][:, (t % 2) * D:(t % 2 + 1) * D],
                                              xrT[:, k, t * P:(t + 1) * P], wr[:, k, :], start=k == 0, stop=k == KC - 1)
                    if t % 2:
                        mm.then_inc(r_done, 1)
                if not last:
                    trans_z(b + 1)
                pe.wait_ge(ka_ready, KC * b + KC)
                if not first:
                    pe.wait_ge(y_ready, TT // 2 * b)
                for t in range(TT):
                    for m in range(KC):
                        mm = nc.tensor.matmul(bank[6 + t // 2][:, (t % 2) * D:(t % 2 + 1) * D],
                                              kaT[:, m, t * P:(t + 1) * P], wv[:, m, :], start=m == 0, stop=m == KC - 1)
                    if t % 2:
                        mm.then_inc(kv_done, 1)

            trans_z(0)
            pe.wait_ge(w_in, W_IN)
            body(0, first=True)
            with pe.Fori(1, B - 1) as b:
                body(b)
            body(B - 1, last=True)


def hedgehog_layer(nc, s, w):
    x, nm, bank, ident = s.x, s.norm, s.bank, s.ident
    NF = 2 * HEADS * 2 * HD
    QW = NF // 2
    with ExitStack() as ctx:
        sb = lambda n, shape, d=F32: ctx.enter_context(nc.sbuf_tensor("hh_" + n, shape, d))
        sem = lambda n: ctx.enter_context(nc.semaphore("hh_" + n))
        rows = sb("rows", [P, 2 * KC, D])
        maps = sb("maps", [P, 2, P])
        wqk = sb("wqk", [P, KC, 2 * D])
        wv, wo = sb("wv", [P, KC, D]), sb("wo", [P, KC, D])
        bias = sb("bias", [P, 2, 1, HD])
        causal = sb("causal", [P, 1, P])
        z = sb("z", [P, TT * D])
        zT = sb("zT", [P, KC, T])
        p = sb("p", [P, 2 * HEADS, HD])
        pmax, pmin = sb("pmax", [P, 2 * HEADS, 1]), sb("pmin", [P, 2 * HEADS, 1])
        ex = sb("ex", [P, 2 * HEADS, 2, HD])
        tot, rtot = sb("tot", [P, 4 * HEADS, 1]), sb("rtot", [P, 4 * HEADS, 1])
        feat = sb("feat", [P, 2, NF])
        v1 = sb("v1", [P, 2, HEADS, VW])
        qT, kT = sb("qT", [P, FC * P]), sb("kT", [P, FC * P])
        att = sb("att", [P, HPC, FC, P])
        state = sb("state", [P, FC, P])
        yu = sb("yu", [P, FC, P])
        den, rden = sb("den", [P, HEADS]), sb("rden", [P, HEADS, 1])
        y = sb("y", [P, HEADS, HD])
        yT = sb("yT", [P, KC, P])
        o = sb("o", [P, TT, D])
        zn = sb("zn", [P, TT, D])
        b_y, b_st = bank[6], bank[7]

        w_in, fill, comp_done, comp_ready, dve_step = (sem(n) for n in ("w_in", "fill", "comp_done", "comp_ready", "dve_step"))
        map_in = sem("map_in")
        var_ready, rstd_ready = sem("var_ready"), sem("rstd_ready")
        z_ready, zT_done, zT_ready = sem("z_ready"), sem("zT_done"), sem("zT_ready")
        p_done, v_done, p_ready, v_ready = sem("p_done"), sem("v_done"), sem("p_ready"), sem("v_ready")
        max_ready, arg_ready, exp_ready, feat_ready = sem("max_ready"), sem("arg_ready"), sem("exp_ready"), sem("feat_ready")
        fT_done, fT_ready, sc_done = sem("fT_done"), sem("fT_ready"), sem("sc_done")
        even_ready, odd_moved, odd_ready = sem("even_ready"), sem("odd_moved"), sem("odd_ready")
        yu_done, yu_ready, y_done, y_ready = sem("yu_done"), sem("yu_ready"), sem("y_done"), sem("y_ready")
        st_done, st_ready = sem("st_done"), sem("st_ready")
        yT_done, yT_ready, o_done, o_ready, o_read = (sem(n) for n in ("yT_done", "yT_ready", "o_done", "o_ready", "o_read"))

        block = ctx.enter_context(nc.Block())
        W_IN, MAP_IN = 16 * 4, 16 * 18

        @block.sync
        def _(sp):
            sp.dma_start(rows[:, :, :], w["w_qk"].rearrange("(m p) c -> p m c", p=P)).then_inc(w_in, 16)
            sp.dma_start(wv[:, :, :], w["w_vT"].rearrange("(k p) n -> p k n", p=P)).then_inc(w_in, 16)
            sp.dma_start(wo[:, :, :], w["w_outT"].rearrange("(k p) n -> p k n", p=P)).then_inc(w_in, 16)
            sp.dma_start(causal[:, 0, :], w["causal"]).then_inc(w_in, 16)
            sp.dma_start(bias[:, 0, 0, :], w["bq_map"].partition_broadcast(P)).then_inc(map_in, 16)
            sp.dma_start(bias[:, 1, 0, :], w["bk_map"].partition_broadcast(P)).then_inc(map_in, 16)
            sp.wait_ge(fill, 1)
            for m, src in ((0, w["wq_mapT"]), (1, w["wk_mapT"])):
                for h in range(P // HD):
                    hs = slice(h * HD, (h + 1) * HD)
                    sp.dma_start(maps[hs, m, hs], src).then_inc(map_in, 16)

        @block.gpsimd
        def _(pool):
            pool.memset(maps[:, :, :], 0.0).then_inc(fill, 1)
            pool.memset(v1[:, :, :, HD:VW], 1.0).then_inc(fill, 1)
            pool.memset(state[:, :, :], 0.0).then_inc(fill, 1)
            pool.wait_ge(fill, 3)
            pool.wait_ge(var_ready, 1)
            nm.root(pool, rstd_ready)

            def args(g):
                pool.wait_ge(max_ready, 2 * g + 1)
                pool.tensor_tensor(ex[:, :, 0, :], p[:, :, :], pmax[:, :, :].to_broadcast([P, 2 * HEADS, HD]),
                                   ALU.subtract).then_inc(arg_ready, 1)
                pool.wait_ge(max_ready, 2 * g + 2)
                pool.tensor_tensor(ex[:, :, 1, :], pmin[:, :, :].to_broadcast([P, 2 * HEADS, HD]), p[:, :, :],
                                   ALU.subtract).then_inc(arg_ready, 1)

            def body(b, first=False, last=False):
                for t in range(TT):
                    g = TT * b + t
                    if not (last and t == TT - 1):
                        args(g + 1)
                    for i in range(HPC // 2):
                        pool.wait_ge(odd_moved, HPC // 2 * g + i + 1)
                        pool.tensor_tensor(att[:, 2 * i + 1, :, :], att[:, 2 * i + 1, :, :],
                                           causal[:, :, :].to_broadcast([P, FC, P]), ALU.mult).then_inc(odd_ready, 1)
                    if t == 0 and not last:
                        pool.wait_ge(var_ready, 2 * b + (2 if first else 1))
                        nm.root(pool, rstd_ready)
                    if t == 1 and not first:
                        pool.wait_ge(var_ready, 2 * b + (1 if last else 2))
                        nm.root(pool, rstd_ready)

            args(0)
            body(0, first=True)
            with pool.Fori(1, B - 1) as b:
                body(b)
            body(B - 1, last=True)
            pool.wait_ge(var_ready, 2 * B)
            nm.root(pool, rstd_ready)

        @block.scalar
        def _(act):
            def copy(out, in_, ready):
                nc.scalar.activation(out, in_, ACT.Copy).then_inc(ready, 1)

            def move_zT(b):
                for k in range(KC):
                    act.wait_ge(zT_done, KC * b + k + 1)
                    copy(zT[:, k, :], bank[1 + k][:, :], zT_ready)

            def move_v(g, par):
                act.wait_ge(v_done, g + 1)
                copy(v1[:, par, :, 0:HD], bank[3][:, 0:D].rearrange("p (h e) -> p h e", h=HEADS), v_ready)

            def exps(g):
                act.wait_ge(arg_ready, 2 * g + 2)
                nc.scalar.activation(ex[:, :, :, :], ex[:, :, :, :], ACT.Exp).then_inc(exp_ready, 1)

            def move_yu(g):
                act.wait_ge(yu_done, g + 1)
                copy(yu[:, :, :], b_y[:, :].rearrange("p (c i) -> p c i", c=FC), yu_ready)

            def move_yT(g):
                act.wait_ge(yT_done, g + 1)
                copy(yT[:, :, :], bank[0][:, 0:D].rearrange("p (k i) -> p k i", k=KC), yT_ready)

            def move_o(g, t, b_read):
                if t == 0:
                    act.wait_ge(o_read, TT * b_read)
                act.wait_ge(o_done, g + 1)
                copy(o[:, t, :], bank[3][:, D:2 * D], o_ready)

            def body(b, first=False, last=False):
                for t in range(TT):
                    g = TT * b + t
                    nxt = not (last and t == TT - 1)
                    if not (first and t < 2):
                        move_o(g - 2, (t - 2) % TT, b)
                    for i, dst in enumerate((qT, kT)):
                        act.wait_ge(fT_done, 2 * g + i + 1)
                        copy(dst[:, :], bank[i][:, :], fT_ready)
                    if nxt:
                        move_v(g + 1, (t + 1) % 2)
                    for i in range(HPC // 2):
                        act.wait_ge(sc_done, HPC * g + 2 * i + 2)
                        copy(att[:, 2 * i + 1, :, :], bank[5][:, :].rearrange("p (c i) -> p c i", c=FC), odd_moved)
                        if i == 0 and nxt:
                            exps(g + 1)
                    if t == 2 and not last:
                        move_zT(b + 1)
                    move_yu(g)
                    if not (first and t == 0):
                        move_yT(g - 1)

            act.wait_ge(comp_done, 2)
            for k in range(KC):
                copy(wqk[:, k, :], bank[4 + k][:, :], comp_ready)
            act.wait_ge(fill, 3)
            move_zT(0)
            move_v(0, 0)
            exps(0)
            body(0, first=True)
            with act.Fori(1, B - 1) as b:
                body(b)
            body(B - 1, last=True)
            move_o(TT * B - 2, TT - 2, B)
            move_yT(TT * B - 1)
            move_o(TT * B - 1, TT - 1, B)

        @block.vector
        def _(dve):
            steps = Steps(dve, dve_step)

            def front_stats(b):
                nm.stats(nc, steps, [tile_of(x, b, t) for t in range(TT)], var_ready)

            def front_norm(b, at):
                dve.wait_ge(rstd_ready, at)
                for t in range(TT):
                    nm.apply(nc, z[:, t * D:(t + 1) * D], tile_of(x, b, t), t).then_inc(z_ready, 1)

            def rest_stats(b):
                dve.wait_ge(o_ready, TT * b + TT)
                nm.stats(nc, steps, [o[:, t, :] for t in range(TT)], var_ready)

            def rest_norm(b, at):
                dve.wait_ge(rstd_ready, at)
                for t in range(TT):
                    nm.apply(nc, zn[:, t, :], o[:, t, :], t).then_inc(o_read, 1)

            def rest_add(b):
                dve.wait_ge(o_read, TT * b + TT)
                steps.did(nc.vector.tensor_tensor(batch_of(x, b), batch_of(x, b),
                                                  zn[:, :, :].rearrange("p t c -> p (t c)"), ALU.add))

            def project(g):
                dve.wait_ge(p_done, g + 1)
                nc.vector.tensor_tensor(p[:, :, :].rearrange("p (m h) e -> p m h e", m=2),
                                        bank[2][:, :].rearrange("p (m h e) -> p m h e", m=2, h=HEADS),
                                        bias[:, :, :, :].to_broadcast([P, 2, HEADS, HD]), ALU.add).then_inc(p_ready, 1)
                dve.wait_ge(p_ready, g + 1)
                nc.vector.tensor_reduce(pmax[:, :, 0], p[:, :, :], AX.X, ALU.max).then_inc(max_ready, 1)
                nc.vector.tensor_reduce(pmin[:, :, 0], p[:, :, :], AX.X, ALU.min).then_inc(max_ready, 1)

            def softmax(g, par):
                dve.wait_ge(exp_ready, g + 1)
                e = ex[:, :, :, :].rearrange("p h s e -> p (h s) e")
                steps.did(nc.vector.tensor_reduce(tot[:, :, 0], e, AX.X, ALU.add))
                steps.settle()
                steps.did(nc.vector.reciprocal(rtot[:, :, :], tot[:, :, :]))
                steps.settle()
                nc.vector.tensor_tensor(feat[:, par, :].rearrange("p (h e) -> p h e", e=HD), e,
                                        rtot[:, :, :].to_broadcast([P, 4 * HEADS, HD]), ALU.mult).then_inc(feat_ready, 1)

            def divide(g):
                dve.wait_ge(y_done, g + 1)
                yv = bank[0][:, :].rearrange("p (h e) -> p h e", e=2 * HD)
                steps.did(nc.vector.tensor_scalar(den[:, :], yv[:, :, HD], 1e-6, None, ALU.max))
                steps.settle()
                steps.did(nc.vector.reciprocal(rden[:, :, 0], den[:, :]))
                steps.settle()
                nc.vector.tensor_tensor(y[:, :, :], yv[:, :, 0:HD], rden[:, :, :].to_broadcast([P, HEADS, HD]),
                                        ALU.mult).then_inc(y_ready, 1)

            def body(b, first=False, last=False):
                for t in range(TT):
                    g = TT * b + t
                    if not (last and t == TT - 1):
                        project(g + 1)
                    if t == 1 and not last:
                        front_norm(b + 1, 2 * b + (2 if first else 1))
                    for i in range(HPC // 2):
                        dve.wait_ge(sc_done, HPC * g + 2 * i + 1)
                        nc.vector.tensor_tensor(att[:, 2 * i, :, :], bank[4][:, :].rearrange("p (c i) -> p c i", c=FC),
                                                causal[:, :, :].to_broadcast([P, FC, P]), ALU.mult).then_inc(even_ready, 1)
                    if t == 1 and not first:
                        rest_stats(b - 1)
                    if not (first and t == 0):
                        divide(g - 1)
                    if not (last and t == TT - 1):
                        softmax(g + 1, (t + 1) % 2)
                    if t == 0 and not last:
                        front_stats(b + 1)
                    if t == 1 and not first:
                        rest_norm(b - 1, 2 * b + (1 if last else 2))
                    if t == 2 and not first:
                        rest_add(b - 1)
                    if t < TT - 1:
                        dve.wait_ge(st_done, (TT - 1) * b + t + 1)
                    else:
                        dve.wait_ge(yu_done, g + 1)
                    for r in range(HPC):
                        rs, cs = slice(r * 2 * HD, (r + 1) * 2 * HD), slice(r * VW, (r + 1) * VW)
                        block_r = state[rs, :, r * 2 * HD:r * 2 * HD + VW]
                        if t < TT - 1:
                            nc.vector.tensor_tensor(block_r, block_r, b_st[rs, 0:HEADS * VW].rearrange(
                                "p (c n) -> p c n", c=FC)[:, :, cs], ALU.add).then_inc(st_ready, 1)
                        elif not last:
                            nc.vector.memset(block_r, 0.0).then_inc(st_ready, 1)

            front_stats(0)
            front_norm(0, 1)
            dve.wait_ge(map_in, MAP_IN)
            dve.wait_ge(w_in, W_IN)
            project(0)
            softmax(0, 0)
            BODY = TT * 4 + 1 + 2 * Norm.STATS_STEPS
            dve.wait_ge(fill, 3)
            body(0, first=True)
            steps.loop(1, B - 1, body, BODY)
            body(B - 1, last=True)
            divide(TT * B - 1)
            rest_stats(B - 1)
            rest_norm(B - 1, 2 * B)
            rest_add(B - 1)

        @block.tensor
        def _(pe):
            def trans_z(b):
                pe.wait_ge(z_ready, TT * b + TT)
                for k in range(KC):
                    for t in range(TT):
                        last = nc.tensor.transpose(bank[1 + k][:, t * P:(t + 1) * P],
                                                   z[:, t * D + k * P:t * D + (k + 1) * P], ident[:, :])
                    last.then_inc(zT_done, 1)

            def project(t):
                for k in range(KC):
                    last = nc.tensor.matmul(bank[2][:, :], zT[:, k, t * P:(t + 1) * P], wqk[:, k, :],
                                            start=k == 0, stop=k == KC - 1)
                last.then_inc(p_done, 1)

            def values(t):
                for k in range(KC):
                    last = nc.tensor.matmul(bank[3][:, 0:D], zT[:, k, t * P:(t + 1) * P], wv[:, k, :],
                                            start=k == 0, stop=k == KC - 1)
                last.then_inc(v_done, 1)

            def trans_yu(g):
                pe.wait_ge(yu_ready, g + 1)
                for c in range(FC):
                    last = nc.tensor.transpose(bank[0][:, c * P:(c + 1) * P], yu[:, c, :], ident[:, :])
                last.then_inc(y_done, 1)

            def trans_y(g):
                pe.wait_ge(y_ready, g + 1)
                for k in range(KC):
                    last = nc.tensor.transpose(bank[0][:, k * P:(k + 1) * P],
                                               y[:, k * HEADS // KC:(k + 1) * HEADS // KC, :].rearrange("p h e -> p (h e)"),
                                               ident[:, :])
                last.then_inc(yT_done, 1)

            def out(g):
                pe.wait_ge(yT_ready, g + 1)
                for k in range(KC):
                    last = nc.tensor.matmul(bank[3][:, D:2 * D], yT[:, k, :], wo[:, k, :], start=k == 0, stop=k == KC - 1)
                last.then_inc(o_done, 1)

            def body(b, first=False, last=False):
                for t in range(TT):
                    g, par = TT * b + t, t % 2
                    nxt = not (last and t == TT - 1)
                    if not (first and t < 2):
                        pe.wait_ge(v_ready, g + 1)
                        out(g - 2)
                    if nxt:
                        if t == TT - 1:
                            pe.wait_ge(zT_ready, KC * b + 2 * KC)
                        pe.wait_ge(p_ready, g + 1)
                        project((t + 1) % TT)
                    pe.wait_ge(feat_ready, g + 1)
                    if not (first and t < 1):
                        pe.wait_ge(yT_ready, g - 1)
                    for i in range(2):
                        for c in range(FC):
                            f = i * QW + c * P
                            mm = nc.tensor.transpose(bank[i][:, c * P:(c + 1) * P], feat[:, par, f:f + P], ident[:, :])
                        mm.then_inc(fT_done, 1)
                    if nxt:
                        if not (first and t < 1):
                            pe.wait_ge(o_ready, g - 1)
                        pe.wait_ge(v_ready, g + 1)
                        values((t + 1) % TT)
                    pe.wait_ge(fT_ready, 2 * g + 2)
                    for r in range(HPC):
                        rs = slice(r * 2 * HD, (r + 1) * 2 * HD)
                        if r % 2 == 0:
                            pe.wait_ge(even_ready, HPC // 2 * g + r // 2)
                        else:
                            pe.wait_ge(odd_moved, HPC // 2 * g + r // 2)
                        for c in range(FC):
                            cs = slice(c * P, (c + 1) * P)
                            mm = nc.tensor.matmul(bank[4 + r % 2][:, cs], kT[rs, cs], qT[rs, cs], start=True, stop=True)
                        mm.then_inc(sc_done, 1)
                    if not (first and t == 0):
                        trans_yu(g - 1)
                    if t == 2 and not last:
                        pe.wait_ge(p_ready, g + 2)
                        trans_z(b + 1)
                    pe.wait_ge(st_ready, HPC * g)
                    for c in range(FC):
                        cs = slice(c * P, (c + 1) * P)
                        nc.tensor.matmul(b_y[:, cs], state[:, c, :], qT[:, cs], start=c == 0, stop=False)
                    for r in range(HPC):
                        if r % 2 == 0:
                            pe.wait_ge(even_ready, HPC // 2 * g + r // 2 + 1)
                        else:
                            pe.wait_ge(odd_ready, HPC // 2 * g + r // 2 + 1)
                        for c in range(FC):
                            mm = nc.tensor.matmul(b_y[r * 2 * HD:r * 2 * HD + VW, c * P:(c + 1) * P],
                                                  v1[:, par, HPC * c + r, :], att[:, r, c, :],
                                                  start=False, stop=c == FC - 1)
                    mm.then_inc(yu_done, 1)
                    if t < TT - 1:
                        for c in range(FC):
                            mm = nc.tensor.matmul(b_st[:, c * HPC * VW:(c + 1) * HPC * VW],
                                                  feat[:, par, QW + c * P:QW + (c + 1) * P],
                                                  v1[:, par, c * HPC:(c + 1) * HPC, :].rearrange("p h e -> p (h e)"),
                                                  start=True, stop=True)
                        mm.then_inc(st_done, 1)
                    if not (first and t == 0):
                        trans_y(g - 1)

            pe.wait_ge(w_in, W_IN)
            pe.wait_ge(map_in, MAP_IN)
            for k in range(KC):
                for m in range(2 * KC):
                    mm = nc.tensor.matmul(bank[4 + k][:, m * P:(m + 1) * P], rows[:, m, k * P:(k + 1) * P],
                                          maps[:, m // KC, :], start=True, stop=True)
                mm.then_inc(comp_done, 1)
            trans_z(0)
            pe.wait_ge(comp_ready, 2)
            pe.wait_ge(zT_ready, KC)
            project(0)
            values(0)
            pe.wait_ge(fill, 3)
            body(0, first=True)
            with pe.Fori(1, B - 1) as b:
                body(b)
            body(B - 1, last=True)
            out(TT * B - 2)
            trans_yu(TT * B - 1)
            trans_y(TT * B - 1)
            pe.wait_ge(o_ready, TT * B - 1)
            out(TT * B - 1)


G_TILES = B * TT
ZW = D + NE
BLK = CAP // P
BITS = 30


def route(nc, s, w):
    x, nm, bank, ident = s.x, s.norm, s.bank, s.ident
    GE = G_TILES * NE
    with ExitStack() as ctx:
        sb = lambda n, shape, d=F32: ctx.enter_context(nc.sbuf_tensor("rt_" + n, shape, d))
        sem = lambda n: ctx.enter_context(nc.semaphore("rt_" + n))
        wg = sb("wg", [P, KC, NE])
        z = sb("z", [P, 2, TT * D])
        zT = sb("zT", [P, KC, T])
        ones, below = sb("ones", [P, P], BF16), sb("below", [P, P], BF16)
        lo_row = sb("lo_row", [P, P], BF16)
        hi_row = sb("hi_row", [P, 1, BLK])
        tile_no = sb("tile_no", [P, GE, 1])
        lane_no = sb("lane_no", [P, 1])
        carry_on = sb("carry_on", [P, GE])
        bit, next_bit = sb("bit", [P, BITS]), sb("next_bit", [P, BITS], I32)
        zeros = sb("zeros", [P, TT * D])
        top, rsum, esum = sb("top", [P, G_TILES, 1]), sb("rsum", [P, G_TILES, 1]), sb("esum", [P, G_TILES, 1])
        score = sb("score", [P, G_TILES, NE])
        by_exp = sb("by_exp", [P, NE, G_TILES])
        flag, take = sb("flag", [P, NE, G_TILES], BF16), sb("take", [P, NE, G_TILES], BF16)
        chosen = sb("chosen", [P, NE, G_TILES], BF16)
        part = sb("part", [P, NE], BF16)
        inc, low, cand = (sb(n, [P, NE, 1], I32) for n in ("inc", "low", "cand"))
        need = sb("need", [P, NE, 1])
        total, upto, rank = sb("total", [P, GE]), sb("upto", [P, GE]), sb("rank", [P, GE])
        slot, lo_i, hi_i = (sb(n, [P, GE], I32) for n in ("slot", "lo_i", "hi_i"))
        lo, hi = sb("lo", [P, GE]), sb("hi", [P, GE, 1])
        hot_hi = sb("hot_hi", [P, GE, BLK])
        number = sb("number", [P, GE, 2, BLK], BF16)
        hot_lo = sb("hot_lo", [P, 2, G_TILES, P], BF16)
        pair = sb("pair", [P, NE, 2, BLK])

        w_in, c_in, fill, dve_step = sem("w_in"), sem("c_in"), sem("fill"), sem("dve_step")
        var_ready, rstd_ready, z_ready = sem("var_ready"), sem("rstd_ready"), sem("z_ready")
        zT_done, zT_ready, logits_done = sem("zT_done"), sem("zT_ready"), sem("logits_done")
        z_out, zero_out, score_out = [sem("z_out0"), sem("z_out1")], sem("zero_out"), sem("score_out")
        shifted, exp_ready, score_ready = sem("shifted"), sem("exp_ready"), sem("score_ready")
        part_ready, count_done, flags_ready, ranks_done = sem("part_ready"), sem("count_done"), sem("flags_ready"), sem("ranks_done")
        number_ready = sem("number_ready")
        hot_ready, hot_used = [sem("hot_ready0"), sem("hot_ready1")], [sem("hot_used0"), sem("hot_used1")]
        block = ctx.enter_context(nc.Block())
        C_IN = 16 * 9
        z_rows = s.z_dram.rearrange("(g p) c -> p g c", p=P)
        acc_rows = s.acc_dram.rearrange("(g p) c -> p g c", p=P)

        @block.sync
        def _(sp):
            sp.dma_start(wg[:, :, :], w["wg"].rearrange("(k p) n -> p k n", p=P)).then_inc(w_in, 16)
            for dst, src in ((ones[:, :], w["ones"]), (below[:, :], w["below"]), (lo_row[:, :], w["lo_row"]),
                             (hi_row[:, 0, :], w["hi_row"]), (tile_no[:, :, 0], w["tile_no"]), (lane_no[:, :], w["lane_no"]),
                             (carry_on[:, :], w["carry_on"]), (bit[:, :], w["bit"]), (next_bit[:, :], w["next_bit"])):
                sp.dma_start(dst, src).then_inc(c_in, 16)
            sp.wait_ge(fill, 1)
            with sp.Fori(0, B // 2) as i:
                for par in range(2):
                    b = 2 * i + par
                    sp.wait_ge(z_ready, TT * b + TT)
                    sp.dma_start(z_rows[:, bass.ds(TT * b, TT), 0:D], z[:, par, :].rearrange("p (t c) -> p t c", t=TT))\
                        .then_inc(z_out[par], 16)
                    sp.dma_start(acc_rows[:, bass.ds(TT * b, TT), :], zeros[:, :].rearrange("p (t c) -> p t c", t=TT))\
                        .then_inc(zero_out, 16)
            sp.wait_ge(score_ready, 1)
            sp.dma_start(z_rows[:, :, D:ZW], score[:, :, :]).then_inc(score_out, 16)
            for par in range(2):
                sp.wait_ge(z_out[par], 16 * B // 2)
            sp.wait_ge(zero_out, 16 * B)
            sp.wait_ge(score_out, 16)

        @block.gpsimd
        def _(pool):
            pool.memset(zeros[:, :], 0.0).then_inc(fill, 1)
            with pool.Fori(0, B) as b:
                pool.wait_ge(var_ready, b + 1)
                nm.root(pool, rstd_ready)

        @block.scalar
        def _(act):
            with act.Fori(0, B) as b:
                for k in range(KC):
                    act.wait_ge(zT_done, KC * b + k + 1)
                    nc.scalar.activation(zT[:, k, :], bank[k][:, :], ACT.Copy).then_inc(zT_ready, 1)
            act.wait_ge(shifted, 1)
            nc.scalar.activation(score[:, :, :], score[:, :, :], ACT.Exp).then_inc(exp_ready, 1)

        @block.vector
        def _(dve):
            steps = Steps(dve, dve_step)

            def norm_pair(i):
                for par in range(2):
                    b = 2 * i + par
                    nm.stats(nc, steps, [tile_of(x, b, t) for t in range(TT)], var_ready)
                    dve.wait_ge(rstd_ready, b + 1)
                    dve.wait_ge(z_out[par], 16 * i)
                    dve.wait_ge(zT_done, 2 * KC * i)
                    for t in range(TT):
                        nm.apply(nc, z[:, par, t * D:(t + 1) * D], tile_of(x, b, t), t).then_inc(z_ready, 1)

            steps.loop(0, B // 2, norm_pair, 2 * Norm.STATS_STEPS)
            logits = bank[2][:, 0:GE].rearrange("p (g e) -> p g e", e=NE)
            wide = [P, G_TILES, NE]
            dve.wait_ge(logits_done, B)
            steps.did(nc.vector.tensor_reduce(top[:, :, 0], logits, AX.X, ALU.max))
            steps.settle()
            nc.vector.tensor_tensor(score[:, :, :], logits, top[:, :, :].to_broadcast(wide), ALU.subtract).then_inc(shifted, 1)
            dve.wait_ge(exp_ready, 1)
            steps.did(nc.vector.tensor_reduce(esum[:, :, 0], score[:, :, :], AX.X, ALU.add))
            steps.settle()
            steps.did(nc.vector.reciprocal(rsum[:, :, :], esum[:, :, :]))
            steps.settle()
            nc.vector.tensor_tensor(score[:, :, :], score[:, :, :], rsum[:, :, :].to_broadcast(wide), ALU.mult)\
                .then_inc(score_ready, 1)
            dve.wait_ge(score_ready, 1)
            steps.did(nc.vector.tensor_copy(by_exp[:, :, :], score[:, :, :].rearrange("p g e -> p e g")))
            dve.wait_ge(c_in, C_IN)
            steps.did(nc.vector.memset(low[:, :, :], 0))
            steps.did(nc.vector.memset(cand[:, :, :], 1 << (BITS - 1)))
            steps.settle()
            tall = [P, NE, G_TILES]
            count = bank[3][:, 0:NE].rearrange("p (e a) -> p e a", a=1)

            def search(i):
                steps.did(nc.vector.tensor_tensor(flag[:, :, :], by_exp[:, :, :], cand[:, :, :].bitcast(F32).to_broadcast(tall),
                                                  ALU.is_ge))
                steps.settle()
                with nc.allow_low_precision(reason="counts up to 32 are exact in bfloat16"):
                    nc.vector.tensor_reduce(part[:, :], flag[:, :, :], AX.X, ALU.add).then_inc(part_ready, 1)
                dve.wait_ge(count_done, i + 1)
                steps.did(nc.vector.scalar_tensor_tensor(
                    out=inc[:, :, :], in0=count, scalar=float(CAP),
                    in1=bit[:, bass.ds(i, 1)].rearrange("p (a o) -> p a o", a=1).to_broadcast([P, NE, 1]),
                    op0=ALU.is_ge, op1=ALU.mult))
                steps.settle()
                steps.did(nc.vector.scalar_tensor_tensor(out=cand[:, :, :], in0=low[:, :, :], scalar=next_bit[:, bass.ds(i, 1)],
                                                         in1=inc[:, :, :], op0=ALU.bitwise_or, op1=ALU.bitwise_or))
                steps.settle()
                steps.did(nc.vector.tensor_tensor(low[:, :, :], low[:, :, :], inc[:, :, :], ALU.bitwise_or))

            steps.loop(0, BITS, search, 4)
            steps.settle()
            edge = low[:, :, :].bitcast(F32).to_broadcast(tall)
            steps.did(nc.vector.tensor_tensor(flag[:, :, :], by_exp[:, :, :], edge, ALU.is_gt))
            nc.vector.tensor_tensor(take[:, :, :], by_exp[:, :, :], edge, ALU.is_equal).then_inc(flags_ready, 1)
            steps.settle()
            with nc.allow_low_precision(reason="counts up to 32 are exact in bfloat16"):
                nc.vector.tensor_reduce(part[:, :], flag[:, :, :], AX.X, ALU.add).then_inc(part_ready, 1)
            dve.wait_ge(count_done, BITS + 1)
            steps.did(nc.vector.tensor_scalar(need[:, :, :], count, -1.0, float(CAP), ALU.mult, ALU.add))

            def ranks(n, out):
                dve.wait_ge(ranks_done, n)
                steps.did(nc.vector.tensor_copy(total[:, :], bank[5][:, 0:GE]))
                steps.settle()
                steps.did(nc.vector.tensor_tensor_scan(upto[:, :], carry_on[:, :], total[:, :], 0.0, ALU.mult, ALU.add))
                steps.settle()
                steps.did(nc.vector.tensor_tensor(upto[:, :], upto[:, :], total[:, :], ALU.subtract))
                steps.settle()
                steps.did(nc.vector.tensor_tensor(out, bank[4][:, 0:GE], upto[:, :], ALU.add))
                steps.settle()

            ranks(1, rank[:, :])
            steps.did(nc.vector.tensor_tensor(chosen[:, :, :], rank[:, :].rearrange("p (e g) -> p e g", e=NE),
                                              need[:, :, :].to_broadcast(tall), ALU.is_lt))
            steps.settle()
            steps.did(nc.vector.tensor_tensor(take[:, :, :], chosen[:, :, :], take[:, :, :], ALU.mult))
            steps.settle()
            nc.vector.tensor_tensor(chosen[:, :, :], flag[:, :, :], take[:, :, :], ALU.add).then_inc(flags_ready, 1)
            ranks(2, slot[:, :])
            steps.did(nc.vector.tensor_scalar(lo_i[:, :], slot[:, :], P - 1, None, ALU.bitwise_and))
            steps.did(nc.vector.tensor_scalar(hi_i[:, :], slot[:, :], P.bit_length() - 1, None, ALU.logical_shift_right))
            steps.settle()
            steps.did(nc.vector.scalar_tensor_tensor(out=lo[:, :], in0=lo_i[:, :], scalar=1.0,
                                                     in1=chosen[:, :, :].rearrange("p e g -> p (e g)"),
                                                     op0=ALU.add, op1=ALU.mult))
            steps.did(nc.vector.tensor_copy(hi[:, :, 0], hi_i[:, :]))
            steps.settle()
            steps.did(nc.vector.tensor_tensor(hot_hi[:, :, :], hi[:, :, :].to_broadcast([P, GE, BLK]),
                                              hi_row[:, :, :].to_broadcast([P, GE, BLK]), ALU.is_equal))
            steps.settle()
            nc.vector.tensor_tensor(number[:, :, 0, :], hot_hi[:, :, :], tile_no[:, :, :].to_broadcast([P, GE, BLK]),
                                    ALU.mult).then_inc(number_ready, 1)
            nc.vector.tensor_scalar(number[:, :, 1, :], hot_hi[:, :, :], lane_no[:, :], None, ALU.mult).then_inc(number_ready, 1)
            with dve.Fori(0, NE // 2) as i:
                for par in range(2):
                    for g in range(G_TILES):
                        if g == 0:
                            dve.wait_ge(hot_used[par], i)
                        hot = nc.vector.tensor_scalar(hot_lo[:, par, g, :], lo_row[:, :],
                                                      lo[:, bass.ds((2 * i + par) * G_TILES + g, 1)], None, ALU.is_equal)
                        if g % 8 == 7:
                            hot.then_inc(hot_ready[par], 1)
            dve.wait_ge(hot_used[0], NE // 2)
            dve.wait_ge(hot_used[1], NE // 2)
            steps.did(nc.vector.tensor_copy(pair[:, :, :, :], bank[6][:, 0:NE * 2 * BLK]
                                            .rearrange("p (e a h) -> p e a h", e=NE, a=2)))
            steps.settle()
            steps.did(nc.vector.scalar_tensor_tensor(out=s.token[:, :, :], in0=pair[:, :, 0, :], scalar=float(P),
                                                     in1=pair[:, :, 1, :], op0=ALU.mult, op1=ALU.add))
            steps.settle()

        @block.tensor
        def _(pe):
            pe.wait_ge(w_in, 16)
            with pe.Fori(0, B // 2) as i:
                for par in range(2):
                    b = 2 * i + par
                    pe.wait_ge(z_ready, TT * b + TT)
                    for k in range(KC):
                        for t in range(TT):
                            last = nc.tensor.transpose(bank[k][:, t * P:(t + 1) * P],
                                                       z[:, par, t * D + k * P:t * D + (k + 1) * P], ident[:, :])
                        last.then_inc(zT_done, 1)
                    pe.wait_ge(zT_ready, KC * b + KC)
                    for t in range(TT):
                        for k in range(KC):
                            last = nc.tensor.matmul(bank[2][:, bass.ds((TT * b + t) * NE, NE)], zT[:, k, t * P:(t + 1) * P],
                                                    wg[:, k, :], start=k == 0, stop=k == KC - 1)
                    last.then_inc(logits_done, 1)
            pe.wait_ge(c_in, C_IN)
            with pe.Fori(0, BITS + 1) as i:
                pe.wait_ge(part_ready, i + 1)
                nc.tensor.matmul(bank[3][:, 0:NE], ones[:, :], part[:, :], start=True, stop=True).then_inc(count_done, 1)
            for n, src in enumerate((take, chosen)):
                pe.wait_ge(flags_ready, n + 1)
                v = src[:, :, :].rearrange("p e g -> p (e g)")
                nc.tensor.matmul(bank[4][:, 0:GE], below[:, :], v, start=True, stop=True)
                nc.tensor.matmul(bank[5][:, 0:GE], ones[:, :], v, start=True, stop=True).then_inc(ranks_done, 1)
            pe.wait_ge(number_ready, 2)
            W = 2 * BLK
            flat = number[:, :, :, :].rearrange("p n a h -> p (n a h)")
            with pe.Fori(0, NE // 2) as i:
                for par in range(2):
                    for g in range(G_TILES):
                        if g % 8 == 0:
                            pe.wait_ge(hot_ready[par], G_TILES // 8 * i + g // 8 + 1)
                        last = nc.tensor.matmul(bank[6][:, bass.ds((2 * i + par) * W, W)], hot_lo[:, par, g, :],
                                                flat[:, bass.ds(((2 * i + par) * G_TILES + g) * W, W)],
                                                start=g == 0, stop=g == G_TILES - 1)
                    last.then_inc(hot_used[par], 1)


def experts(nc, s, w):
    bank, ident = s.bank, s.ident
    HC = HID // P
    HB = BLK // 2
    with ExitStack() as ctx:
        sb = lambda n, shape, d=F32: ctx.enter_context(nc.sbuf_tensor("ex_" + n, shape, d))
        sem = lambda n: ctx.enter_context(nc.semaphore("ex_" + n))
        both = lambda n: [sem(n + "0"), sem(n + "1")]
        WN, W1, W3, W2 = 2 * KC * HID + HC * D, 0, KC * HID, 2 * KC * HID
        raw = sb("raw", [P, WN])
        wh, wl = sb("wh", [P, 2, WN], F32R), sb("wl", [P, 2, WN], F32R)
        mine = [sb(f"mine{par}", [P, BLK], I32) for par in range(2)]
        got = sb("got", [P, 2, BLK, ZW])
        rh, rl = sb("rh", [P, KC, CAP], F32R), sb("rl", [P, KC, CAP], F32R)
        gate = sb("gate", [P, 2, T])
        h = sb("h", [P, 2, T])
        hh, hl = sb("hh", [P, 2, HC, T], F32R), sb("hl", [P, 2, HC, T], F32R)
        o = sb("o", [P, BLK, D])
        nil, tick = sb("nil", [P, 1]), sb("tick", [P, 1])

        w_in, wh_ready, wl_ready = sem("w_in"), sem("wh_ready"), sem("wl_ready")
        gathered = [sem("gathered0"), sem("gathered1")]
        fill, ticked, mine_ready = sem("fill"), sem("ticked"), sem("mine_ready")
        scaled, rT_done, rh_ready, rl_ready = sem("scaled"), sem("rT_done"), sem("rh_ready"), sem("rl_ready")
        h1_done, h3_done, gate_ready, h_ready = sem("h1_done"), sem("h3_done"), sem("gate_ready"), sem("h_ready")
        hh_ready, hl_ready = sem("hh_ready"), sem("hl_ready")
        o_done, o_ready, added = sem("o_done"), sem("o_ready"), sem("added")
        block = ctx.enter_context(nc.Block())
        WC = 6
        piece = lambda c: slice(c * WN // WC, (c + 1) * WN // WC)
        NH, NT, NO, ADDS = 2 * HC, 2 * KC, BLK // 2, 16 * BLK

        def each(eng, body):
            with eng.Fori(0, NE // 2 - 1) as i:
                body(2 * i, 0, i, False)
                body(2 * i + 1, 1, i, False)
            body(NE - 2, 0, NE // 2 - 1, False)
            body(NE - 1, 1, NE // 2 - 1, True)

        @block.sync
        def _(sp):
            def load(e):
                for at, src in ((W1, w["w1"]), (W3, w["w3"]), (W2, w["w2"])):
                    n = src.shape[2]
                    sp.dma_start(raw[:, at:at + KC * HID].rearrange("p (k n) -> p k n", n=n),
                                 src[bass.ds(e, 1), :, :].rearrange("a (k p) n -> p (a k) n", p=P)).then_inc(w_in, 16)
            load(0)
            with sp.Fori(1, NE) as e:
                sp.wait_ge(wl_ready, WC * e)
                load(e)

        @block.gpsimd
        def _(pool):
            TICKS = 3 + NO

            def wait_ahead(sem, value, e, n):
                pool.wait_ge(ticked, TICKS * e + n)
                pool.wait_ge(sem, value)
                pool.tensor_tensor(tick[:, :], nil[:, :], nil[:, :], ALU.add).then_inc(ticked, 1)

            def gather(e, par, i):
                for j in range(BLK):
                    pool.indirect_dma_start(got[:, par, j, :], None, s.z_dram, bass.IndirectOffsetOnAxis(
                        ap=mine[par][:, j:j + 1], axis=0)).then_inc(gathered[par], 16)

            def split(e, par):
                for c in range(WC):
                    pool.wait_ge(wh_ready, WC * e + c + 1)
                    pool.tensor_tensor(wl[:, par, piece(c)], raw[:, piece(c)], wh[:, par, piece(c)].bitcast(F32),
                                       ALU.subtract).then_inc(wl_ready, 1)

            def body(e, par, i, last):
                if not last:
                    wait_ahead(rT_done, NT * e + NT, e, 0)
                    wait_ahead(mine_ready, e + 2, e, 1)
                    gather(e + 1, 1 - par, i)
                    split(e + 1, 1 - par)
                n = 0 if last else 2
                wait_ahead(added, ADDS * e, e, n)
                for j in range(BLK):
                    if j % 2 == 0:
                        wait_ahead(o_ready, NO * e + j // 2 + 1, e, n + 1 + j // 2)
                    pool.indirect_dma_start(s.acc_dram, bass.IndirectOffsetOnAxis(ap=mine[par][:, j:j + 1], axis=0),
                                            o[:, j, :], None, compute_op=ALU.add).then_inc(added, 16)

            pool.memset(nil[:, :], 0.0).then_inc(fill, 1)
            pool.wait_ge(fill, 1)
            pool.wait_ge(mine_ready, 1)
            gather(0, 0, 0)
            split(0, 0)
            each(pool, body)
            pool.wait_ge(added, ADDS * NE)

        @block.scalar
        def _(act):
            def move_rT(e):
                for n in range(NT):
                    half, k = n // KC, n % KC
                    act.wait_ge(rT_done, NT * e + n + 1)
                    nc.scalar.activation(rh[:, k, half * T:(half + 1) * T], bank[n][:, :], ACT.Copy).then_inc(rh_ready, 1)

            def move_o(e, half):
                if half == 0:
                    act.wait_ge(added, ADDS * e)
                for n in range(2 * half, 2 * half + 2):
                    act.wait_ge(o_done, NO * e + n + 1)
                    nc.scalar.activation(o[:, 2 * n:2 * n + 2, :], bank[6 + n % 2][:, :].rearrange("p (a c) -> p a c", a=2),
                                         ACT.Copy).then_inc(o_ready, 1)

            def split(e, par, c):
                nc.scalar.activation(wh[:, par, piece(c)], raw[:, piece(c)], ACT.Copy).then_inc(wh_ready, 1)

            def high(e, q):
                act.wait_ge(h_ready, NH * e + q + 1)
                nc.scalar.activation(hh[:, q // HC, q % HC, :], h[:, q % 2, :], ACT.Copy).then_inc(hh_ready, 1)

            def body(e, par, i, last):
                for q in range(NH):
                    act.wait_ge(h1_done, NH * e + q + 1)
                    nc.scalar.activation(gate[:, q % 2, :], bank[2 + q % 2][:, :], ACT.Silu).then_inc(gate_ready, 1)
                    if q > 0:
                        high(e, q - 1)
                    if not last and q >= NH - WC:
                        if q == NH - WC:
                            act.wait_ge(w_in, 48 * (e + 2))
                        split(e + 1, 1 - par, q - (NH - WC))
                high(e, NH - 1)
                move_o(e, 0)
                if not last:
                    move_rT(e + 1)
                move_o(e, 1)

            nc.scalar.preload_act_table(ACT.Silu)
            act.wait_ge(w_in, 48)
            for c in range(WC):
                split(0, 0, c)
            move_rT(0)
            each(act, body)

        @block.vector
        def _(dve):
            def name(e, par):
                nc.vector.tensor_scalar(mine[par][:, :], s.token[:, bass.ds(e, 1), :].rearrange("p a h -> p (a h)"),
                                        0.0, None, ALU.add).then_inc(mine_ready, 1)

            def scale(e, par, i):
                dve.wait_ge(gathered[par], ADDS * (i + 1))
                for j in range(BLK):
                    row = got[:, par, :, :].rearrange("p b c -> p (b c)")
                    nc.vector.tensor_scalar(got[:, par, j, 0:D], got[:, par, j, 0:D], row[:, bass.ds(j * ZW + D + e, 1)],
                                            None, ALU.mult).then_inc(scaled, 1)

            def low(e, q):
                dve.wait_ge(hh_ready, NH * e + q + 1)
                nc.vector.tensor_tensor(hl[:, q // HC, q % HC, :], h[:, q % 2, :], hh[:, q // HC, q % HC, :].bitcast(F32),
                                        ALU.subtract).then_inc(hl_ready, 1)

            def low_rT(e):
                for n in range(NT):
                    at = slice(n // KC * T, (n // KC + 1) * T)
                    dve.wait_ge(rh_ready, NT * e + n + 1)
                    nc.vector.tensor_tensor(rl[:, n % KC, at], bank[n][:, :], rh[:, n % KC, at].bitcast(F32),
                                            ALU.subtract).then_inc(rl_ready, 1)

            def body(e, par, i, last):
                for q in range(NH):
                    if q == HC and not last:
                        dve.wait_ge(added, ADDS * e)
                        name(e + 1, 1 - par)
                    dve.wait_ge(h3_done, NH * e + q + 1)
                    dve.wait_ge(gate_ready, NH * e + q + 1)
                    if q > 1:
                        dve.wait_ge(hl_ready, NH * e + q - 1)
                    nc.vector.tensor_tensor(h[:, q % 2, :], bank[4 + q % 2][:, :], gate[:, q % 2, :], ALU.mult)\
                        .then_inc(h_ready, 1)
                    if q > 0:
                        low(e, q - 1)
                low(e, NH - 1)
                if not last:
                    scale(e + 1, 1 - par, i + par)
                    low_rT(e + 1)

            name(0, 0)
            scale(0, 0, 0)
            low_rT(0)
            each(dve, body)

        @block.tensor
        def _(pe):
            def trans(e, par):
                pe.wait_ge(scaled, BLK * e + BLK)
                for n in range(NT):
                    half, k = n // KC, n % KC
                    for j in range(BLK // 2):
                        last = nc.tensor.transpose(bank[n][:, j * P:(j + 1) * P],
                                                   got[:, par, half * BLK // 2 + j, k * P:(k + 1) * P], ident[:, :])
                    last.then_inc(rT_done, 1)

            def product(out, stationary, moving, first, last):
                (sh, sl), (mh, ml) = stationary, moving
                nc.tensor.matmul(out, sl, mh, start=first, stop=False)
                nc.tensor.matmul(out, sh, ml, start=False, stop=False)
                return nc.tensor.matmul(out, sh, mh, start=False, stop=last)

            def out(e, par, half):
                for j in range(BLK // 2):
                    if j % 2 == 0:
                        pe.wait_ge(o_ready, NO * e + (j // 2 + 1 if half else 0))
                    for c in range(HC):
                        last = product(bank[6 + j // 2][:, (j % 2) * D:(j % 2 + 1) * D],
                                       [a[:, half, c, j * P:(j + 1) * P] for a in (hh, hl)],
                                       [a[:, par, W2 + c * D:W2 + (c + 1) * D] for a in (wh, wl)], c == 0, c == HC - 1)
                    if j % 2:
                        last.then_inc(o_done, 1)

            def body(e, par, i, last):
                pe.wait_ge(wl_ready, WC * (e + 1))
                pe.wait_ge(rl_ready, NT * e + NT)
                for q in range(NH):
                    half, c = q // HC, q % HC
                    for at, b0, done, free in ((W1, 2, h1_done, gate_ready), (W3, 4, h3_done, h_ready)):
                        pe.wait_ge(free, NH * e + max(q - 1, 0))
                        for k in range(KC):
                            col = at + k * HID + c * P
                            mm = product(bank[b0 + q % 2][:, :], [a[:, par, col:col + P] for a in (wh, wl)],
                                         [a[:, k, half * T:(half + 1) * T] for a in (rh, rl)], k == 0, k == KC - 1)
                        mm.then_inc(done, 1)
                pe.wait_ge(hl_ready, NH * e + HC)
                out(e, par, 0)
                if not last:
                    pe.wait_ge(gate_ready, NH * e + NH)
                    trans(e + 1, 1 - par)
                pe.wait_ge(hl_ready, NH * e + NH)
                out(e, par, 1)

            trans(0, 0)
            each(pe, body)


def close(nc, s, w, out):
    x, nm = s.x, s.norm
    with ExitStack() as ctx:
        sb = lambda n, shape, d=F32: ctx.enter_context(nc.sbuf_tensor("cl_" + n, shape, d))
        sem = lambda n: ctx.enter_context(nc.semaphore("cl_" + n))
        y = sb("y", [P, 2, TT, D])
        zn = sb("zn", [P, 2, TT, D])
        y_in, x_out = [sem("y_in0"), sem("y_in1")], [sem("x_out0"), sem("x_out1")]
        dve_step, var_ready, rstd_ready, y_read, x_ready = (sem(n) for n in ("dve_step", "var_ready", "rstd_ready", "y_read", "x_ready"))
        block = ctx.enter_context(nc.Block())
        acc_rows = s.acc_dram.rearrange("(g p) c -> p g c", p=P)
        out_rows = out.rearrange("b (t p) c -> p (b t) c", p=P)

        @block.sync
        def _(sp):
            with sp.Fori(0, B // 2) as i:
                for par in range(2):
                    sp.wait_ge(y_read, TT * 2 * i)
                    sp.dma_start(y[:, par, :, :], acc_rows[:, bass.ds(TT * (2 * i + par), TT), :]).then_inc(y_in[par], 16)

        @block.scalar
        def _(act):
            with act.Fori(0, B // 2) as i:
                for par in range(2):
                    act.wait_ge(x_ready, 2 * i + par + 1)
                    act.dma_start(out_rows[:, bass.ds(TT * (2 * i + par), TT), :], zn[:, par, :, :]).then_inc(x_out[par], 16)
            act.wait_ge(x_out[0], 16 * B // 2)
            act.wait_ge(x_out[1], 16 * B // 2)

        @block.gpsimd
        def _(pool):
            with pool.Fori(0, B) as b:
                pool.wait_ge(var_ready, b + 1)
                nm.root(pool, rstd_ready)

        @block.vector
        def _(dve):
            steps = Steps(dve, dve_step)

            def body(i):
                for par in range(2):
                    b = 2 * i + par
                    dve.wait_ge(y_in[par], 16 * i + 16)
                    nm.stats(nc, steps, [y[:, par, t, :] for t in range(TT)], var_ready)
                    dve.wait_ge(x_out[par], 16 * i)
                    dve.wait_ge(rstd_ready, b + 1)
                    for t in range(TT):
                        nm.apply(nc, zn[:, par, t, :], y[:, par, t, :], t).then_inc(y_read, 1)
                    dve.wait_ge(y_read, TT * b + TT)
                    flat = zn[:, par, :, :].rearrange("p t c -> p (t c)")
                    nc.vector.tensor_tensor(flat, flat, batch_of(x, b), ALU.add).then_inc(x_ready, 1)

            steps.loop(0, B // 2, body, 2 * Norm.STATS_STEPS)


class Shared:
    pass


def build(nc, ins, out):
    w = dict(ins)
    pos = np.arange(T, dtype=np.float32)
    freq = (np.float32(10000.0) ** (-np.arange(QK // 2, dtype=np.float32) / np.float32(QK // 2))).astype(np.float32)
    angle = (pos[:, None] * freq[None, :]).astype(np.float32)
    turn = np.zeros((P, P), np.float32)
    for i in range(P):
        if i % QK < QK // 2:
            turn[i + QK // 2, i] = -1.0
        else:
            turn[i - QK // 2, i] = 1.0
    for name, a in (("ident", np.eye(P)), ("turn", turn), ("cos", np.tile(np.cos(angle).T, (4, 1))),
                    ("sin", np.tile(np.sin(angle).T, (4, 1))), ("causal", np.triu(np.ones((P, P)))),
                    ("hi_row", np.tile(np.arange(BLK), (P, 1))),
                    ("tile_no", np.tile(np.arange(G_TILES), (P, NE))), ("lane_no", np.arange(P)[:, None]),
                    ("carry_on", np.tile(np.arange(G_TILES) > 0, (P, NE))),
                    ("bit", np.tile(2.0 ** np.arange(BITS - 1, -1, -1), (P, 1)))):
        w[name] = nc.inline_tensor(np.ascontiguousarray(a, dtype=np.float32), "const_" + name).ap()
    half = mybir.dt.np(BF16)
    for name, a, dt in (("ones", np.ones((P, P)), half), ("below", np.triu(np.ones((P, P)), 1), half),
                        ("lo_row", np.tile(np.arange(1, P + 1), (P, 1)), half),
                        ("next_bit", np.tile((1 << np.arange(BITS - 1, -1, -1)) >> 1, (P, 1)), np.int32)):
        w[name] = nc.inline_tensor(np.ascontiguousarray(a.astype(dt)), "const_" + name).ap()
    with ExitStack() as ctx:
        s = Shared()
        sb = lambda n, shape, d=F32: ctx.enter_context(nc.sbuf_tensor(n, shape, d))
        s.x = sb("x", [P, B * TT * D])
        s.ident = sb("ident", [P, P])
        s.token = sb("token", [P, NE, BLK])
        s.z_dram = nc.dram_tensor("z_dram", (NTOK, ZW), F32, kind="Internal").ap()
        s.acc_dram = nc.dram_tensor("acc_dram", (NTOK, D), F32, kind="Internal").ap()
        s.norm, s.norm2 = Norm(sb), Norm(sb, "_2")
        s.bank = [ctx.enter_context(nc.psum_tensor(f"bank{i}", [P, 512], F32)) for i in range(8)]
        gau_layer(nc, s, w)
        mix_layer(nc, s, w)
        hedgehog_layer(nc, s, w)
        route(nc, s, w)
        experts(nc, s, w)
        close(nc, s, w, out)


def laid_out(i):
    flip = lambda a: a.T
    cols = lambda a: a.reshape(-1, P).T
    g = lambda n: i[n]
    return {
        "x": g("L0_attn_x").reshape(B, TT, P, D).transpose(0, 2, 1, 3).reshape(B, P, TT * D),
        "Wqk2T": np.concatenate([g("L0_attn_Wqk"), g("L0_attn_Wqk")]).T,
        "WvT": flip(g("L0_attn_Wv")), "WgT": flip(g("L0_attn_Wg")), "WoT": flip(g("L0_attn_Wo")),
        "ln1_wT": cols(g("L0_attn_ln1_w")), "ln1_bT": cols(g("L0_attn_ln1_b")),
        "bqk2": np.concatenate([g("L0_attn_bqk"), g("L0_attn_bqk")]).reshape(P, 1),
        "gammaT": cols(g("L0_attn_gamma")), "betaT": cols(g("L0_attn_beta")), "bgT": cols(g("L0_attn_bg")),
        "bv": g("L0_attn_bv"), "bo": g("L0_attn_bo"), "ln2_w": g("L0_attn_ln2_w"), "ln2_b": g("L0_attn_ln2_b"),
        "pos_emb": g("L0_attn_pos_emb"),
        "ffn_WrT": flip(g("L0_ffn_W_r")), "ffn_WkT": flip(g("L0_ffn_W_k")), "ffn_WvT": flip(g("L0_ffn_W_v")),
        "mu_rT": cols(g("L0_ffn_mu_r")), "mu_kT": cols(g("L0_ffn_mu_k")),
        "w_qk": g("L1_attn_w_qkv")[:2 * D], "w_vT": flip(g("L1_attn_w_qkv")[2 * D:]),
        "wq_mapT": flip(g("L1_attn_wq_map")), "wk_mapT": flip(g("L1_attn_wk_map")),
        "bq_map": g("L1_attn_bq_map"), "bk_map": g("L1_attn_bk_map"), "w_outT": flip(g("L1_attn_w_out")),
        "wg": g("L1_ffn_wg"), "w1": g("L1_ffn_w1"), "w3": g("L1_ffn_w3"), "w2": g("L1_ffn_w2"),
    }


def kernel(**inputs):
    import concourse.bacc as bacc
    from concourse.bass_utils import run_bass_kernel_spmd

    nc = bacc.Bacc("TRN2", target_bir_lowering=False, num_devices=1)
    arrays, ins = {}, {}
    for name, a in laid_out({n: np.asarray(a) for n, a in inputs.items()}).items():
        arrays["in_" + name] = np.ascontiguousarray(a)
        ins[name] = nc.dram_tensor("in_" + name, a.shape, mybir.dt.from_np(a.dtype), kind="ExternalInput").ap()
    out = nc.dram_tensor("out_0", (B, T, D), F32, kind="ExternalOutput").ap()
    build(nc, ins, out)
    r = run_bass_kernel_spmd(nc, [arrays], core_ids=[0])
    return r.results[0]["out_0"]
```

```python
import numpy as np
from contextlib import ExitStack

import concourse.bass as bass
from concourse import mybir

F32 = mybir.dt.float32
F32R = mybir.dt.float32r
BF16 = mybir.dt.bfloat16
I32 = mybir.dt.int32
ALU = mybir.AluOpType
ACT = mybir.ActivationFunctionType
AX = mybir.AxisListType

B, T, D = 8, 512, 256
P = 128
TT = T // P
KC = D // P
NTOK = B * T
EPS = 1e-5
QK, H = 64, 512
EC = H // P
GROUP, MAX_REL = 64, 32
HEADS, HD = 16, 16
HPC = 4
FC = HEADS // HPC
VW = HD + 1
NE, CAP, HID = 8, 1024, 512


class Steps:

    def __init__(self, sem):
        self.sem, self.count, self.reg = sem, 0, None

    def on(self, eng):
        self.eng = eng
        return self

    def did(self, ins):
        ins.then_inc(self.sem, 1)
        self.count += 1

    def settle(self):
        if self.reg is None:
            self.eng.wait_ge(self.sem, self.count)
        else:
            self.eng.wait_ge(self.sem, self.reg * self.per + (self.count - self.lo * self.per))

    def loop(self, lo, hi, body, per):
        first = self.count
        with self.eng.Fori(lo, hi) as i:
            self.reg, self.per, self.lo = i, per, lo
            body(i)
        assert self.count - first == per, (self.count - first, per)
        self.reg, self.count = None, first + per * (hi - lo)


class Split:

    def __init__(self, sb, name, shape, full=True):
        self.full = sb(name, shape) if full else None
        self.high, self.low = sb(name + "_high", shape, F32R), sb(name + "_low", shape, F32R)

    def parts(self, k, cols=slice(None)):
        return self.high[:, k, cols], self.low[:, k, cols]


def product(nc, out, stationary, moving, first, last):
    (sh, sl), (mh, ml) = stationary, moving
    nc.tensor.matmul(out, sl, mh, start=first, stop=False)
    nc.tensor.matmul(out, sh, ml, start=False, stop=False)
    return nc.tensor.matmul(out, sh, mh, start=False, stop=last)


def tile_of(x, b, t):
    return x[:, bass.ds(b * (TT * D) + t * D, D)]


def batch_of(x, b):
    return x[:, bass.ds(b * (TT * D), TT * D)]


class Norm:

    def __init__(self, sb, tag=""):
        sb = lambda n, shape, sb=sb: sb(n + tag, shape)
        self.st = sb("ln_stats", [P, TT, 6])
        self.sum = sb("ln_sum", [P, TT])
        self.dif = sb("ln_dif", [P, TT])
        self.cv = sb("ln_cv", [P, TT])
        self.sq = sb("ln_sq", [P, TT])
        self.v = sb("ln_v", [P, TT])
        self.mean = sb("ln_mean", [P, TT])
        self.var = sb("ln_var", [P, TT])
        self.rstd = sb("ln_rstd", [P, TT])
        self.mhalf = sb("ln_mhalf", [P, TT])
        self.shift = sb("ln_shift", [P, TT])

    def stats(self, nc, steps, tiles, var_ready, twice=False, minus=False):
        for t in range(len(tiles)):
            steps.did(nc.vector.bn_stats(self.st[:, t, :], tiles[t]))
        steps.settle()
        steps.did(nc.vector.tensor_tensor(self.dif[:, :], self.st[:, :, 1], self.st[:, :, 4], ALU.subtract))
        steps.did(nc.vector.tensor_tensor(self.sum[:, :], self.st[:, :, 1], self.st[:, :, 4], ALU.add))
        steps.did(nc.vector.tensor_tensor(self.cv[:, :], self.st[:, :, 2], self.st[:, :, 5], ALU.add))
        steps.settle()
        steps.did(nc.vector.tensor_tensor(self.sq[:, :], self.dif[:, :], self.dif[:, :], ALU.mult))
        steps.did(nc.vector.tensor_scalar(self.mean[:, :], self.sum[:, :], -0.5 if minus else 0.5, None, ALU.mult))
        steps.settle()
        steps.did(nc.vector.scalar_tensor_tensor(out=self.v[:, :], in0=self.sq[:, :], scalar=D / 4.0,
                                                 in1=self.cv[:, :], op0=ALU.mult, op1=ALU.add))
        steps.settle()
        a, e = (1 + EPS, EPS * EPS) if twice else (1.0, EPS)
        nc.vector.tensor_scalar(self.var[:, :], self.v[:, :], a / D, e, ALU.mult, ALU.add).then_inc(var_ready, 1)

    STATS_STEPS = TT + 6

    def root(self, pool, rstd_ready):
        pool.tensor_tensor(self.rstd[:, :], self.var[:, :], self.mhalf[:, :], ALU.pow).then_inc(rstd_ready, 1)

    def root_shift(self, pool, rstd_ready, at, shift_ready):
        self.root(pool, rstd_ready)
        pool.wait_ge(rstd_ready, at)
        pool.tensor_tensor(self.shift[:, :], self.mean[:, :], self.rstd[:, :], ALU.mult).then_inc(shift_ready, 1)

    def scaled(self, nc, out, in_, t):
        return nc.scalar.activation(out, in_, ACT.Identity, bias=self.shift[:, t:t + 1], scale=self.rstd[:, t:t + 1])

    def ahead_stats(self, nc, s, steps):
        self.stats(nc, steps, [tile_of(s.x, 0, t) for t in range(TT)], s.ahead_var)
        s.aheads += 1

    def ahead_root(self, pool, s, n):
        pool.wait_ge(s.ahead_var, n)
        self.root(pool, s.ahead_rstd)

    def ahead_norm(self, nc, s, steps):
        steps.eng.wait_ge(s.ahead_rstd, s.aheads)
        for t in range(TT):
            steps.did(self.apply(nc, s.z[:, t * D:(t + 1) * D], tile_of(s.x, 0, t), t))
        steps.settle()

    def apply(self, nc, out, in_, t):
        return nc.vector.tensor_scalar(out, in_, self.mean[:, t:t + 1], self.rstd[:, t:t + 1],
                                       ALU.subtract, ALU.mult)


def gau_layer(nc, s, w):
    x, nm, bank, ident = s.x, s.norm, s.bank, s.ident
    with ExitStack() as ctx:
        sb = lambda n, shape, d=F32: ctx.enter_context(nc.sbuf_tensor("gau_" + n, shape, d))
        sems = []

        def sem(n):
            sems.append(ctx.enter_context(nc.semaphore("gau_" + n)))
            return sems[-1]

        wqk = Split(sb, "wqk", [P, KC, 2 * QK])
        wv = Split(sb, "wv", [P, KC, H])
        wg = Split(sb, "wg", [P, KC, H])
        wo = Split(sb, "wo", [P, EC, D])
        cos, sin = sb("cos", [P, T]), sb("sin", [P, T])
        turn = sb("turn", [P, P])
        ln1 = sb("ln1", [P, 2, KC])
        bqk = sb("bqk", [P, 1])
        gamma, beta = sb("gamma", [P, 2]), sb("beta", [P, 2])
        bg = sb("bg", [P, EC])
        bv_row = sb("bv_row", [P, H])
        bo_row = sb("bo_row", [P, D])
        ln2 = sb("ln2", [P, 2, D])
        pos_row = sb("pos_row", [1, 2 * MAX_REL + 1])
        rel_row = sb("rel_row", [1, 2 * GROUP])
        rel_flip = sb("rel_flip", [P, GROUP])
        rel = sb("rel", [P, 1, GROUP])
        z = s.z
        xnT = Split(sb, "xnT", [P, KC, T])
        sT = sb("sT", [P, T])
        lin = sb("lin", [P, 2, T])
        lcos = sb("lcos", [P, 2, T])
        lsin = sb("lsin", [P, 2, T])
        rope = sb("rope", [P, 2, T])
        v = sb("v", [P, TT, H])
        k_tok = sb("k_tok", [P, TT, P])
        sim = sb("sim", [P, TT, GROUP])
        att = sb("att", [P, TT, P])
        kv = sb("kv", [P, H])
        gT = sb("gT", [P, EC, T])
        oT = Split(sb, "oT", [P, EC, T])
        y = sb("y", [P, TT, D])
        zn = sb("zn", [P, TT, D])
        wz = sb("wz", [P, TT, D])
        rel_dram = nc.dram_tensor("rel_dram", (2 * GROUP,), F32, kind="Internal").ap()

        w_early, w_late, w_rows = sem("w_early"), sem("w_late"), sem("w_rows")
        pos_in, rel_out, rel_in = sem("pos_in"), sem("rel_out"), sem("rel_in")
        x_first, x_rest = sem("x_first"), sem("x_rest")
        fill = sem("fill")
        dve_step = s.steps.sem
        var_ready, rstd_ready = sem("var_ready"), sem("rstd_ready")
        z_ready, zT_done = sem("z_ready"), sem("zT_done")
        w_high, w_low, xn_high, xn_low, o_high, o_low = (sem(n) for n in (
            "w_high", "w_low", "xn_high", "xn_low", "o_high", "o_low"))
        qk_done, s_ready, lin_ready = sem("qk_done"), sem("s_ready"), sem("lin_ready")
        v_done, v_biased, v_ready = sem("v_done"), sem("v_biased"), sem("v_ready")
        turn_done, lcos_ready, rope_ready = sem("turn_done"), sem("lcos_ready"), sem("rope_ready")
        sim_done, att_ready = sem("sim_done"), sem("att_ready")
        kT_done, k_ready, kv_done, kv_ready = sem("kT_done"), sem("k_ready"), sem("kv_done"), sem("kv_ready")
        g_done, g_ready, o_done, o_ready, y_done = (sem(n) for n in ("g_done", "g_ready", "o_done", "o_ready", "y_done"))
        y_moved, zn_ready, wz_ready = sem("y_moved"), sem("zn_ready"), sem("wz_ready")

        block = ctx.enter_context(nc.Block())

        @block.sync
        def _(sp):
            sp.dma_start(batch_of(x, 0), w["x"][0]).then_inc(x_first, 16)
            sp.dma_start(ident[:, :], w["ident"]).then_inc(w_early, 16)
            sp.dma_start(ln1[:, 0, :], w["ln1_wT"]).then_inc(w_early, 16)
            sp.dma_start(ln1[:, 1, :], w["ln1_bT"]).then_inc(w_early, 16)
            sp.dma_start(wqk.full[:, :, :], w["Wqk2T"].rearrange("(k p) n -> p k n", p=P)).then_inc(w_early, 16)
            sp.dma_start(bqk[:, :], w["bqk2"]).then_inc(w_early, 16)
            sp.dma_start(gamma[:, :], w["gammaT"]).then_inc(w_early, 16)
            sp.dma_start(beta[:, :], w["betaT"]).then_inc(w_early, 16)
            sp.dma_start(wv.full[:, :, :], w["WvT"].rearrange("(k p) n -> p k n", p=P)).then_inc(w_late, 16)
            sp.dma_start(wg.full[:, :, :], w["WgT"].rearrange("(k p) n -> p k n", p=P)).then_inc(w_late, 16)
            sp.dma_start(turn[:, :], w["turn"]).then_inc(w_late, 16)
            sp.dma_start(bg[:, :], w["bgT"]).then_inc(w_late, 16)
            sp.dma_start(wo.full[:, :, :], w["WoT"].rearrange("(k p) n -> p k n", p=P)).then_inc(w_late, 16)
            for b in range(1, B):
                sp.dma_start(batch_of(x, b), w["x"][b]).then_inc(x_rest, 16)
            sp.wait_ge(dve_step, Norm.STATS_STEPS + 3)
            sp.dma_start(rel_dram, rel_row[0, :]).then_inc(rel_out, 16)
            sp.wait_ge(rel_out, 16)
            for g in range(2):
                sp.dma_start(rel_flip[g * GROUP:(g + 1) * GROUP, :],
                             bass.AP(tensor=rel_dram.tensor, offset=0, ap=[[1, GROUP], [1, GROUP]])).then_inc(rel_in, 16)
            s.mix_loads.issue(sp, w)

        W_EARLY, W_LATE, W_ROWS = 16 * 7, 16 * 5, 16 * 6

        @block.gpsimd
        def _(pool):
            pool.memset(nm.mhalf[:, :], -0.5).then_inc(fill, 1)
            pool.memset(s.norm2.mhalf[:, :], -0.5).then_inc(fill, 1)
            pool.memset(att[:, :, :], 0.0).then_inc(fill, 1)
            pool.wait_ge(w_rows, W_ROWS)
            pool.wait_ge(fill, 3)
            pool.wait_ge(var_ready, 1)
            nm.root(pool, rstd_ready)

            def root(at):
                pool.wait_ge(var_ready, at)
                nm.root(pool, rstd_ready)

            def scale_ln2(b):
                pool.wait_ge(zn_ready, TT * b + TT)
                pool.tensor_tensor(wz[:, :, :], zn[:, :, :], ln2[:, 0:1, :].to_broadcast([P, TT, D]), ALU.mult)\
                    .then_inc(wz_ready, 1)

            def body(b, first=False, last=False):
                if not first:
                    root(3 * b)
                for j in (1, 0):
                    pool.wait_ge(lin_ready, 2 * b + 2 - j)
                    pool.tensor_tensor(lcos[:, j, :], lin[:, j, :], cos[:, :], ALU.mult).then_inc(lcos_ready, 1)
                if not first:
                    scale_ln2(b - 1)
                    root(3 * b + 1)
                if not last:
                    root(3 * b + 2)

            body(0, first=True)
            with pool.Fori(1, B - 1) as b:
                body(b)
            body(B - 1, last=True)
            root(3 * B - 1)
            s.norm2.ahead_root(pool, s, 1)
            scale_ln2(B - 1)
            root(3 * B)

        @block.scalar
        def _(act):
            act.dma_start(pos_row[:, :], w["pos_emb"].rearrange("(a n) -> a n", a=1)).then_inc(pos_in, 16)
            act.dma_start(cos[:, :], w["cos"]).then_inc(w_rows, 16)
            act.dma_start(sin[:, :], w["sin"]).then_inc(w_rows, 16)
            act.dma_start(bv_row[:, :], w["bv"].partition_broadcast(P)).then_inc(w_rows, 16)
            act.dma_start(bo_row[:, :], w["bo"].partition_broadcast(P)).then_inc(w_rows, 16)
            act.dma_start(ln2[:, 0, :], w["ln2_w"].partition_broadcast(P)).then_inc(w_rows, 16)
            act.dma_start(ln2[:, 1, :], w["ln2_b"].partition_broadcast(P)).then_inc(w_rows, 16)
            act.wait_ge(w_early, W_EARLY)
            for m in (wqk, wv, wg, wo):
                if m is wv:
                    act.wait_ge(w_late, W_LATE)
                nc.scalar.activation(m.high[:, :, :], m.full[:, :, :], ACT.Copy).then_inc(w_high, 1)

            def move_xn(b):
                for k in range(KC):
                    act.wait_ge(zT_done, KC * b + k + 1)
                    for to in (xnT.full, xnT.high):
                        nc.scalar.activation(to[:, k, :], bank[k][:, :], ACT.Identity, bias=ln1[:, 1, k:k + 1],
                                             scale=ln1[:, 0, k:k + 1]).then_inc(xn_high, 1)

            def body(b, last=False):
                act.wait_ge(qk_done, b + 1)
                nc.scalar.activation(sT[:, :], bank[2][:, :], ACT.Silu, bias=bqk[:, :]).then_inc(s_ready, 1)
                for t in range(TT):
                    act.wait_ge(v_biased, TT * b + t + 1)
                    nc.scalar.activation(v[:, t, :], v[:, t, :], ACT.Silu).then_inc(v_ready, 1)
                for e in range(EC):
                    if e == 3:
                        act.wait_ge(kv_done, b + 1)
                        nc.scalar.activation(kv[QK:P, :], bank[7][QK:P, :], ACT.Copy, scale=1.0 / T).then_inc(kv_ready, 1)
                    if e == 2:
                        act.wait_ge(kT_done, b + 1)
                        nc.scalar.activation(k_tok[:, :, :], bank[7][:, :].rearrange("p (t n) -> p t n", t=TT),
                                             ACT.Copy).then_inc(k_ready, 1)
                    act.wait_ge(g_done, EC * b + e + 1)
                    nc.scalar.activation(gT[:, e, :], bank[5 + e % 2][:, :], ACT.Silu, bias=bg[:, e:e + 1])\
                        .then_inc(g_ready, 1)
                for e in range(EC):
                    act.wait_ge(o_ready, EC * b + e + 1)
                    nc.scalar.activation(oT.high[:, e, :], oT.full[:, e, :], ACT.Copy).then_inc(o_high, 1)
                if not last:
                    move_xn(b + 1)

            nc.scalar.preload_act_table(ACT.Silu)
            move_xn(0)
            with act.Fori(0, B - 1) as b:
                body(b)
            body(B - 1, last=True)

        @block.vector
        def _(dve):
            steps = s.steps.on(dve)

            def low_xn(b):
                for k in range(KC):
                    dve.wait_ge(xn_high, 2 * (KC * b + k + 1))
                    nc.vector.tensor_tensor(xnT.low[:, k, :], xnT.full[:, k, :], xnT.high[:, k, :].bitcast(F32),
                                            ALU.subtract).then_inc(xn_low, 1)

            def low_o(b, e):
                dve.wait_ge(o_high, EC * b + e + 1)
                nc.vector.tensor_tensor(oT.low[:, e, :], oT.full[:, e, :], oT.high[:, e, :].bitcast(F32),
                                        ALU.subtract).then_inc(o_low, 1)

            def front_stats(b):
                nm.stats(nc, steps, [tile_of(x, b, t) for t in range(TT)], var_ready, twice=True)

            def front_norm(b, at):
                dve.wait_ge(rstd_ready, at)
                for t in range(TT):
                    nm.apply(nc, z[:, t * D:(t + 1) * D], tile_of(x, b, t), t).then_inc(z_ready, 1)

            def rest_stats(b):
                dve.wait_ge(y_moved, TT // 2 * (b + 1))
                nm.stats(nc, steps, [y[:, t, :] for t in range(TT)], var_ready)

            def rest_norm(at):
                dve.wait_ge(rstd_ready, at)
                for t in range(TT):
                    nm.apply(nc, zn[:, t, :], y[:, t, :], t).then_inc(zn_ready, 1)

            def rest_affine(b):
                dve.wait_ge(wz_ready, b + 1)
                steps.did(nc.vector.tensor_tensor(y[:, :, :], wz[:, :, :], ln2[:, 1:2, :].to_broadcast([P, TT, D]), ALU.add))
                steps.settle()
                nm.stats(nc, steps, [y[:, t, :] for t in range(TT)], var_ready)

            def rest_add(b, at):
                dve.wait_ge(rstd_ready, at)
                for t in range(TT):
                    steps.did(nm.apply(nc, zn[:, t, :], y[:, t, :], t))
                steps.settle()
                steps.did(nc.vector.tensor_tensor(batch_of(x, b), batch_of(x, b),
                                                  zn[:, :, :].rearrange("p t c -> p (t c)"), ALU.add))

            REST = 2 * Norm.STATS_STEPS + TT + 2

            def body(b, first=False, last=False):
                if not first:
                    rest_stats(b - 1)
                dve.wait_ge(s_ready, b + 1)
                for j in (1, 0):
                    nc.vector.tensor_scalar(lin[:, j, :], sT[:, :], gamma[:, j:j + 1], beta[:, j:j + 1],
                                            ALU.mult, ALU.add).then_inc(lin_ready, 1)
                for t in range(TT):
                    dve.wait_ge(v_done, TT * b + t + 1)
                    nc.vector.tensor_tensor(v[:, t, :], bank[5 + t % 2][:, :], bv_row[:, :], ALU.add)\
                        .then_inc(v_biased, 1)
                    if t == 1 and not first:
                        rest_norm(3 * b)
                for i, j in enumerate((1, 0)):
                    dve.wait_ge(turn_done, 2 * b + i + 1)
                    steps.did(nc.vector.tensor_tensor(lsin[:, j, :], bank[3 + j][:, :], sin[:, :], ALU.mult))
                steps.settle()
                for i, j in enumerate((1, 0)):
                    dve.wait_ge(lcos_ready, 2 * b + i + 1)
                    nc.vector.tensor_tensor(rope[:, j, :], lcos[:, j, :], lsin[:, j, :], ALU.add).then_inc(rope_ready, 1)
                if not first:
                    rest_affine(b - 1)
                if first:
                    dve.wait_ge(rel_in, 32)
                    steps.did(nc.vector.tensor_copy(rel[:, 0, :], rel_flip[:, ::-1]))
                    steps.settle()
                dve.wait_ge(sim_done, b + 1)
                for g in range(2):
                    rows = slice(g * GROUP, (g + 1) * GROUP)
                    steps.did(nc.vector.scalar_tensor_tensor(
                        out=sim[rows, :, :], in0=bank[2][rows, :].rearrange("p (t i) -> p t i", t=TT)[:, :, rows],
                        scalar=1.0 / GROUP, in1=rel[rows, :, :].to_broadcast([GROUP, TT, GROUP]), op0=ALU.mult, op1=ALU.add))
                steps.settle()
                for g in range(2):
                    rows = slice(g * GROUP, (g + 1) * GROUP)
                    nc.vector.scalar_tensor_tensor(out=att[rows, :, rows], in0=sim[rows, :, :], scalar=0.0,
                                                   in1=sim[rows, :, :], op0=ALU.max, op1=ALU.mult).then_inc(att_ready, 1)
                if not first:
                    rest_add(b - 1, 3 * b + 1)
                if not last:
                    front_stats(b + 1)
                for e in range(EC):
                    if e == 1 and not last:
                        front_norm(b + 1, 3 * b + 2)
                    dve.wait_ge(o_done, EC * b + e + 1)
                    dve.wait_ge(g_ready, EC * b + e + 1)
                    nc.vector.tensor_tensor(oT.full[:, e, :], bank[3 + e % 2][:, :], gT[:, e, :], ALU.mult).then_inc(o_ready, 1)
                    if e > 0:
                        low_o(b, e - 1)
                low_o(b, EC - 1)
                if not last:
                    low_xn(b + 1)
                for i in range(TT // 2):
                    dve.wait_ge(y_done, TT // 2 * b + i + 1)
                    nc.vector.tensor_tensor(y[:, 2 * i:2 * i + 2, :], bank[5 + i][:, :].rearrange("p (t c) -> p t c", t=2),
                                            bo_row[:, :].rearrange("p (a c) -> p a c", a=1).to_broadcast([P, 2, D]),
                                            ALU.add).then_inc(y_moved, 1)

            BODY = 4 + Norm.STATS_STEPS + REST
            dve.wait_ge(x_first, 16)
            front_stats(0)
            front_norm(0, 1)
            for n, m in enumerate((wqk, wv, wg, wo)):
                if n == 1:
                    low_xn(0)
                dve.wait_ge(w_high, n + 1)
                nc.vector.tensor_tensor(m.low[:, :, :], m.full[:, :, :], m.high[:, :, :].bitcast(F32), ALU.subtract)\
                    .then_inc(w_low, 1)
            dve.wait_ge(pos_in, 16)
            steps.did(nc.vector.tensor_copy(rel_row[:, :], pos_row[:, MAX_REL:MAX_REL + 1].to_broadcast([1, 2 * GROUP])))
            steps.settle()
            mid = GROUP - 1
            steps.did(nc.vector.tensor_copy(rel_row[:, mid:mid + MAX_REL], pos_row[:, 0:MAX_REL]))
            steps.did(nc.vector.tensor_copy(rel_row[:, mid - MAX_REL + 1:mid], pos_row[:, 1:MAX_REL][:, ::-1]))
            dve.wait_ge(w_early, W_EARLY)
            dve.wait_ge(w_rows, W_ROWS)
            dve.wait_ge(fill, 3)
            dve.wait_ge(x_rest, 16 * (B - 1))
            body(0, first=True)
            steps.loop(1, B - 1, body, BODY)
            body(B - 1, last=True)
            rest_stats(B - 1)
            s.norm2.ahead_stats(nc, s, steps)
            rest_norm(3 * B - 1)
            s.norm2.ahead_norm(nc, s, steps)
            rest_affine(B - 1)
            rest_add(B - 1, 3 * B)

        @block.tensor
        def _(pe):
            pe.wait_ge(w_early, W_EARLY)

            def gate(b, e):
                pe.wait_ge(v_biased, TT * b + 3 + e) if e < 2 else pe.wait_ge(g_ready, EC * b + e - 1)
                for k in range(KC):
                    last = product(nc, bank[5 + e % 2][:, :], wg.parts(k, slice(e * P, (e + 1) * P)), xnT.parts(k),
                                   k == 0, k == KC - 1)
                last.then_inc(g_done, 1)

            def trans_z(b):
                pe.wait_ge(z_ready, TT * b + TT)
                for k in range(KC):
                    for t in range(TT):
                        last = nc.tensor.transpose(bank[k][:, t * P:(t + 1) * P],
                                                   z[:, t * D + k * P:t * D + (k + 1) * P], ident[:, :])
                    last.then_inc(zT_done, 1)

            def body(b, final=False):
                pe.wait_ge(xn_low, KC * b + KC)
                for k in range(KC):
                    last = product(nc, bank[2][:, :], wqk.parts(k), xnT.parts(k), k == 0, k == KC - 1)
                last.then_inc(qk_done, 1)
                for t in range(TT):
                    if t < 2:
                        pe.wait_ge(y_moved, TT // 2 * b)
                    else:
                        pe.wait_ge(v_biased, TT * b + t - 1)
                    for k in range(KC):
                        last = product(nc, bank[5 + t % 2][:, :], xnT.parts(k, slice(t * P, (t + 1) * P)), wv.parts(k),
                                       k == 0, k == KC - 1)
                    last.then_inc(v_done, 1)
                for i, j in enumerate((1, 0)):
                    pe.wait_ge(lin_ready, 2 * b + i + 1)
                    pe.wait_ge(o_ready, EC * b)
                    nc.tensor.matmul(bank[3 + j][:, :], turn[:, :], lin[:, j, :], start=True, stop=True).then_inc(turn_done, 1)
                gate(b, 0)
                gate(b, 1)
                pe.wait_ge(rope_ready, 2 * b + 2)
                for t in range(TT):
                    ts = slice(t * P, (t + 1) * P)
                    last = nc.tensor.matmul(bank[2][:, ts], rope[0:QK, 1, ts], rope[0:QK, 0, ts], start=True, stop=True)
                last.then_inc(sim_done, 1)
                pe.wait_ge(kv_ready, b)
                for t in range(TT):
                    ts = slice(t * P, (t + 1) * P)
                    last = nc.tensor.transpose(bank[7][:, ts], rope[:, 1, ts], ident[:, :])
                last.then_inc(kT_done, 1)
                gate(b, 2)
                pe.wait_ge(k_ready, b + 1)
                pe.wait_ge(v_ready, TT * b + TT)
                for t in range(TT):
                    last = nc.tensor.matmul(bank[7][:, :], k_tok[:, t, :], v[:, t, :], start=t == 0, stop=t == TT - 1)
                last.then_inc(kv_done, 1)
                gate(b, 3)
                pe.wait_ge(kv_ready, b + 1)
                pe.wait_ge(att_ready, 2 * b + 2)
                for e in range(EC):
                    es = slice(e * P, (e + 1) * P)
                    if e >= 2:
                        pe.wait_ge(o_ready, EC * b + e - 1)
                    nc.tensor.matmul(bank[3 + e % 2][:, :], kv[QK:P, es], rope[QK:P, 0, :], start=True, stop=False)
                    for t in range(TT):
                        ts = slice(t * P, (t + 1) * P)
                        last = nc.tensor.matmul(bank[3 + e % 2][:, ts], v[:, t, es], att[:, t, :], start=False,
                                                stop=t == TT - 1)
                    last.then_inc(o_done, 1)
                if not final:
                    trans_z(b + 1)
                pe.wait_ge(g_ready, EC * b + EC)
                pe.wait_ge(o_low, EC * b + EC - 1)
                for t in range(TT):
                    if t % 2 == 0:
                        for u in (t, t + 1):
                            for e in range(EC - 1):
                                product(nc, bank[5 + u // 2][:, (u % 2) * D:(u % 2 + 1) * D],
                                        oT.parts(e, slice(u * P, (u + 1) * P)), wo.parts(e), e == 0 and u % 2 == 0, False)
                        if t == 0:
                            pe.wait_ge(o_low, EC * b + EC)
                    last = product(nc, bank[5 + t // 2][:, (t % 2) * D:(t % 2 + 1) * D],
                                   oT.parts(EC - 1, slice(t * P, (t + 1) * P)), wo.parts(EC - 1), False, t % 2 == 1)
                    if t % 2:
                        last.then_inc(y_done, 1)

            trans_z(0)
            pe.wait_ge(w_late, W_LATE)
            pe.wait_ge(w_low, 4)
            pe.wait_ge(fill, 3)
            with pe.Fori(0, B - 1) as b:
                body(b)
            body(B - 1, final=True)
    first = min(sem.num for sem in sems)
    assert sorted(sem.num for sem in sems) == list(range(first, first + len(sems)))
    nc.all_engine_barrier(sems_to_clear=range(first, first + len(sems)))


class MixLoads:

    def __init__(self, nc, ctx):
        sb = lambda n, shape: ctx.enter_context(nc.sbuf_tensor("mix_" + n, shape, F32))
        self.wr, self.wk, self.wv = (sb(n, [P, KC, D]) for n in ("wr", "wk", "wv"))
        self.mu = sb("mu", [P, 2, KC])
        self.loaded, self.LOADED = ctx.enter_context(nc.semaphore("mix_loaded")), 16 * 5

    def issue(self, sp, w):
        sp.dma_start(self.mu[:, 0, :], w["mu_rT"]).then_inc(self.loaded, 16)
        sp.dma_start(self.mu[:, 1, :], w["mu_kT"]).then_inc(self.loaded, 16)
        for dst, src in ((self.wk, w["ffn_WkT"]), (self.wr, w["ffn_WrT"]), (self.wv, w["ffn_WvT"])):
            sp.dma_start(dst[:, :, :], src.rearrange("(k p) n -> p k n", p=P)).then_inc(self.loaded, 16)


def mix_layer(nc, s, w):
    x, nm, nm2, bank, ident = s.x, s.norm, s.norm2, s.bank, s.ident
    with ExitStack() as ctx:
        sb = lambda n, shape, d=F32: ctx.enter_context(nc.sbuf_tensor("mix_" + n, shape, d))
        sem = lambda n: ctx.enter_context(nc.semaphore("mix_" + n))
        early = s.mix_loads
        wr, wk, wv, mu, w_in, W_IN = early.wr, early.wk, early.wv, early.mu, early.loaded, early.LOADED
        z = s.z
        zT = sb("zT", [P, KC, T + 1])
        dT = sb("dT", [P, KC, T])
        xrT, xkT = sb("xrT", [P, KC, T]), sb("xkT", [P, KC, T])
        kT = sb("kT", [P, KC, T])
        kaT = sb("kaT", [P, KC, T])
        r = sb("r", [P, TT, D])
        y = sb("y", [P, TT, D])
        zn = sb("zn", [P, TT, D])

        fill = sem("fill")
        var_ready, rstd_ready = sem("var_ready"), sem("rstd_ready")
        yvar_ready, yrstd_ready, yshift_ready = sem("yvar_ready"), sem("yrstd_ready"), sem("yshift_ready")
        zn_ready, sum_ready = sem("zn_ready"), sem("sum_ready")
        z_ready, zT_done, zT_ready = sem("z_ready"), sem("zT_done"), sem("zT_ready")
        xk_ready, xr_ready = sem("xk_ready"), sem("xr_ready")
        k_done, k_ready, ka_ready = sem("k_done"), sem("k_ready"), sem("ka_ready")
        r_done, r_ready, kv_done, y_ready = sem("r_done"), sem("r_ready"), sem("kv_done"), sem("y_ready")

        block = ctx.enter_context(nc.Block())

        @block.sync
        def _(sp):
            s.hedgehog_loads.issue(sp, w)

        @block.gpsimd
        def _(pool):
            pool.memset(zT[:, :, 0:1], 0.0).then_inc(fill, 1)
            pool.memset(s.hedgehog_loads.maps[:, :, :], 0.0).then_inc(s.hedgehog_loads.cleared, 1)
            pool.wait_ge(fill, 1)

            def root_z(b):
                pool.wait_ge(var_ready, b)
                nm.root(pool, rstd_ready)

            def body(b, last=False):
                if not last:
                    root_z(b + 1)
                for m in range(KC):
                    pool.wait_ge(k_ready, KC * b + m + 1)
                    pool.tensor_tensor(kaT[:, m, :], kT[:, m, :], kT[:, m, :], ALU.mult).then_inc(ka_ready, 1)
                pool.wait_ge(yvar_ready, b + 1)
                nm2.root_shift(pool, yrstd_ready, b + 1, yshift_ready)

            with pool.Fori(0, B - 1) as b:
                body(b)
            nm.ahead_root(pool, s, 2)
            body(B - 1, last=True)

        @block.scalar
        def _(act):
            def move_zT(b):
                for k in range(KC):
                    act.wait_ge(zT_done, KC * b + k + 1)
                    nc.scalar.activation(zT[:, k, 1:T + 1], bank[k][:, :], ACT.Copy).then_inc(zT_ready, 1)

            def body(b, first=False, last=False):
                if not first:
                    norm_y(b - 1)
                for m in range(KC):
                    act.wait_ge(k_done, KC * b + m + 1)
                    nc.scalar.activation(kT[:, m, :], bank[2 + m][:, :], ACT.Relu).then_inc(k_ready, 1)
                for i in range(TT // 2):
                    act.wait_ge(r_done, TT // 2 * b + i + 1)
                    if not first:
                        act.wait_ge(y_ready, TT // 2 * b)
                    nc.scalar.activation(r[:, 2 * i:2 * i + 2, :], bank[4 + i][:, :].rearrange("p (t c) -> p t c", t=2),
                                         ACT.Sigmoid).then_inc(r_ready, 1)
                if not last:
                    move_zT(b + 1)

            def norm_y(b):
                act.wait_ge(yshift_ready, b + 1)
                for t in range(TT):
                    nm2.scaled(nc, zn[:, t, :], y[:, t, :], t).then_inc(zn_ready, 1)

            nc.scalar.preload_act_table(ACT.Sigmoid)
            move_zT(0)
            body(0, first=True)
            with act.Fori(1, B - 1) as b:
                body(b)
            body(B - 1, last=True)
            norm_y(B - 1)

        @block.vector
        def _(dve):
            steps = s.steps.on(dve)

            def front_stats(b):
                nm.stats(nc, steps, [tile_of(x, b, t) for t in range(TT)], var_ready)

            def front_norm(b):
                dve.wait_ge(rstd_ready, b)
                for t in range(TT):
                    nm.apply(nc, z[:, t * D:(t + 1) * D], tile_of(x, b, t), t).then_inc(z_ready, 1)

            def shift(b):
                for k in range(KC):
                    dve.wait_ge(zT_ready, KC * b + k + 1)
                    steps.did(nc.vector.tensor_tensor(dT[:, k, :], zT[:, k, 1:T + 1], zT[:, k, 0:T], ALU.subtract))
                steps.settle()
                for i, (dst, ready) in enumerate(((xkT, xk_ready), (xrT, xr_ready))):
                    for k in range(KC):
                        nc.vector.scalar_tensor_tensor(out=dst[:, k, :], in0=dT[:, k, :], scalar=mu[:, 1 - i, k:k + 1],
                                                       in1=zT[:, k, 0:T], op0=ALU.mult, op1=ALU.add).then_inc(ready, 1)

            def gate(b):
                for i in range(TT // 2):
                    dve.wait_ge(kv_done, TT // 2 * b + i + 1)
                    dve.wait_ge(r_ready, TT // 2 * b + i + 1)
                    nc.vector.tensor_tensor(y[:, 2 * i:2 * i + 2, :], bank[6 + i][:, :].rearrange("p (t c) -> p t c", t=2),
                                            r[:, 2 * i:2 * i + 2, :], ALU.mult).then_inc(y_ready, 1)
                dve.wait_ge(y_ready, TT // 2 * b + TT // 2)
                nm2.stats(nc, steps, [y[:, t, :] for t in range(TT)], yvar_ready, minus=True)

            def rest(b):
                dve.wait_ge(zn_ready, TT * b + TT)
                nc.vector.tensor_tensor(batch_of(x, b), batch_of(x, b),
                                        zn[:, :, :].rearrange("p t c -> p (t c)"), ALU.add).then_inc(sum_ready, 1)

            def body(b, first=False, last=False):
                if not last:
                    front_stats(b + 1)
                    front_norm(b + 1)
                if not first:
                    rest(b - 1)
                if not last:
                    shift(b + 1)
                gate(b)

            dve.wait_ge(w_in, W_IN)
            dve.wait_ge(fill, 1)
            shift(0)
            body(0, first=True)
            steps.loop(1, B - 1, body, KC + 2 * Norm.STATS_STEPS)
            nm.ahead_stats(nc, s, steps)
            body(B - 1, last=True)
            nm.ahead_norm(nc, s, steps)
            rest(B - 1)

        @block.tensor
        def _(pe):
            def trans_z(b, first=False):
                if not first:
                    pe.wait_ge(z_ready, TT * b)
                for k in range(KC):
                    for t in range(TT):
                        last = nc.tensor.transpose(bank[k][:, t * P:(t + 1) * P],
                                                   z[:, t * D + k * P:t * D + (k + 1) * P], ident[:, :])
                    last.then_inc(zT_done, 1)

            def body(b, first=False, last=False):
                pe.wait_ge(xk_ready, KC * b + KC)
                for m in range(KC):
                    for k in range(KC):
                        mm = nc.tensor.matmul(bank[2 + m][:, :], wk[:, k, m * P:(m + 1) * P], xkT[:, k, :],
                                              start=k == 0, stop=k == KC - 1)
                    mm.then_inc(k_done, 1)
                pe.wait_ge(xr_ready, KC * b + KC)
                for t in range(TT):
                    for k in range(KC):
                        mm = nc.tensor.matmul(bank[4 + t // 2][:, (t % 2) * D:(t % 2 + 1) * D],
                                              xrT[:, k, t * P:(t + 1) * P], wr[:, k, :], start=k == 0, stop=k == KC - 1)
                    if t % 2:
                        mm.then_inc(r_done, 1)
                if not last:
                    trans_z(b + 1)
                pe.wait_ge(ka_ready, KC * b + KC)
                if not first:
                    pe.wait_ge(y_ready, TT // 2 * b)
                for t in range(TT):
                    for m in range(KC):
                        mm = nc.tensor.matmul(bank[6 + t // 2][:, (t % 2) * D:(t % 2 + 1) * D],
                                              kaT[:, m, t * P:(t + 1) * P], wv[:, m, :], start=m == 0, stop=m == KC - 1)
                    if t % 2:
                        mm.then_inc(kv_done, 1)

            trans_z(0, first=True)
            pe.wait_ge(w_in, W_IN)
            body(0, first=True)
            with pe.Fori(1, B - 1) as b:
                body(b)
            body(B - 1, last=True)


class HedgehogLoads:

    def __init__(self, nc, ctx):
        sb = lambda n, shape: ctx.enter_context(nc.sbuf_tensor("hh_" + n, shape, F32))
        self.rows = sb("rows", [P, 2 * KC, D])
        self.maps = sb("maps", [P, 2, P])
        self.wv, self.wo = sb("wv", [P, KC, D]), sb("wo", [P, KC, D])
        self.bias = sb("bias", [P, 2, 1, HD])
        self.causal = sb("causal", [P, 1, P])
        self.cleared = ctx.enter_context(nc.semaphore("hh_cleared"))
        self.loaded = ctx.enter_context(nc.semaphore("hh_loaded"))
        self.LOADED = 16 * (6 + 2 * P // HD)

    def issue(self, sp, w):
        sp.dma_start(self.rows[:, :, :], w["w_qk"].rearrange("(m p) c -> p m c", p=P)).then_inc(self.loaded, 16)
        sp.dma_start(self.wv[:, :, :], w["w_vT"].rearrange("(k p) n -> p k n", p=P)).then_inc(self.loaded, 16)
        sp.dma_start(self.wo[:, :, :], w["w_outT"].rearrange("(k p) n -> p k n", p=P)).then_inc(self.loaded, 16)
        sp.dma_start(self.causal[:, 0, :], w["causal"]).then_inc(self.loaded, 16)
        sp.dma_start(self.bias[:, 0, 0, :], w["bq_map"].partition_broadcast(P)).then_inc(self.loaded, 16)
        sp.dma_start(self.bias[:, 1, 0, :], w["bk_map"].partition_broadcast(P)).then_inc(self.loaded, 16)
        sp.wait_ge(self.cleared, 1)
        for m, src in ((0, w["wq_mapT"]), (1, w["wk_mapT"])):
            for h in range(P // HD):
                hs = slice(h * HD, (h + 1) * HD)
                sp.dma_start(self.maps[hs, m, hs], src).then_inc(self.loaded, 16)


def hedgehog_layer(nc, s, w):
    x, nm, nm2, bank, ident = s.x, s.norm, s.norm2, s.bank, s.ident
    early = s.hedgehog_loads
    NF = 2 * HEADS * 2 * HD
    QW = NF // 2
    with ExitStack() as ctx:
        sb = lambda n, shape, d=F32: ctx.enter_context(nc.sbuf_tensor("hh_" + n, shape, d))
        sem = lambda n: ctx.enter_context(nc.semaphore("hh_" + n))
        rows, maps, causal, bias, wo = early.rows, early.maps, early.causal, early.bias, early.wo
        wqk = Split(sb, "wqk", [P, KC, 2 * D], full=False)
        wv = Split(sb, "wv", [P, KC, D], full=False)
        wv.full = early.wv
        z = s.z
        zT = Split(sb, "zT", [P, KC, T], full=False)
        p = sb("p", [P, 2 * HEADS, HD])
        pmax, pmin = sb("pmax", [P, 2 * HEADS, 1]), sb("pmin", [P, 2 * HEADS, 1])
        ex = sb("ex", [P, 2 * HEADS, 2, HD])
        tot, rtot = sb("tot", [P, 4 * HEADS, 1]), sb("rtot", [P, 4 * HEADS, 1])
        feat = sb("feat", [P, 2, NF])
        v1 = sb("v1", [P, 2, HEADS, VW])
        qT, kT = sb("qT", [P, FC * P]), sb("kT", [P, FC * P])
        att = sb("att", [P, HPC, FC, P])
        state = sb("state", [P, FC, P])
        yu = sb("yu", [P, FC, P])
        den, rden = sb("den", [P, HEADS]), sb("rden", [P, HEADS, 1])
        y = sb("y", [P, HEADS, HD])
        yT = sb("yT", [P, KC, P])
        o = sb("o", [P, TT, D])
        zn = sb("zn", [P, TT, D])
        b_y, b_st = bank[6], bank[7]

        w_in, W_IN = early.loaded, early.LOADED
        fill, comp_done = sem("fill"), sem("comp_done")
        var_ready, rstd_ready, shift_ready = sem("var_ready"), sem("rstd_ready"), sem("shift_ready")
        z_ready, zT_done, zT_high, zT_low = sem("z_ready"), sem("zT_done"), sem("zT_high"), sem("zT_low")
        w_high, w_low = sem("w_high"), sem("w_low")
        p_done, v_done, p_ready, v_ready = sem("p_done"), sem("v_done"), sem("p_ready"), sem("v_ready")
        max_ready, arg_ready, exp_ready, feat_ready = sem("max_ready"), sem("arg_ready"), sem("exp_ready"), sem("feat_ready")
        fT_done, fT_ready, sc_done = sem("fT_done"), sem("fT_ready"), sem("sc_done")
        even_ready, odd_moved, odd_ready = sem("even_ready"), sem("odd_moved"), sem("odd_ready")
        yu_done, yu_ready, y_done, y_ready = sem("yu_done"), sem("yu_ready"), sem("y_done"), sem("y_ready")
        st_done, st_ready = sem("st_done"), sem("st_ready")
        yT_done, yT_ready = sem("yT_done"), sem("yT_ready")
        o_done, o_ready, o_read = sem("o_done"), sem("o_ready"), sem("o_read")

        block = ctx.enter_context(nc.Block())
        @block.gpsimd
        def _(pool):
            pool.memset(v1[:, :, :, HD:VW], 1.0).then_inc(fill, 1)
            pool.memset(state[:, :, :], 0.0).then_inc(fill, 1)
            pool.wait_ge(fill, 2)

            def args(g):
                pool.wait_ge(max_ready, 2 * g + 1)
                pool.tensor_tensor(ex[:, :, 0, :], p[:, :, :], pmax[:, :, :].to_broadcast([P, 2 * HEADS, HD]),
                                   ALU.subtract).then_inc(arg_ready, 1)
                pool.wait_ge(max_ready, 2 * g + 2)
                pool.tensor_tensor(ex[:, :, 1, :], pmin[:, :, :].to_broadcast([P, 2 * HEADS, HD]), p[:, :, :],
                                   ALU.subtract).then_inc(arg_ready, 1)

            def body(b, first=False, last=False):
                for t in range(TT):
                    g = TT * b + t
                    if not (last and t == TT - 1):
                        args(g + 1)
                    for i in range(HPC // 2):
                        pool.wait_ge(odd_moved, HPC // 2 * g + i + 1)
                        pool.tensor_tensor(att[:, 2 * i + 1, :, :], att[:, 2 * i + 1, :, :],
                                           causal[:, :, :].to_broadcast([P, FC, P]), ALU.mult).then_inc(odd_ready, 1)
                    if t == 0 and not last:
                        pool.wait_ge(var_ready, 2 * b + (1 if first else 0))
                        nm.root(pool, rstd_ready)
                    if t == 1 and not first:
                        at = 2 * b + (0 if last else 1)
                        pool.wait_ge(var_ready, at)
                        nm2.root_shift(pool, rstd_ready, at, shift_ready)

            args(0)
            body(0, first=True)
            with pool.Fori(1, B - 1) as b:
                body(b)
            body(B - 1, last=True)
            pool.wait_ge(var_ready, 2 * B - 1)
            nm2.root_shift(pool, rstd_ready, 2 * B - 1, shift_ready)

        @block.scalar
        def _(act):
            def copy(out, in_, ready):
                nc.scalar.activation(out, in_, ACT.Copy).then_inc(ready, 1)

            def move_zT(b):
                for k in range(KC):
                    act.wait_ge(zT_done, KC * b + k + 1)
                    copy(zT.high[:, k, :], bank[1 + k][:, :], zT_high)

            def move_v(g, par):
                act.wait_ge(v_done, g + 1)
                copy(v1[:, par, :, 0:HD], bank[3][:, 0:D].rearrange("p (h e) -> p h e", h=HEADS), v_ready)

            def exps(g):
                act.wait_ge(arg_ready, 2 * g + 2)
                nc.scalar.activation(ex[:, :, :, :], ex[:, :, :, :], ACT.Exp).then_inc(exp_ready, 1)

            def move_yu(g):
                act.wait_ge(yu_done, g + 1)
                copy(yu[:, :, :], b_y[:, :].rearrange("p (c i) -> p c i", c=FC), yu_ready)

            def move_yT(g):
                act.wait_ge(yT_done, g + 1)
                copy(yT[:, :, :], bank[0][:, 0:D].rearrange("p (k i) -> p k i", k=KC), yT_ready)

            def move_o(g, t, b_read):
                if t == 0:
                    act.wait_ge(o_read, TT * b_read)
                act.wait_ge(o_done, g + 1)
                copy(o[:, t, :], bank[3][:, D:2 * D], o_ready)

            def norm_o(b):
                act.wait_ge(shift_ready, b + 1)
                for t in range(TT):
                    nm2.scaled(nc, zn[:, t, :], o[:, t, :], t).then_inc(o_read, 1)

            def body(b, first=False, last=False):
                for t in range(TT):
                    g = TT * b + t
                    nxt = not (last and t == TT - 1)
                    if not (first and t < 2):
                        move_o(g - 2, (t - 2) % TT, b)
                    for i, dst in enumerate((qT, kT)):
                        act.wait_ge(fT_done, 2 * g + i + 1)
                        copy(dst[:, :], bank[i][:, :], fT_ready)
                    if nxt:
                        move_v(g + 1, (t + 1) % 2)
                    for i in range(HPC // 2):
                        act.wait_ge(sc_done, HPC * g + 2 * i + 2)
                        copy(att[:, 2 * i + 1, :, :], bank[5][:, :].rearrange("p (c i) -> p c i", c=FC), odd_moved)
                        if i == 0 and nxt:
                            exps(g + 1)
                    if t == 2 and not last:
                        move_zT(b + 1)
                    move_yu(g)
                    if not (first and t == 0):
                        move_yT(g - 1)
                    if t == 1 and not first:
                        norm_o(b - 1)

            act.wait_ge(w_in, W_IN)
            copy(wv.high[:, :, :], wv.full[:, :, :], w_high)
            nc.scalar.preload_act_table(ACT.Exp)
            act.wait_ge(comp_done, 2)
            for k in range(KC):
                copy(wqk.high[:, k, :], bank[4 + k][:, :], w_high)
            act.wait_ge(fill, 2)
            move_zT(0)
            move_v(0, 0)
            exps(0)
            body(0, first=True)
            with act.Fori(1, B - 1) as b:
                body(b)
            body(B - 1, last=True)
            move_o(TT * B - 2, TT - 2, B)
            move_yT(TT * B - 1)
            move_o(TT * B - 1, TT - 1, B)
            norm_o(B - 1)

        @block.vector
        def _(dve):
            steps = s.steps.on(dve)

            def front_stats(b):
                nm.stats(nc, steps, [tile_of(x, b, t) for t in range(TT)], var_ready)

            def front_norm(b, at):
                dve.wait_ge(rstd_ready, at)
                for t in range(TT):
                    nm.apply(nc, z[:, t * D:(t + 1) * D], tile_of(x, b, t), t).then_inc(z_ready, 1)

            def rest_stats(b):
                dve.wait_ge(o_ready, TT * b + TT)
                nm2.stats(nc, steps, [o[:, t, :] for t in range(TT)], var_ready, minus=True)

            def rest_add(b):
                dve.wait_ge(o_read, TT * b + TT)
                steps.did(nc.vector.tensor_tensor(batch_of(x, b), batch_of(x, b),
                                                  zn[:, :, :].rearrange("p t c -> p (t c)"), ALU.add))

            def low(m, k, from_, high, at, ready):
                dve.wait_ge(high, at)
                nc.vector.tensor_tensor(m.low[:, k, :], from_, m.high[:, k, :].bitcast(F32), ALU.subtract).then_inc(ready, 1)

            def low_zT(b):
                for k in range(KC):
                    low(zT, k, bank[1 + k][:, :], zT_high, KC * b + k + 1, zT_low)

            def project(g):
                dve.wait_ge(p_done, g + 1)
                nc.vector.tensor_tensor(p[:, :, :].rearrange("p (m h) e -> p m h e", m=2),
                                        bank[2][:, :].rearrange("p (m h e) -> p m h e", m=2, h=HEADS),
                                        bias[:, :, :, :].to_broadcast([P, 2, HEADS, HD]), ALU.add).then_inc(p_ready, 1)
                dve.wait_ge(p_ready, g + 1)
                nc.vector.tensor_reduce(pmax[:, :, 0], p[:, :, :], AX.X, ALU.max).then_inc(max_ready, 1)
                nc.vector.tensor_reduce(pmin[:, :, 0], p[:, :, :], AX.X, ALU.min).then_inc(max_ready, 1)

            def softmax(g, par):
                dve.wait_ge(exp_ready, g + 1)
                e = ex[:, :, :, :].rearrange("p h s e -> p (h s) e")
                steps.did(nc.vector.tensor_reduce(tot[:, :, 0], e, AX.X, ALU.add))
                steps.settle()
                steps.did(nc.vector.reciprocal(rtot[:, :, :], tot[:, :, :]))
                steps.settle()
                nc.vector.tensor_tensor(feat[:, par, :].rearrange("p (h e) -> p h e", e=HD), e,
                                        rtot[:, :, :].to_broadcast([P, 4 * HEADS, HD]), ALU.mult).then_inc(feat_ready, 1)

            def divide(g):
                dve.wait_ge(y_done, g + 1)
                yv = bank[0][:, :].rearrange("p (h e) -> p h e", e=2 * HD)
                steps.did(nc.vector.tensor_scalar(den[:, :], yv[:, :, HD], 1e-6, None, ALU.max))
                steps.settle()
                steps.did(nc.vector.reciprocal(rden[:, :, 0], den[:, :]))
                steps.settle()
                nc.vector.tensor_tensor(y[:, :, :], yv[:, :, 0:HD], rden[:, :, :].to_broadcast([P, HEADS, HD]),
                                        ALU.mult).then_inc(y_ready, 1)

            def body(b, first=False, last=False):
                for t in range(TT):
                    g = TT * b + t
                    if not (last and t == TT - 1):
                        project(g + 1)
                    for i in range(HPC // 2):
                        dve.wait_ge(sc_done, HPC * g + 2 * i + 1)
                        nc.vector.tensor_tensor(att[:, 2 * i, :, :], bank[4][:, :].rearrange("p (c i) -> p c i", c=FC),
                                                causal[:, :, :].to_broadcast([P, FC, P]), ALU.mult).then_inc(even_ready, 1)
                    if t == 1 and not first:
                        rest_stats(b - 1)
                    if t == 2 and not last:
                        front_norm(b + 1, 2 * b + (1 if first else 0))
                    if not (first and t == 0):
                        divide(g - 1)
                    if not (last and t == TT - 1):
                        softmax(g + 1, (t + 1) % 2)
                    if t == 0 and not last:
                        front_stats(b + 1)
                    if t == 2 and not last:
                        low_zT(b + 1)
                    if t < TT - 1:
                        dve.wait_ge(st_done, (TT - 1) * b + t + 1)
                    else:
                        dve.wait_ge(yu_done, g + 1)
                    for r in range(HPC):
                        rs, cs = slice(r * 2 * HD, (r + 1) * 2 * HD), slice(r * VW, (r + 1) * VW)
                        block_r = state[rs, :, r * 2 * HD:r * 2 * HD + VW]
                        if t < TT - 1:
                            nc.vector.tensor_tensor(block_r, block_r, b_st[rs, 0:HEADS * VW].rearrange(
                                "p (c n) -> p c n", c=FC)[:, :, cs], ALU.add).then_inc(st_ready, 1)
                        elif not last:
                            nc.vector.memset(block_r, 0.0).then_inc(st_ready, 1)
                    if t == 2 and not first:
                        rest_add(b - 1)

            dve.wait_ge(w_in, W_IN)
            low(wv, slice(0, KC), wv.full[:, :, :], w_high, 1, w_low)
            for k in range(KC):
                low(wqk, k, bank[4 + k][:, :], w_high, 1 + k + 1, w_low)
            low_zT(0)
            project(0)
            softmax(0, 0)
            BODY = TT * 4 + 1 + 2 * Norm.STATS_STEPS
            dve.wait_ge(fill, 2)
            body(0, first=True)
            steps.loop(1, B - 1, body, BODY)
            body(B - 1, last=True)
            divide(TT * B - 1)
            rest_stats(B - 1)
            rest_add(B - 1)

        @block.tensor
        def _(pe):
            def trans_z(b, first=False):
                if not first:
                    pe.wait_ge(z_ready, TT * b)
                for k in range(KC):
                    for t in range(TT):
                        last = nc.tensor.transpose(bank[1 + k][:, t * P:(t + 1) * P],
                                                   z[:, t * D + k * P:t * D + (k + 1) * P], ident[:, :])
                    last.then_inc(zT_done, 1)

            def project(t):
                for k in range(KC):
                    last = product(nc, bank[2][:, :], zT.parts(k, slice(t * P, (t + 1) * P)), wqk.parts(k),
                                   k == 0, k == KC - 1)
                last.then_inc(p_done, 1)

            def values(t):
                for k in range(KC):
                    last = product(nc, bank[3][:, 0:D], zT.parts(k, slice(t * P, (t + 1) * P)), wv.parts(k),
                                   k == 0, k == KC - 1)
                last.then_inc(v_done, 1)

            def trans_yu(g):
                pe.wait_ge(yu_ready, g + 1)
                for c in range(FC):
                    last = nc.tensor.transpose(bank[0][:, c * P:(c + 1) * P], yu[:, c, :], ident[:, :])
                last.then_inc(y_done, 1)

            def trans_y(g):
                pe.wait_ge(y_ready, g + 1)
                for k in range(KC):
                    last = nc.tensor.transpose(bank[0][:, k * P:(k + 1) * P],
                                               y[:, k * HEADS // KC:(k + 1) * HEADS // KC, :].rearrange("p h e -> p (h e)"),
                                               ident[:, :])
                last.then_inc(yT_done, 1)

            def out(g):
                pe.wait_ge(yT_ready, g + 1)
                for k in range(KC):
                    last = nc.tensor.matmul(bank[3][:, D:2 * D], yT[:, k, :], wo[:, k, :], start=k == 0, stop=k == KC - 1)
                last.then_inc(o_done, 1)

            def body(b, first=False, last=False):
                for t in range(TT):
                    g, par = TT * b + t, t % 2
                    nxt = not (last and t == TT - 1)
                    if nxt:
                        if t == TT - 1:
                            pe.wait_ge(zT_low, KC * b + 2 * KC)
                        pe.wait_ge(p_ready, g + 1)
                        project((t + 1) % TT)
                    if not (first and t < 2):
                        pe.wait_ge(v_ready, g + 1)
                        out(g - 2)
                    pe.wait_ge(feat_ready, g + 1)
                    if not (first and t < 1):
                        pe.wait_ge(yT_ready, g - 1)
                    for i in range(2):
                        for c in range(FC):
                            f = i * QW + c * P
                            mm = nc.tensor.transpose(bank[i][:, c * P:(c + 1) * P], feat[:, par, f:f + P], ident[:, :])
                        mm.then_inc(fT_done, 1)
                    if nxt:
                        if not (first and t < 1):
                            pe.wait_ge(o_ready, g - 1)
                        pe.wait_ge(v_ready, g + 1)
                        values((t + 1) % TT)
                    pe.wait_ge(fT_ready, 2 * g + 2)
                    for r in range(HPC):
                        rs = slice(r * 2 * HD, (r + 1) * 2 * HD)
                        if r % 2 == 0:
                            pe.wait_ge(even_ready, HPC // 2 * g + r // 2)
                        else:
                            pe.wait_ge(odd_moved, HPC // 2 * g + r // 2)
                        for c in range(FC):
                            cs = slice(c * P, (c + 1) * P)
                            mm = nc.tensor.matmul(bank[4 + r % 2][:, cs], kT[rs, cs], qT[rs, cs], start=True, stop=True)
                        mm.then_inc(sc_done, 1)
                    if not (first and t == 0):
                        trans_yu(g - 1)
                    if t == 2 and not last:
                        pe.wait_ge(p_ready, g + 2)
                        trans_z(b + 1)
                    pe.wait_ge(st_ready, HPC * g)
                    for c in range(FC):
                        cs = slice(c * P, (c + 1) * P)
                        nc.tensor.matmul(b_y[:, cs], state[:, c, :], qT[:, cs], start=c == 0, stop=False)
                    for r in range(HPC):
                        if r % 2 == 0:
                            pe.wait_ge(even_ready, HPC // 2 * g + r // 2 + 1)
                        else:
                            pe.wait_ge(odd_ready, HPC // 2 * g + r // 2 + 1)
                        for c in range(FC):
                            mm = nc.tensor.matmul(b_y[r * 2 * HD:r * 2 * HD + VW, c * P:(c + 1) * P],
                                                  v1[:, par, HPC * c + r, :], att[:, r, c, :],
                                                  start=False, stop=c == FC - 1)
                    mm.then_inc(yu_done, 1)
                    if t < TT - 1:
                        for c in range(FC):
                            mm = nc.tensor.matmul(b_st[:, c * HPC * VW:(c + 1) * HPC * VW],
                                                  feat[:, par, QW + c * P:QW + (c + 1) * P],
                                                  v1[:, par, c * HPC:(c + 1) * HPC, :].rearrange("p h e -> p (h e)"),
                                                  start=True, stop=True)
                        mm.then_inc(st_done, 1)
                    if not (first and t == 0):
                        trans_y(g - 1)

            pe.wait_ge(w_in, W_IN)
            for k in range(KC):
                for m in range(2 * KC):
                    mm = nc.tensor.matmul(bank[4 + k][:, m * P:(m + 1) * P], rows[:, m, k * P:(k + 1) * P],
                                          maps[:, m // KC, :], start=True, stop=True)
                mm.then_inc(comp_done, 1)
            trans_z(0, first=True)
            pe.wait_ge(w_low, 1 + KC)
            pe.wait_ge(zT_low, KC)
            project(0)
            values(0)
            pe.wait_ge(fill, 2)
            body(0, first=True)
            with pe.Fori(1, B - 1) as b:
                body(b)
            body(B - 1, last=True)
            out(TT * B - 2)
            trans_yu(TT * B - 1)
            trans_y(TT * B - 1)
            pe.wait_ge(o_ready, TT * B - 1)
            out(TT * B - 1)


G_TILES = B * TT
ZW = D + NE
BLK = CAP // P
BITS = 30
ROUNDS = BITS // 2


def route(nc, s, w):
    x, norms, bank, ident = s.x, (s.norm, s.norm2), s.bank, s.ident
    GE = G_TILES * NE
    with ExitStack() as ctx:
        sb = lambda n, shape, d=F32: ctx.enter_context(nc.sbuf_tensor("rt_" + n, shape, d))
        sem = lambda n: ctx.enter_context(nc.semaphore("rt_" + n))
        wg = sb("wg", [P, KC, NE])
        z = sb("z", [P, 2, TT * D])
        zT = sb("zT", [P, 2, KC, T])
        ones, below = sb("ones", [P, P], BF16), sb("below", [P, P], BF16)
        lo_row = sb("lo_row", [P, P], BF16)
        hi_row = sb("hi_row", [P, 1, BLK])
        tile_no = sb("tile_no", [P, GE, 1])
        lane_no = sb("lane_no", [P, 1])
        carry_on = sb("carry_on", [P, GE])
        same = sb("same", [P, P], BF16)
        unit = sb("unit", [P, ROUNDS])
        next_cand = sb("next_cand", [P, ROUNDS * 3], I32)
        cols = sb("cols", [P, 2 * P])
        met = sb("met", [P, 3, 2 * P], BF16)
        part, hit, hits = sb("part", [P, 3], BF16), sb("hit", [P, 3]), sb("hits", [P, 1])
        inc, low, cand = sb("inc", [P, 1], I32), sb("low", [P, 1], I32), sb("cand", [P, 3], I32)
        low_wide = sb("low_wide", [P, P])
        zeros = sb("zeros", [P, TT * D])
        top, rsum, esum = sb("top", [P, G_TILES, 1]), sb("rsum", [P, G_TILES, 1]), sb("esum", [P, G_TILES, 1])
        score = sb("score", [P, G_TILES, NE])
        by_exp = sb("by_exp", [P, NE, G_TILES])
        flag, take = sb("flag", [P, NE, G_TILES], BF16), sb("take", [P, NE, G_TILES], BF16)
        chosen = sb("chosen", [P, NE, G_TILES], BF16)
        above = sb("above", [P, NE], BF16)
        need = sb("need", [P, NE, 1])
        total, upto, rank = sb("total", [P, GE]), sb("upto", [P, GE]), sb("rank", [P, GE])
        slot, lo_i, hi_i = (sb(n, [P, GE], I32) for n in ("slot", "lo_i", "hi_i"))
        lo, hi = sb("lo", [P, GE]), sb("hi", [P, GE, 1])
        hot_hi = sb("hot_hi", [P, GE, BLK])
        number = sb("number", [P, GE, 2, BLK], BF16)
        hot_lo = sb("hot_lo", [P, 2, G_TILES, P], BF16)
        LATE = 12
        late = [P, LATE, P]
        off = sb("off", [P, 2, LATE, P])
        pair = sb("pair", [P, NE, 2, BLK])

        w_in, c_in, fill = sem("w_in"), sem("c_in"), sem("fill")
        var_ready, rstd_ready, z_ready = sem("var_ready"), sem("rstd_ready"), sem("z_ready")
        zT_done, zT_ready, logits_done = sem("zT_done"), sem("zT_ready"), sem("logits_done")
        z_out, zero_out, score_out = [sem("z_out0"), sem("z_out1")], sem("zero_out"), sem("score_out")
        shifted, exp_ready, score_ready = sem("shifted"), sem("exp_ready"), sem("score_ready")
        part_ready, count_done, flags_ready, ranks_done = sem("part_ready"), sem("count_done"), sem("flags_ready"), sem("ranks_done")
        aside_ready, aside_done = sem("aside_ready"), sem("aside_done")
        number_ready, lo_ready, hot_late = sem("number_ready"), sem("lo_ready"), sem("hot_late")
        off_ready, off_abs = sem("off_ready"), sem("off_abs")
        hot_ready, hot_used = [sem("hot_ready0"), sem("hot_ready1")], [sem("hot_used0"), sem("hot_used1")]
        block = ctx.enter_context(nc.Block())
        C_IN = 16 * 10
        z_rows = s.z_dram.rearrange("(g p) c -> p g c", p=P)
        acc_rows = s.acc_dram.rearrange("(g p) c -> p g c", p=P)

        @block.sync
        def _(sp):
            sp.dma_start(wg[:, :, :], w["wg"].rearrange("(k p) n -> p k n", p=P)).then_inc(w_in, 16)
            for dst, src in ((ones[:, :], w["ones"]), (below[:, :], w["below"]), (lo_row[:, :], w["lo_row"]),
                             (hi_row[:, 0, :], w["hi_row"]), (tile_no[:, :, 0], w["tile_no"]), (lane_no[:, :], w["lane_no"]),
                             (carry_on[:, :], w["carry_on"]), (same[:, :], w["same"]), (unit[:, :], w["unit"]),
                             (next_cand[:, :], w["next_cand"])):
                sp.dma_start(dst, src).then_inc(c_in, 16)
            sp.wait_ge(fill, 1)
            with sp.Fori(0, B // 2) as i:
                for par in range(2):
                    b = 2 * i + par
                    sp.wait_ge(z_ready, TT * b + TT)
                    sp.dma_start(z_rows[:, bass.ds(TT * b, TT), 0:D], z[:, par, :].rearrange("p (t c) -> p t c", t=TT))\
                        .then_inc(z_out[par], 16)
                    sp.dma_start(acc_rows[:, bass.ds(TT * b, TT), :], zeros[:, :].rearrange("p (t c) -> p t c", t=TT))\
                        .then_inc(zero_out, 16)
            sp.wait_ge(score_ready, 1)
            sp.dma_start(z_rows[:, :, D:ZW], score[:, :, :]).then_inc(score_out, 16)
            for par in range(2):
                sp.wait_ge(z_out[par], 16 * B // 2)
            sp.wait_ge(zero_out, 16 * B)
            sp.wait_ge(score_out, 16)

        @block.gpsimd
        def _(pool):
            pool.memset(zeros[:, :], 0.0).then_inc(fill, 1)
            with pool.Fori(0, B // 2) as i:
                for par in range(2):
                    pool.wait_ge(var_ready, 2 * i + par + 1)
                    norms[par].root(pool, rstd_ready)
            pool.wait_ge(lo_ready, 1)
            for e in range(NE):
                if e >= 2:
                    pool.wait_ge(hot_late, e - 1)
                at = e * G_TILES + G_TILES - LATE
                pool.tensor_tensor(off[:, e % 2, :, :], lo_row[:, :].rearrange("p (a n) -> p a n", a=1).to_broadcast(late),
                                   lo[:, at:at + LATE].rearrange("p (g a) -> p g a", a=1).to_broadcast(late),
                                   ALU.subtract).then_inc(off_ready, 1)

        @block.scalar
        def _(act):
            nc.scalar.preload_act_table(ACT.Exp)
            with act.Fori(0, B // 2) as i:
                for par in range(2):
                    for k in range(KC):
                        act.wait_ge(zT_done, KC * (2 * i + par) + k + 1)
                        nc.scalar.activation(zT[:, par, k, :], bank[4 * par + k][:, :], ACT.Copy).then_inc(zT_ready, 1)
            act.wait_ge(shifted, 1)
            nc.scalar.activation(score[:, :, :], score[:, :, :], ACT.Exp).then_inc(exp_ready, 1)
            for e in range(NE):
                act.wait_ge(off_ready, e + 1)
                nc.scalar.activation(off[:, e % 2, :, :], off[:, e % 2, :, :], ACT.Abs).then_inc(off_abs, 1)
                act.wait_ge(off_abs, e + 1)
                if e >= 2:
                    act.wait_ge(hot_used[e % 2], e // 2)
                nc.scalar.activation(hot_lo[:, e % 2, G_TILES - LATE:G_TILES, :], off[:, e % 2, :, :], ACT.Relu,
                                     bias=1.0, scale=-1.0).then_inc(hot_late, 1)

        @block.vector
        def _(dve):
            steps = s.steps.on(dve)

            def stats(b, par):
                norms[par].stats(nc, steps, [tile_of(x, b, t) for t in range(TT)], var_ready)

            def norm(i, par):
                b = 2 * i + par
                dve.wait_ge(rstd_ready, b + 1)
                dve.wait_ge(z_out[par], 16 * i)
                dve.wait_ge(zT_done, 2 * KC * i)
                for t in range(TT):
                    norms[par].apply(nc, z[:, par, t * D:(t + 1) * D], tile_of(x, b, t), t).then_inc(z_ready, 1)

            def norm_pair(i, last=False):
                stats(2 * i + 1, 1)
                norm(i, 0)
                if not last:
                    stats(2 * i + 2, 0)
                norm(i, 1)

            stats(0, 0)
            steps.loop(0, B // 2 - 1, norm_pair, 2 * Norm.STATS_STEPS)
            norm_pair(B // 2 - 1, last=True)
            logits = bank[2][:, 0:GE].rearrange("p (g e) -> p g e", e=NE)
            wide = [P, G_TILES, NE]
            dve.wait_ge(logits_done, B)
            steps.did(nc.vector.tensor_reduce(top[:, :, 0], logits, AX.X, ALU.max))
            steps.settle()
            nc.vector.tensor_tensor(score[:, :, :], logits, top[:, :, :].to_broadcast(wide), ALU.subtract).then_inc(shifted, 1)
            dve.wait_ge(exp_ready, 1)
            steps.did(nc.vector.tensor_reduce(esum[:, :, 0], score[:, :, :], AX.X, ALU.add))
            steps.settle()
            steps.did(nc.vector.reciprocal(rsum[:, :, :], esum[:, :, :]))
            steps.settle()
            nc.vector.tensor_tensor(score[:, :, :], score[:, :, :], rsum[:, :, :].to_broadcast(wide), ALU.mult)\
                .then_inc(score_ready, 1)
            dve.wait_ge(score_ready, 1)
            steps.did(nc.vector.tensor_copy(by_exp[:, :, :], score[:, :, :].rearrange("p g e -> p e g")))
            dve.wait_ge(c_in, C_IN)
            steps.did(nc.vector.memset(low[:, :], 0))
            steps.did(nc.vector.memset(inc[:, :], 0))
            for j in range(3):
                steps.did(nc.vector.memset(cand[:, j:j + 1], (j + 1) << (BITS - 2)))
            dve.wait_ge(aside_done, 1)
            steps.did(nc.vector.tensor_copy(cols[:, :], bank[0][:, 0:2 * P]))
            steps.settle()

            def search(i):
                for j in range(3):
                    nc.vector.tensor_scalar(met[:, j, :], cols[:, :], cand[:, j:j + 1].bitcast(F32), None, ALU.is_ge, ALU.add,
                                            accum_out=part[:, j:j + 1]).then_inc(part_ready, 1)
                steps.did(nc.vector.tensor_tensor(low[:, :], low[:, :], inc[:, :], ALU.bitwise_or))
                dve.wait_ge(count_done, i + 1)
                steps.did(nc.vector.tensor_scalar(hit[:, :], bank[3][:, 0:3], float(CAP), None, ALU.is_ge, ALU.add,
                                                  accum_out=hits[:, :]))
                steps.settle()
                steps.did(nc.vector.tensor_tensor(inc[:, :], hits[:, :], unit[:, bass.ds(i, 1)], ALU.mult))
                steps.settle()
                steps.did(nc.vector.scalar_tensor_tensor(out=cand[:, :], in0=next_cand[:, bass.ds(3 * i, 3)],
                                                         scalar=low[:, :], in1=inc[:, :].to_broadcast([P, 3]),
                                                         op0=ALU.bitwise_or, op1=ALU.bitwise_or))
                steps.settle()

            UNROLL = 3
            steps.loop(0, ROUNDS // UNROLL, lambda i: [search(UNROLL * i + k) for k in range(UNROLL)], 4 * UNROLL)
            steps.did(nc.vector.tensor_tensor(low[:, :], low[:, :], inc[:, :], ALU.bitwise_or))
            steps.settle()
            nc.vector.tensor_copy(low_wide[:, :], low[:, :].bitcast(F32).to_broadcast([P, P])).then_inc(aside_ready, 1)
            dve.wait_ge(aside_done, 2)
            tall = [P, NE, G_TILES]
            edge = bank[1][:, 0:NE].rearrange("p (e a) -> p e a", a=1).to_broadcast(tall)
            steps.did(nc.vector.tensor_tensor(flag[:, :, :], by_exp[:, :, :], edge, ALU.is_gt))
            nc.vector.tensor_tensor(take[:, :, :], by_exp[:, :, :], edge, ALU.is_equal).then_inc(flags_ready, 1)
            steps.settle()
            with nc.allow_low_precision(reason="counts up to 32 are exact in bfloat16"):
                nc.vector.tensor_reduce(above[:, :], flag[:, :, :], AX.X, ALU.add).then_inc(aside_ready, 1)
            dve.wait_ge(aside_done, 3)
            steps.did(nc.vector.tensor_scalar(need[:, :, 0], bank[3][:, NE:2 * NE], -1.0, float(CAP), ALU.mult, ALU.add))

            def ranks(n, out):
                dve.wait_ge(ranks_done, n)
                steps.did(nc.vector.tensor_copy(total[:, :], bank[5][:, 0:GE]))
                steps.settle()
                steps.did(nc.vector.tensor_tensor_scan(upto[:, :], carry_on[:, :], total[:, :], 0.0, ALU.mult, ALU.add))
                steps.settle()
                steps.did(nc.vector.tensor_tensor(upto[:, :], upto[:, :], total[:, :], ALU.subtract))
                steps.settle()
                steps.did(nc.vector.tensor_tensor(out, bank[4][:, 0:GE], upto[:, :], ALU.add))
                steps.settle()

            ranks(1, rank[:, :])
            steps.did(nc.vector.tensor_tensor(chosen[:, :, :], rank[:, :].rearrange("p (e g) -> p e g", e=NE),
                                              need[:, :, :].to_broadcast(tall), ALU.is_lt))
            steps.settle()
            steps.did(nc.vector.tensor_tensor(take[:, :, :], chosen[:, :, :], take[:, :, :], ALU.mult))
            steps.settle()
            nc.vector.tensor_tensor(chosen[:, :, :], flag[:, :, :], take[:, :, :], ALU.add).then_inc(flags_ready, 1)
            ranks(2, slot[:, :])
            steps.did(nc.vector.tensor_scalar(lo_i[:, :], slot[:, :], P - 1, None, ALU.bitwise_and))
            steps.did(nc.vector.tensor_scalar(hi_i[:, :], slot[:, :], P.bit_length() - 1, None, ALU.logical_shift_right))
            steps.settle()
            nc.vector.scalar_tensor_tensor(out=lo[:, :], in0=lo_i[:, :], scalar=1.0,
                                           in1=chosen[:, :, :].rearrange("p e g -> p (e g)"),
                                           op0=ALU.add, op1=ALU.mult).then_inc(lo_ready, 1)
            steps.did(nc.vector.tensor_copy(hi[:, :, 0], hi_i[:, :]))
            steps.settle()
            steps.did(nc.vector.tensor_tensor(hot_hi[:, :, :], hi[:, :, :].to_broadcast([P, GE, BLK]),
                                              hi_row[:, :, :].to_broadcast([P, GE, BLK]), ALU.is_equal))
            steps.settle()
            nc.vector.tensor_tensor(number[:, :, 0, :], hot_hi[:, :, :], tile_no[:, :, :].to_broadcast([P, GE, BLK]),
                                    ALU.mult).then_inc(number_ready, 1)
            nc.vector.tensor_scalar(number[:, :, 1, :], hot_hi[:, :, :], lane_no[:, :], None, ALU.mult).then_inc(number_ready, 1)
            dve.wait_ge(lo_ready, 1)
            with dve.Fori(0, NE // 2) as i:
                for par in range(2):
                    for g in range(G_TILES - LATE):
                        if g == 0:
                            dve.wait_ge(hot_used[par], i)
                        hot = nc.vector.tensor_scalar(hot_lo[:, par, g, :], lo_row[:, :],
                                                      lo[:, bass.ds((2 * i + par) * G_TILES + g, 1)], None, ALU.is_equal)
                        if g % 4 == 3:
                            hot.then_inc(hot_ready[par], 1)
            dve.wait_ge(hot_used[0], NE // 2)
            dve.wait_ge(hot_used[1], NE // 2)
            steps.did(nc.vector.tensor_copy(pair[:, :, :, :], bank[6][:, 0:NE * 2 * BLK]
                                            .rearrange("p (e a h) -> p e a h", e=NE, a=2)))
            steps.settle()
            steps.did(nc.vector.scalar_tensor_tensor(out=s.token[:, :, :], in0=pair[:, :, 0, :], scalar=float(P),
                                                     in1=pair[:, :, 1, :], op0=ALU.mult, op1=ALU.add))
            steps.settle()

        @block.tensor
        def _(pe):
            pe.wait_ge(w_in, 16)

            def trans(b, par):
                pe.wait_ge(z_ready, TT * b + TT)
                for k in range(KC):
                    for t in range(TT):
                        last = nc.tensor.transpose(bank[4 * par + k][:, t * P:(t + 1) * P],
                                                   z[:, par, t * D + k * P:t * D + (k + 1) * P], ident[:, :])
                    last.then_inc(zT_done, 1)

            def logit(b, par):
                pe.wait_ge(zT_ready, KC * b + KC)
                for t in range(TT):
                    for k in range(KC):
                        last = nc.tensor.matmul(bank[2][:, bass.ds((TT * b + t) * NE, NE)], zT[:, par, k, t * P:(t + 1) * P],
                                                wg[:, k, :], start=k == 0, stop=k == KC - 1)
                last.then_inc(logits_done, 1)

            def pair(i, last=False):
                trans(2 * i + 1, 1)
                logit(2 * i, 0)
                if not last:
                    trans(2 * i + 2, 0)
                logit(2 * i + 1, 1)

            trans(0, 0)
            with pe.Fori(0, B // 2 - 1) as i:
                pair(i)
            pair(B // 2 - 1, last=True)
            pe.wait_ge(score_ready, 1)
            for n in range(2):
                last = nc.tensor.transpose(bank[0][:, n * P:(n + 1) * P],
                                           score[:, n * P // NE:(n + 1) * P // NE, :].rearrange("p g e -> p (g e)"),
                                           ident[:, :])
            last.then_inc(aside_done, 1)
            pe.wait_ge(c_in, C_IN)
            with pe.Fori(0, ROUNDS) as i:
                pe.wait_ge(part_ready, 3 * i + 3)
                nc.tensor.matmul(bank[3][:, 0:3], same[:, :], part[:, :], start=True, stop=True).then_inc(count_done, 1)
            pe.wait_ge(aside_ready, 1)
            nc.tensor.transpose(bank[1][:, 0:P], low_wide[:, :], ident[:, :]).then_inc(aside_done, 1)
            pe.wait_ge(aside_ready, 2)
            nc.tensor.matmul(bank[3][:, NE:2 * NE], ones[:, :], above[:, :], start=True, stop=True).then_inc(aside_done, 1)
            for n, src in enumerate((take, chosen)):
                pe.wait_ge(flags_ready, n + 1)
                v = src[:, :, :].rearrange("p e g -> p (e g)")
                nc.tensor.matmul(bank[4][:, 0:GE], below[:, :], v, start=True, stop=True)
                nc.tensor.matmul(bank[5][:, 0:GE], ones[:, :], v, start=True, stop=True).then_inc(ranks_done, 1)
            pe.wait_ge(number_ready, 2)
            W = 2 * BLK
            flat = number[:, :, :, :].rearrange("p n a h -> p (n a h)")
            with pe.Fori(0, NE // 2) as i:
                for par in range(2):
                    for g in range(G_TILES):
                        if g == G_TILES - LATE:
                            pe.wait_ge(hot_late, 2 * i + par + 1)
                        elif g < G_TILES - LATE and g % 4 == 0:
                            pe.wait_ge(hot_ready[par], (G_TILES - LATE) // 4 * i + g // 4 + 1)
                        last = nc.tensor.matmul(bank[6][:, bass.ds((2 * i + par) * W, W)], hot_lo[:, par, g, :],
                                                flat[:, bass.ds(((2 * i + par) * G_TILES + g) * W, W)],
                                                start=g == 0, stop=g == G_TILES - 1)
                    last.then_inc(hot_used[par], 1)


def experts(nc, s, w):
    bank, ident = s.bank, s.ident
    HC = HID // P
    HB = BLK // 2
    with ExitStack() as ctx:
        sb = lambda n, shape, d=F32: ctx.enter_context(nc.sbuf_tensor("ex_" + n, shape, d))
        sem = lambda n: ctx.enter_context(nc.semaphore("ex_" + n))
        both = lambda n: [sem(n + "0"), sem(n + "1")]
        WN, W1, W3, W2 = 2 * KC * HID + HC * D, 0, KC * HID, 2 * KC * HID
        raw = sb("raw", [P, WN])
        wh, wl = sb("wh", [P, 2, WN], F32R), sb("wl", [P, 2, WN], F32R)
        mine = [sb(f"mine{par}", [P, BLK], I32) for par in range(2)]
        got = sb("got", [P, 2, BLK, ZW])
        rh, rl = sb("rh", [P, KC, CAP], F32R), sb("rl", [P, KC, CAP], F32R)
        gate = sb("gate", [P, 2, T])
        h = sb("h", [P, 2, T])
        hh, hl = sb("hh", [P, 2, HC, T], F32R), sb("hl", [P, 2, HC, T], F32R)
        o = sb("o", [P, BLK, D])
        nil, tick = sb("nil", [P, 1]), sb("tick", [P, 1])

        w_in, wh_ready, wl_ready = sem("w_in"), sem("wh_ready"), sem("wl_ready")
        gathered = [sem("gathered0"), sem("gathered1")]
        fill, ticked, mine_ready = sem("fill"), sem("ticked"), sem("mine_ready")
        scaled, rT_done, rh_ready, rl_ready = sem("scaled"), sem("rT_done"), sem("rh_ready"), sem("rl_ready")
        h1_done, h3_done, gate_ready, h_ready = sem("h1_done"), sem("h3_done"), sem("gate_ready"), sem("h_ready")
        hh_ready, hl_ready = sem("hh_ready"), sem("hl_ready")
        o_done, o_ready, added = sem("o_done"), sem("o_ready"), sem("added")
        block = ctx.enter_context(nc.Block())
        WC = 6
        piece = lambda c: slice(c * WN // WC, (c + 1) * WN // WC)
        NH, NT, NO, ADDS = 2 * HC, 2 * KC, BLK // 2, 16 * BLK

        def each(eng, body):
            with eng.Fori(0, NE // 2 - 1) as i:
                body(2 * i, 0, i, False)
                body(2 * i + 1, 1, i, False)
            body(NE - 2, 0, NE // 2 - 1, False)
            body(NE - 1, 1, NE // 2 - 1, True)

        @block.sync
        def _(sp):
            def load(e):
                for at, src in ((W1, w["w1"]), (W3, w["w3"]), (W2, w["w2"])):
                    n = src.shape[2]
                    sp.dma_start(raw[:, at:at + KC * HID].rearrange("p (k n) -> p k n", n=n),
                                 src[bass.ds(e, 1), :, :].rearrange("a (k p) n -> p (a k) n", p=P)).then_inc(w_in, 16)
            load(0)
            with sp.Fori(1, NE) as e:
                sp.wait_ge(wl_ready, WC * e)
                load(e)

        @block.gpsimd
        def _(pool):
            TICKS = 3 + NO

            def wait_ahead(sem, value, e, n):
                pool.wait_ge(ticked, TICKS * e + n)
                pool.wait_ge(sem, value)
                pool.tensor_tensor(tick[:, :], nil[:, :], nil[:, :], ALU.add).then_inc(ticked, 1)

            def gather(e, par, i):
                for j in range(BLK):
                    pool.indirect_dma_start(got[:, par, j, :], None, s.z_dram, bass.IndirectOffsetOnAxis(
                        ap=mine[par][:, j:j + 1], axis=0)).then_inc(gathered[par], 16)

            def split(e, par):
                for c in range(WC):
                    pool.wait_ge(wh_ready, WC * e + c + 1)
                    pool.tensor_tensor(wl[:, par, piece(c)], raw[:, piece(c)], wh[:, par, piece(c)].bitcast(F32),
                                       ALU.subtract).then_inc(wl_ready, 1)

            def body(e, par, i, last):
                if not last:
                    wait_ahead(rT_done, NT * e + NT, e, 0)
                    wait_ahead(mine_ready, e + 2, e, 1)
                    gather(e + 1, 1 - par, i)
                    split(e + 1, 1 - par)
                n = 0 if last else 2
                wait_ahead(added, ADDS * e, e, n)
                for j in range(BLK):
                    if j % 2 == 0:
                        wait_ahead(o_ready, NO * e + j // 2 + 1, e, n + 1 + j // 2)
                    pool.indirect_dma_start(s.acc_dram, bass.IndirectOffsetOnAxis(ap=mine[par][:, j:j + 1], axis=0),
                                            o[:, j, :], None, compute_op=ALU.add).then_inc(added, 16)

            pool.memset(nil[:, :], 0.0).then_inc(fill, 1)
            pool.wait_ge(fill, 1)
            pool.wait_ge(mine_ready, 1)
            gather(0, 0, 0)
            split(0, 0)
            each(pool, body)
            pool.wait_ge(added, ADDS * NE)

        @block.scalar
        def _(act):
            def move_rT(e):
                for n in range(NT):
                    half, k = n // KC, n % KC
                    act.wait_ge(rT_done, NT * e + n + 1)
                    nc.scalar.activation(rh[:, k, half * T:(half + 1) * T], bank[n][:, :], ACT.Copy).then_inc(rh_ready, 1)

            def move_o(e, half):
                if half == 0:
                    act.wait_ge(added, ADDS * e)
                for n in range(2 * half, 2 * half + 2):
                    act.wait_ge(o_done, NO * e + n + 1)
                    nc.scalar.activation(o[:, 2 * n:2 * n + 2, :], bank[6 + n % 2][:, :].rearrange("p (a c) -> p a c", a=2),
                                         ACT.Copy).then_inc(o_ready, 1)

            def split(e, par, c):
                nc.scalar.activation(wh[:, par, piece(c)], raw[:, piece(c)], ACT.Copy).then_inc(wh_ready, 1)

            def high(e, q):
                act.wait_ge(h_ready, NH * e + q + 1)
                nc.scalar.activation(hh[:, q // HC, q % HC, :], h[:, q % 2, :], ACT.Copy).then_inc(hh_ready, 1)

            def body(e, par, i, last):
                for q in range(NH):
                    act.wait_ge(h1_done, NH * e + q + 1)
                    nc.scalar.activation(gate[:, q % 2, :], bank[2 + q % 2][:, :], ACT.Silu).then_inc(gate_ready, 1)
                    if q > 0:
                        high(e, q - 1)
                    if not last and q >= NH - WC:
                        if q == NH - WC:
                            act.wait_ge(w_in, 48 * (e + 2))
                        split(e + 1, 1 - par, q - (NH - WC))
                high(e, NH - 1)
                move_o(e, 0)
                if not last:
                    move_rT(e + 1)
                move_o(e, 1)

            nc.scalar.preload_act_table(ACT.Silu)
            act.wait_ge(w_in, 48)
            for c in range(WC):
                split(0, 0, c)
            move_rT(0)
            each(act, body)

        @block.vector
        def _(dve):
            def name(e, par):
                nc.vector.tensor_scalar(mine[par][:, :], s.token[:, bass.ds(e, 1), :].rearrange("p a h -> p (a h)"),
                                        0.0, None, ALU.add).then_inc(mine_ready, 1)

            def scale(e, par, i):
                dve.wait_ge(gathered[par], ADDS * (i + 1))
                for j in range(BLK):
                    row = got[:, par, :, :].rearrange("p b c -> p (b c)")
                    nc.vector.tensor_scalar(got[:, par, j, 0:D], got[:, par, j, 0:D], row[:, bass.ds(j * ZW + D + e, 1)],
                                            None, ALU.mult).then_inc(scaled, 1)

            def low(e, q):
                dve.wait_ge(hh_ready, NH * e + q + 1)
                nc.vector.tensor_tensor(hl[:, q // HC, q % HC, :], h[:, q % 2, :], hh[:, q // HC, q % HC, :].bitcast(F32),
                                        ALU.subtract).then_inc(hl_ready, 1)

            def low_rT(e):
                for n in range(NT):
                    at = slice(n // KC * T, (n // KC + 1) * T)
                    dve.wait_ge(rh_ready, NT * e + n + 1)
                    nc.vector.tensor_tensor(rl[:, n % KC, at], bank[n][:, :], rh[:, n % KC, at].bitcast(F32),
                                            ALU.subtract).then_inc(rl_ready, 1)

            def body(e, par, i, last):
                for q in range(NH):
                    if q == HC and not last:
                        dve.wait_ge(added, ADDS * e)
                        name(e + 1, 1 - par)
                    dve.wait_ge(h3_done, NH * e + q + 1)
                    dve.wait_ge(gate_ready, NH * e + q + 1)
                    if q > 1:
                        dve.wait_ge(hl_ready, NH * e + q - 1)
                    nc.vector.tensor_tensor(h[:, q % 2, :], bank[4 + q % 2][:, :], gate[:, q % 2, :], ALU.mult)\
                        .then_inc(h_ready, 1)
                    if q > 0:
                        low(e, q - 1)
                low(e, NH - 1)
                if not last:
                    scale(e + 1, 1 - par, i + par)
                    low_rT(e + 1)

            name(0, 0)
            scale(0, 0, 0)
            low_rT(0)
            each(dve, body)

        @block.tensor
        def _(pe):
            def trans(e, par):
                pe.wait_ge(scaled, BLK * e + BLK)
                for n in range(NT):
                    half, k = n // KC, n % KC
                    for j in range(BLK // 2):
                        last = nc.tensor.transpose(bank[n][:, j * P:(j + 1) * P],
                                                   got[:, par, half * BLK // 2 + j, k * P:(k + 1) * P], ident[:, :])
                    last.then_inc(rT_done, 1)

            def out(e, par, half):
                for j in range(BLK // 2):
                    if j % 2 == 0:
                        pe.wait_ge(o_ready, NO * e + (j // 2 + 1 if half else 0))
                    for c in range(HC):
                        last = product(nc, bank[6 + j // 2][:, (j % 2) * D:(j % 2 + 1) * D],
                                       [a[:, half, c, j * P:(j + 1) * P] for a in (hh, hl)],
                                       [a[:, par, W2 + c * D:W2 + (c + 1) * D] for a in (wh, wl)], c == 0, c == HC - 1)
                    if j % 2:
                        last.then_inc(o_done, 1)

            def body(e, par, i, last):
                pe.wait_ge(wl_ready, WC * (e + 1))
                pe.wait_ge(rl_ready, NT * e + NT)
                for q in range(NH):
                    half, c = q // HC, q % HC
                    for at, b0, done, free in ((W1, 2, h1_done, gate_ready), (W3, 4, h3_done, h_ready)):
                        pe.wait_ge(free, NH * e + max(q - 1, 0))
                        for k in range(KC):
                            col = at + k * HID + c * P
                            mm = product(nc, bank[b0 + q % 2][:, :], [a[:, par, col:col + P] for a in (wh, wl)],
                                         [a[:, k, half * T:(half + 1) * T] for a in (rh, rl)], k == 0, k == KC - 1)
                        mm.then_inc(done, 1)
                pe.wait_ge(hl_ready, NH * e + HC)
                out(e, par, 0)
                if not last:
                    pe.wait_ge(gate_ready, NH * e + NH)
                    trans(e + 1, 1 - par)
                pe.wait_ge(hl_ready, NH * e + NH)
                out(e, par, 1)

            trans(0, 0)
            each(pe, body)


def close(nc, s, w, out):
    x, norms = s.x, (s.norm, s.norm2)
    with ExitStack() as ctx:
        sem = lambda n: ctx.enter_context(nc.semaphore("cl_" + n))
        y = ctx.enter_context(nc.sbuf_tensor("cl_y", [P, B * TT * D], F32))
        y_in = [sem("y_in0"), sem("y_in1")]
        x_out, var_ready, rstd_ready, normed, x_ready = (sem(n) for n in ("x_out", "var_ready", "rstd_ready", "normed", "x_ready"))
        block = ctx.enter_context(nc.Block())
        acc_rows = s.acc_dram.rearrange("(g p) c -> p g c", p=P)
        out_rows = out.rearrange("b (t p) c -> p (b t) c", p=P)

        @block.sync
        def _(sp):
            def load(b, par):
                sp.dma_start(batch_of(y, b).rearrange("p (t c) -> p t c", t=TT), acc_rows[:, bass.ds(TT * b, TT), :])\
                    .then_inc(y_in[par], 16)

            for b in range(B):
                if b >= 2:
                    sp.wait_ge(y_in[b % 2], 16 * (b // 2))
                load(b, b % 2)

        @block.scalar
        def _(act):
            for b in range(B):
                act.wait_ge(y_in[b % 2], 16 * (b // 2 + 1))
                act.wait_ge(x_ready, b + 1)
                act.dma_start(out_rows[:, bass.ds(TT * b, TT), :], batch_of(y, b).rearrange("p (t c) -> p t c", t=TT))\
                    .then_inc(x_out, 16)
            act.wait_ge(x_out, 16 * B)

        @block.gpsimd
        def _(pool):
            with pool.Fori(0, B // 2) as i:
                for par in range(2):
                    pool.wait_ge(var_ready, 2 * i + par + 1)
                    norms[par].root(pool, rstd_ready)

        @block.vector
        def _(dve):
            steps = s.steps.on(dve)

            def stats(b, par):
                norms[par].stats(nc, steps, [tile_of(y, b, t) for t in range(TT)], var_ready)

            def norm(b, par):
                dve.wait_ge(rstd_ready, b + 1)
                for t in range(TT):
                    norms[par].apply(nc, tile_of(y, b, t), tile_of(y, b, t), t).then_inc(normed, 1)

            def add(b):
                dve.wait_ge(normed, TT * b + TT)
                nc.vector.tensor_tensor(batch_of(y, b), batch_of(y, b), batch_of(x, b), ALU.add).then_inc(x_ready, 1)

            dve.wait_ge(y_in[0], 16)
            stats(0, 0)
            for b in range(B):
                if b < B - 1:
                    dve.wait_ge(y_in[(b + 1) % 2], 16 * ((b + 1) // 2 + 1))
                    stats(b + 1, (b + 1) % 2)
                norm(b, b % 2)
                add(b)


class Shared:
    pass


def build(nc, ins, out):
    w = dict(ins)
    pos = np.arange(T, dtype=np.float32)
    freq = (np.float32(10000.0) ** (-np.arange(QK // 2, dtype=np.float32) / np.float32(QK // 2))).astype(np.float32)
    angle = (pos[:, None] * freq[None, :]).astype(np.float32)
    turn = np.zeros((P, P), np.float32)
    for i in range(P):
        if i % QK < QK // 2:
            turn[i + QK // 2, i] = -1.0
        else:
            turn[i - QK // 2, i] = 1.0
    for name, a in (("ident", np.eye(P)), ("turn", turn), ("cos", np.tile(np.cos(angle).T, (4, 1))),
                    ("sin", np.tile(np.sin(angle).T, (4, 1))), ("causal", np.triu(np.ones((P, P)))),
                    ("hi_row", np.tile(np.arange(BLK), (P, 1))),
                    ("tile_no", np.tile(np.arange(G_TILES), (P, NE))), ("lane_no", np.arange(P)[:, None]),
                    ("carry_on", np.tile(np.arange(G_TILES) > 0, (P, NE))),
                    ("unit", np.tile(4.0 ** np.arange(ROUNDS - 1, -1, -1), (P, 1)))):
        w[name] = nc.inline_tensor(np.ascontiguousarray(a, dtype=np.float32), "const_" + name).ap()
    half = mybir.dt.np(BF16)
    for name, a, dt in (("ones", np.ones((P, P)), half), ("below", np.triu(np.ones((P, P)), 1), half),
                        ("lo_row", np.tile(np.arange(1, P + 1), (P, 1)), half),
                        ("same", np.tile(np.eye(NE), (P // NE, P // NE)), half),
                        ("next_cand", np.tile(((4 ** np.arange(ROUNDS - 1, -1, -1) // 4)[:, None]
                                               * np.arange(1, 4)).reshape(-1), (P, 1)), np.int32)):
        w[name] = nc.inline_tensor(np.ascontiguousarray(a.astype(dt)), "const_" + name).ap()
    with ExitStack() as ctx:
        s = Shared()
        sb = lambda n, shape, d=F32: ctx.enter_context(nc.sbuf_tensor(n, shape, d))
        s.x = sb("x", [P, B * TT * D])
        s.ident = sb("ident", [P, P])
        s.token = sb("token", [P, NE, BLK])
        s.z_dram = nc.dram_tensor("z_dram", (NTOK, ZW), F32, kind="Internal").ap()
        s.acc_dram = nc.dram_tensor("acc_dram", (NTOK, D), F32, kind="Internal").ap()
        s.mix_loads = MixLoads(nc, ctx)
        s.hedgehog_loads = HedgehogLoads(nc, ctx)
        s.z = sb("z", [P, TT * D])
        s.ahead_var, s.ahead_rstd = (ctx.enter_context(nc.semaphore(n)) for n in ("ahead_var", "ahead_rstd"))
        s.aheads = 0
        s.steps = Steps(ctx.enter_context(nc.semaphore("dve_step")))
        s.norm, s.norm2 = Norm(sb), Norm(sb, "_2")
        s.bank = [ctx.enter_context(nc.psum_tensor(f"bank{i}", [P, 512], F32)) for i in range(8)]
        gau_layer(nc, s, w)
        mix_layer(nc, s, w)
        hedgehog_layer(nc, s, w)
        route(nc, s, w)
        experts(nc, s, w)
        close(nc, s, w, out)


def laid_out(i):
    flip = lambda a: a.T
    cols = lambda a: a.reshape(-1, P).T
    g = lambda n: i[n]
    return {
        "x": g("L0_attn_x").reshape(B, TT, P, D).transpose(0, 2, 1, 3).reshape(B, P, TT * D),
        "Wqk2T": np.concatenate([g("L0_attn_Wqk"), g("L0_attn_Wqk")]).T,
        "WvT": flip(g("L0_attn_Wv")), "WgT": flip(g("L0_attn_Wg")), "WoT": flip(g("L0_attn_Wo")),
        "ln1_wT": cols(g("L0_attn_ln1_w")), "ln1_bT": cols(g("L0_attn_ln1_b")),
        "bqk2": np.concatenate([g("L0_attn_bqk"), g("L0_attn_bqk")]).reshape(P, 1),
        "gammaT": cols(g("L0_attn_gamma")), "betaT": cols(g("L0_attn_beta")), "bgT": cols(g("L0_attn_bg")),
        "bv": g("L0_attn_bv"), "bo": g("L0_attn_bo"), "ln2_w": g("L0_attn_ln2_w"), "ln2_b": g("L0_attn_ln2_b"),
        "pos_emb": g("L0_attn_pos_emb"),
        "ffn_WrT": flip(g("L0_ffn_W_r")), "ffn_WkT": flip(g("L0_ffn_W_k")), "ffn_WvT": flip(g("L0_ffn_W_v")),
        "mu_rT": cols(g("L0_ffn_mu_r")), "mu_kT": cols(g("L0_ffn_mu_k")),
        "w_qk": g("L1_attn_w_qkv")[:2 * D], "w_vT": flip(g("L1_attn_w_qkv")[2 * D:]),
        "wq_mapT": flip(g("L1_attn_wq_map")), "wk_mapT": flip(g("L1_attn_wk_map")),
        "bq_map": g("L1_attn_bq_map"), "bk_map": g("L1_attn_bk_map"), "w_outT": flip(g("L1_attn_w_out")),
        "wg": g("L1_ffn_wg"), "w1": g("L1_ffn_w1"), "w3": g("L1_ffn_w3"), "w2": g("L1_ffn_w2"),
    }


def kernel(**inputs):
    import concourse.bacc as bacc
    from concourse.bass_utils import run_bass_kernel_spmd

    nc = bacc.Bacc("TRN2", target_bir_lowering=False, num_devices=1)
    arrays, ins = {}, {}
    for name, a in laid_out({n: np.asarray(a) for n, a in inputs.items()}).items():
        arrays["in_" + name] = np.ascontiguousarray(a)
        ins[name] = nc.dram_tensor("in_" + name, a.shape, mybir.dt.from_np(a.dtype), kind="ExternalInput").ap()
    out = nc.dram_tensor("out_0", (B, T, D), F32, kind="ExternalOutput").ap()
    build(nc, ins, out)
    r = run_bass_kernel_spmd(nc, [arrays], core_ids=[0])
    return r.results[0]["out_0"]
```
